# Optimizing a Trainium2 kernel written in Bass

```python
import numpy as np
import jax
import jax.numpy as jnp

def _softmax(x, axis=-1):
    return jax.nn.softmax(x, axis=axis)

def _gelu(x):
    return jax.nn.gelu(x, approximate=True)

def _silu(x):
    return jax.nn.silu(x)

def _sigmoid(x):
    return jax.nn.sigmoid(x)

def _layernorm(x, axis=-1, eps=1e-05):
    m = jnp.mean(x, axis=axis, keepdims=True)
    v = jnp.var(x, axis=axis, keepdims=True)
    return (x - m) / jnp.sqrt(v + eps)

def _scatter_add(tgt, idx, src, axis=0):
    return tgt.at[idx].add(src)

def _segment_sum(src, seg, n):
    return jax.ops.segment_sum(src, seg, n)
kernel_name = 'mk_xattn_ffn_d2_seqx_r8_7f0c51'

def setup_inputs(seed: int=0):
    np.random.seed(seed)
    _w = jnp.asarray

    def _rec_inputs():
        import jax
        import jax.numpy as jnp
        _rk = jax.random.key(seed)
        x = 0.0002279 + 0.9999 * jax.random.normal(jax.random.fold_in(_rk, 1), (32, 128, 128), jnp.float32)
        _lenS = 128 - jax.random.randint(jax.random.fold_in(_rk, 7), (32,), 0, max(1, 128 // 4) + 1, jnp.int32)
        _lenS2 = 77 - jax.random.randint(jax.random.fold_in(_rk, 8), (32,), 0, max(1, 77 // 4) + 1, jnp.int32)
        _ctx_1024P = jax.random.normal(jax.random.fold_in(_rk, 11), (32, 16, 128), jnp.float32)
        _ctx_1024c = jax.random.dirichlet(jax.random.fold_in(_rk, 511), 0.3 * jnp.ones((16,), jnp.float32), (32, 77))
        _ctx_1024t = jnp.einsum('bsk,bkd->bsd', _ctx_1024c, _ctx_1024P)
        _ctx_1024t = _ctx_1024t * jax.lax.rsqrt(jnp.mean(jnp.square(_ctx_1024t)) + 1e-12) * 0.953939
        ctx_1024 = 7.22013e-05 + 1.00017 * (_ctx_1024t + 0.3 * jax.random.normal(jax.random.fold_in(_rk, 611), (32, 77, 128), jnp.float32))
        _validS = jnp.arange(128)[None, :] < _lenS[:, None]
        _validS2 = jnp.arange(77)[None, :] < _lenS2[:, None]
        _causal = jnp.tril(jnp.ones((128, 128), dtype=bool))
        mask_1x1xSxS2_ik0 = jnp.where(jnp.broadcast_to(_validS2[0:1, None, None, :], (1, 1, 128, 77)), 0, 1).astype(jnp.int32)
        return (x, ctx_1024, mask_1x1xSxS2_ik0)
    x, ctx_1024, mask_1x1xSxS2_ik0 = _rec_inputs()

    def _L0_xattn_setup():
        import jax, jax.numpy as jnp
        import numpy as np
        HIDDEN = 128
        H = 16
        HK = 4
        G = H // HK
        D = 64
        EPS = 1e-06

        def rmsnorm(x, w):
            var = jnp.mean(jnp.square(x), axis=-1, keepdims=True)
            return x * jax.lax.rsqrt(var + EPS) * w
        key = jax.random.key(seed)
        ks = jax.random.split(key, 8)
        B, S_KV, S_Q = (2, 512, 64)
        inputs = jax.random.normal(ks[0], (B, S_KV, HIDDEN), dtype=jnp.float32)
        latent = jax.random.normal(ks[1], (B, S_Q, HIDDEN), dtype=jnp.float32)

        def xavier(k, shape, gain=1.0):
            fan_out, fan_in = shape
            limit = gain * np.sqrt(6.0 / (fan_in + fan_out))
            return jax.random.uniform(k, shape, jnp.float32, -limit, limit)
        wq = xavier(ks[2], (H * D, HIDDEN))
        wk = xavier(ks[3], (HK * D, HIDDEN))
        wv = xavier(ks[4], (HK * D, HIDDEN))
        wo = xavier(ks[5], (HIDDEN, H * D), gain=1.0 / np.sqrt(2.0))
        q_norm_w = jnp.ones((D,), jnp.float32)
        k_norm_w = jnp.ones((D,), jnp.float32)
        return {'inputs': inputs, 'latent': latent, 'wq': wq, 'wk': wk, 'wv': wv, 'wo': wo, 'q_norm_w': q_norm_w, 'k_norm_w': k_norm_w}
    _L0_xattn_all = _L0_xattn_setup()
    _L0_xattn_in = {k: v for k, v in _L0_xattn_all.items() if k in ('wq', 'wk', 'wv', 'wo', 'q_norm_w', 'k_norm_w')}
    del _L0_xattn_all

    def _L0_ffn_setup():
        import jax, jax.numpy as jnp
        import numpy as np
        TOP_K = 2
        key = jax.random.key(seed)
        k0, k1, k2, k3, k4 = jax.random.split(key, 5)
        B, S, H, I, E = (1, 512, 128, 256, 8)
        hidden_states = jax.random.normal(k0, (B, S, H), dtype=jnp.float32)
        wg = jax.random.normal(k1, (E, H), dtype=jnp.float32) * 0.02
        w1 = jax.random.normal(k2, (E, I, H), dtype=jnp.float32) * 0.02
        w3 = jax.random.normal(k3, (E, I, H), dtype=jnp.float32) * 0.02
        w2 = jax.random.normal(k4, (E, H, I), dtype=jnp.float32) * 0.02
        return {'hidden_states': hidden_states, 'wg': wg, 'w1': w1, 'w3': w3, 'w2': w2}
    _L0_ffn_all = _L0_ffn_setup()
    _L0_ffn_in = {k: v for k, v in _L0_ffn_all.items() if k in ('wg', 'w1', 'w3', 'w2')}
    del _L0_ffn_all

    def _L1_xattn_setup():
        import jax, jax.numpy as jnp
        import numpy as np
        D_MODEL = 128
        H = 16
        D_K = D_MODEL // H
        NEG = -1000000000.0
        key = jax.random.key(seed)
        ks = jax.random.split(key, 7)
        B, S = (4, 256)
        q = jax.random.normal(ks[0], (B, S, D_MODEL), dtype=jnp.float32)
        k = jax.random.normal(ks[1], (B, S, D_MODEL), dtype=jnp.float32)
        v = jax.random.normal(ks[2], (B, S, D_MODEL), dtype=jnp.float32)
        mask = jnp.tril(jnp.ones((S, S), dtype=jnp.int32))[None, None, :, :]
        scale = 0.02
        w_q = jax.random.normal(ks[3], (D_MODEL, D_MODEL), dtype=jnp.float32) * scale
        w_k = jax.random.normal(ks[4], (D_MODEL, D_MODEL), dtype=jnp.float32) * scale
        w_v = jax.random.normal(ks[5], (D_MODEL, D_MODEL), dtype=jnp.float32) * scale
        w_o = jax.random.normal(ks[6], (D_MODEL, D_MODEL), dtype=jnp.float32) * scale
        return {'q': q, 'k': k, 'v': v, 'mask': mask, 'w_q': w_q, 'w_k': w_k, 'w_v': w_v, 'w_o': w_o}
    _L1_xattn_all = _L1_xattn_setup()
    _L1_xattn_in = {k: v for k, v in _L1_xattn_all.items() if k in ('w_q', 'w_k', 'w_v', 'w_o')}
    del _L1_xattn_all

    def _L1_ffn_setup():
        import jax, jax.numpy as jnp
        import numpy as np
        DIM = 128
        DEPTH = 2
        HEADS = 8
        DIM_HEAD = 64
        WINDOW = 64
        INNER = HEADS * DIM_HEAD
        HID = int(DIM * 4 * 2 / 3)
        B, N = (2, 1024)
        QK_SCALE = 8.0

        def shift_token(t):
            t1, t2 = jnp.split(t, 2, axis=-1)
            t2 = jnp.pad(t2, ((0, 0), (1, 0), (0, 0)))[:, :-1]
            return jnp.concatenate([t1, t2], axis=-1)

        def l2norm(t):
            return t / jnp.clip(jnp.linalg.norm(t, axis=-1, keepdims=True), 1e-12)

        def rotate_half(x):
            x1, x2 = jnp.split(x, 2, axis=-1)
            return jnp.concatenate([-x2, x1], axis=-1)

        def rotary_xpos(q, k):
            n = q.shape[-2]
            half_idx = jnp.arange(0, DIM_HEAD, 2, dtype=jnp.float32)
            inv_freq = 1.0 / 10000.0 ** (half_idx / DIM_HEAD)
            t = jnp.arange(n, dtype=jnp.float32)
            freqs = t[:, None] * inv_freq[None, :]
            freqs = jnp.concatenate([freqs, freqs], axis=-1)
            base = (half_idx + 0.4 * DIM_HEAD) / (1.4 * DIM_HEAD)
            power = (t - n // 2) / float(WINDOW // 2)
            scale = base[None, :] ** power[:, None]
            scale = jnp.concatenate([scale, scale], axis=-1)
            cos, sin = (jnp.cos(freqs), jnp.sin(freqs))
            q = q * cos * scale + rotate_half(q) * sin * scale
            k = k * cos / scale + rotate_half(k) * sin / scale
            return (q, k)

        def local_attention(q, k, v):
            b, h, n, d = q.shape
            w = n // WINDOW
            bq = q.reshape(b, h, w, WINDOW, d) * QK_SCALE
            bk = k.reshape(b, h, w, WINDOW, d)
            bv = v.reshape(b, h, w, WINDOW, d)

            def look_around(t):
                p = jnp.pad(t, ((0, 0), (0, 0), (1, 0), (0, 0), (0, 0)))
                return jnp.concatenate([p[:, :, :w], p[:, :, 1:]], axis=3)
            bk, bv = (look_around(bk), look_around(bv))
            bt = jnp.arange(n).reshape(w, WINDOW)
            btp = jnp.pad(bt, ((1, 0), (0, 0)), constant_values=-1)
            btk = jnp.concatenate([btp[:w], btp[1:]], axis=1)
            sim = jnp.einsum('bhwid,bhwjd->bhwij', bq, bk)
            i = bt[:, :, None]
            j = btk[:, None, :]
            mask = (i < j) | (i > j + WINDOW) | (j == -1)
            sim = jnp.where(mask, -jnp.finfo(sim.dtype).max, sim)
            attn = jax.nn.softmax(sim, axis=-1)
            out = jnp.einsum('bhwij,bhwjd->bhwid', attn, bv)
            return out.reshape(b, h, n, d)

        def _layer(x, wqkv, qs, ksc, wo, lg, lb, w1, b1, w2, b2):
            b, n, _ = x.shape
            h = shift_token(x)
            qkv = h @ wqkv
            q, k, v = jnp.split(qkv, 3, axis=-1)
            to_heads = lambda t: t.reshape(b, n, HEADS, DIM_HEAD).transpose(0, 2, 1, 3)
            q, k, v = (to_heads(q), to_heads(k), to_heads(v))
            q = l2norm(q) * qs
            k = l2norm(k) * ksc
            q, k = rotary_xpos(q, k)
            o = local_attention(q, k, v)
            o = o.transpose(0, 2, 1, 3).reshape(b, n, INNER)
            x = x + o @ wo
            h = shift_token(x)
            mu = h.mean(-1, keepdims=True)
            var = h.var(-1, keepdims=True)
            h = (h - mu) / jnp.sqrt(var + 1e-05) * lg + lb
            h = h @ w1 + b1
            a, g = jnp.split(h, 2, axis=-1)
            h = a * jax.nn.gelu(g, approximate=False)
            x = x + h @ w2 + b2
            return x
        key = jax.random.key(seed)
        ks = jax.random.split(key, 6)
        return {'x': jax.random.normal(ks[0], (B, N, DIM), jnp.float32), 'wqkv': jax.random.normal(ks[1], (DEPTH, DIM, 3 * INNER), jnp.float32) * 0.02, 'q_scale': jnp.ones((DEPTH, DIM_HEAD), jnp.float32), 'k_scale': jnp.ones((DEPTH, DIM_HEAD), jnp.float32), 'wo': jax.random.normal(ks[2], (DEPTH, INNER, DIM), jnp.float32) * 0.02, 'ln_g': jnp.ones((DEPTH, DIM), jnp.float32), 'ln_b': jnp.zeros((DEPTH, DIM), jnp.float32), 'w1': jax.random.normal(ks[3], (DEPTH, DIM, 2 * HID), jnp.float32) * 0.02, 'b1': jnp.zeros((DEPTH, 2 * HID), jnp.float32), 'w2': jax.random.normal(ks[4], (DEPTH, HID, DIM), jnp.float32) * 0.02, 'b2': jnp.zeros((DEPTH, DIM), jnp.float32)}
    _L1_ffn_all = _L1_ffn_setup()
    _L1_ffn_in = {k: v for k, v in _L1_ffn_all.items() if k in ('wqkv', 'q_scale', 'k_scale', 'wo', 'ln_g', 'ln_b', 'w1', 'b1', 'w2', 'b2')}
    del _L1_ffn_all
    return {'x': x, 'ctx_1024': ctx_1024, 'mask_1x1xSxS2_ik0': mask_1x1xSxS2_ik0, 'L0_xattn_wq': _L0_xattn_in['wq'], 'L0_xattn_wk': _L0_xattn_in['wk'], 'L0_xattn_wv': _L0_xattn_in['wv'], 'L0_xattn_wo': _L0_xattn_in['wo'], 'L0_xattn_q_norm_w': _L0_xattn_in['q_norm_w'], 'L0_xattn_k_norm_w': _L0_xattn_in['k_norm_w'], 'L0_ffn_wg': _L0_ffn_in['wg'], 'L0_ffn_w1': _L0_ffn_in['w1'], 'L0_ffn_w3': _L0_ffn_in['w3'], 'L0_ffn_w2': _L0_ffn_in['w2'], 'L1_xattn_w_q': _L1_xattn_in['w_q'], 'L1_xattn_w_k': _L1_xattn_in['w_k'], 'L1_xattn_w_v': _L1_xattn_in['w_v'], 'L1_xattn_w_o': _L1_xattn_in['w_o'], 'L1_ffn_wqkv': _L1_ffn_in['wqkv'], 'L1_ffn_q_scale': _L1_ffn_in['q_scale'], 'L1_ffn_k_scale': _L1_ffn_in['k_scale'], 'L1_ffn_wo': _L1_ffn_in['wo'], 'L1_ffn_ln_g': _L1_ffn_in['ln_g'], 'L1_ffn_ln_b': _L1_ffn_in['ln_b'], 'L1_ffn_w1': _L1_ffn_in['w1'], 'L1_ffn_b1': _L1_ffn_in['b1'], 'L1_ffn_w2': _L1_ffn_in['w2'], 'L1_ffn_b2': _L1_ffn_in['b2']}

def reference(x, ctx_1024, mask_1x1xSxS2_ik0, L0_xattn_wq, L0_xattn_wk, L0_xattn_wv, L0_xattn_wo, L0_xattn_q_norm_w, L0_xattn_k_norm_w, L0_ffn_wg, L0_ffn_w1, L0_ffn_w3, L0_ffn_w2, L1_xattn_w_q, L1_xattn_w_k, L1_xattn_w_v, L1_xattn_w_o, L1_ffn_wqkv, L1_ffn_q_scale, L1_ffn_k_scale, L1_ffn_wo, L1_ffn_ln_g, L1_ffn_ln_b, L1_ffn_w1, L1_ffn_b1, L1_ffn_w2, L1_ffn_b2):
    import jax
    import jax.numpy as jnp

    def _L0_xattn_ref(inputs, latent, wq, wk, wv, wo, q_norm_w, k_norm_w):
        import jax, jax.numpy as jnp
        import numpy as np
        HIDDEN = 128
        H = 16
        HK = 4
        G = H // HK
        D = 64
        EPS = 1e-06

        def rmsnorm(x, w):
            var = jnp.mean(jnp.square(x), axis=-1, keepdims=True)
            return x * jax.lax.rsqrt(var + EPS) * w
        B, S_q, _ = latent.shape
        S_kv = inputs.shape[1]
        q = (latent @ wq.T).reshape(B, S_q, H, D)
        k = (inputs @ wk.T).reshape(B, S_kv, HK, D)
        v = (inputs @ wv.T).reshape(B, S_kv, HK, D)
        q = rmsnorm(q, q_norm_w)
        k = rmsnorm(k, k_norm_w)
        q = q.transpose(0, 2, 1, 3).reshape(B, HK, G, S_q, D)
        k = k.transpose(0, 2, 1, 3)
        v = v.transpose(0, 2, 1, 3)
        scores = jnp.einsum('bkgqd,bksd->bkgqs', q, k)
        attn = jax.nn.softmax(scores.astype(jnp.float32), axis=-1).astype(q.dtype)
        out = jnp.einsum('bkgqs,bksd->bkgqd', attn, v)
        out = out.reshape(B, H, S_q, D).transpose(0, 2, 1, 3).reshape(B, S_q, H * D)
        return out @ wo.T

    def _L0_ffn_ref(hidden_states, wg, w1, w3, w2):
        import jax, jax.numpy as jnp
        import numpy as np
        TOP_K = 2
        orig_shape = hidden_states.shape
        H = orig_shape[-1]
        E = wg.shape[0]
        x = hidden_states.reshape(-1, H)
        router_logits = x @ wg.T
        probs = jax.nn.softmax(router_logits, axis=-1)
        topk_w, topk_idx = jax.lax.top_k(probs, TOP_K)
        topk_w = topk_w / jnp.sum(topk_w, axis=-1, keepdims=True)
        expert_w = jnp.sum(jax.nn.one_hot(topk_idx, E, dtype=x.dtype) * topk_w[..., None], axis=1)
        h1 = jnp.einsum('th,eih->tei', x, w1)
        h3 = jnp.einsum('th,eih->tei', x, w3)
        y = jnp.einsum('tei,ehi->teh', jax.nn.silu(h1) * h3, w2)
        out = jnp.einsum('te,teh->th', expert_w, y)
        return out.reshape(orig_shape)

    def _L1_xattn_ref(q, k, v, mask, w_q, w_k, w_v, w_o):
        import jax, jax.numpy as jnp
        import numpy as np
        D_MODEL = 128
        H = 16
        D_K = D_MODEL // H
        NEG = -1000000000.0
        B, S, _ = q.shape

        def proj(x, w):
            return (x @ w.T).reshape(B, -1, H, D_K).transpose(0, 2, 1, 3)
        query = proj(q, w_q)
        key_ = proj(k, w_k)
        value = proj(v, w_v)
        scores = jnp.einsum('bhqd,bhkd->bhqk', query, key_) / jnp.sqrt(jnp.asarray(D_K, dtype=query.dtype))
        scores = jnp.where(mask == 0, jnp.asarray(NEG, dtype=scores.dtype), scores)
        attn = jax.nn.softmax(scores, axis=-1)
        out = jnp.einsum('bhqk,bhkd->bhqd', attn, value)
        out = out.transpose(0, 2, 1, 3).reshape(B, -1, H * D_K)
        return out @ w_o.T

    def _L1_ffn_ref(x, wqkv, q_scale, k_scale, wo, ln_g, ln_b, w1, b1, w2, b2):
        import jax, jax.numpy as jnp
        import numpy as np
        DIM = 128
        DEPTH = 2
        HEADS = 8
        DIM_HEAD = 64
        WINDOW = 64
        INNER = HEADS * DIM_HEAD
        HID = int(DIM * 4 * 2 / 3)
        B, N = (2, 1024)
        QK_SCALE = 8.0

        def shift_token(t):
            t1, t2 = jnp.split(t, 2, axis=-1)
            t2 = jnp.pad(t2, ((0, 0), (1, 0), (0, 0)))[:, :-1]
            return jnp.concatenate([t1, t2], axis=-1)

        def l2norm(t):
            return t / jnp.clip(jnp.linalg.norm(t, axis=-1, keepdims=True), 1e-12)

        def rotate_half(x):
            x1, x2 = jnp.split(x, 2, axis=-1)
            return jnp.concatenate([-x2, x1], axis=-1)

        def rotary_xpos(q, k):
            n = q.shape[-2]
            half_idx = jnp.arange(0, DIM_HEAD, 2, dtype=jnp.float32)
            inv_freq = 1.0 / 10000.0 ** (half_idx / DIM_HEAD)
            t = jnp.arange(n, dtype=jnp.float32)
            freqs = t[:, None] * inv_freq[None, :]
            freqs = jnp.concatenate([freqs, freqs], axis=-1)
            base = (half_idx + 0.4 * DIM_HEAD) / (1.4 * DIM_HEAD)
            power = (t - n // 2) / float(WINDOW // 2)
            scale = base[None, :] ** power[:, None]
            scale = jnp.concatenate([scale, scale], axis=-1)
            cos, sin = (jnp.cos(freqs), jnp.sin(freqs))
            q = q * cos * scale + rotate_half(q) * sin * scale
            k = k * cos / scale + rotate_half(k) * sin / scale
            return (q, k)

        def local_attention(q, k, v):
            b, h, n, d = q.shape
            w = n // WINDOW
            bq = q.reshape(b, h, w, WINDOW, d) * QK_SCALE
            bk = k.reshape(b, h, w, WINDOW, d)
            bv = v.reshape(b, h, w, WINDOW, d)

            def look_around(t):
                p = jnp.pad(t, ((0, 0), (0, 0), (1, 0), (0, 0), (0, 0)))
                return jnp.concatenate([p[:, :, :w], p[:, :, 1:]], axis=3)
            bk, bv = (look_around(bk), look_around(bv))
            bt = jnp.arange(n).reshape(w, WINDOW)
            btp = jnp.pad(bt, ((1, 0), (0, 0)), constant_values=-1)
            btk = jnp.concatenate([btp[:w], btp[1:]], axis=1)
            sim = jnp.einsum('bhwid,bhwjd->bhwij', bq, bk)
            i = bt[:, :, None]
            j = btk[:, None, :]
            mask = (i < j) | (i > j + WINDOW) | (j == -1)
            sim = jnp.where(mask, -jnp.finfo(sim.dtype).max, sim)
            attn = jax.nn.softmax(sim, axis=-1)
            out = jnp.einsum('bhwij,bhwjd->bhwid', attn, bv)
            return out.reshape(b, h, n, d)

        def _layer(x, wqkv, qs, ksc, wo, lg, lb, w1, b1, w2, b2):
            b, n, _ = x.shape
            h = shift_token(x)
            qkv = h @ wqkv
            q, k, v = jnp.split(qkv, 3, axis=-1)
            to_heads = lambda t: t.reshape(b, n, HEADS, DIM_HEAD).transpose(0, 2, 1, 3)
            q, k, v = (to_heads(q), to_heads(k), to_heads(v))
            q = l2norm(q) * qs
            k = l2norm(k) * ksc
            q, k = rotary_xpos(q, k)
            o = local_attention(q, k, v)
            o = o.transpose(0, 2, 1, 3).reshape(b, n, INNER)
            x = x + o @ wo
            h = shift_token(x)
            mu = h.mean(-1, keepdims=True)
            var = h.var(-1, keepdims=True)
            h = (h - mu) / jnp.sqrt(var + 1e-05) * lg + lb
            h = h @ w1 + b1
            a, g = jnp.split(h, 2, axis=-1)
            h = a * jax.nn.gelu(g, approximate=False)
            x = x + h @ w2 + b2
            return x
        for l in range(DEPTH):
            x = _layer(x, wqkv[l], q_scale[l], k_scale[l], wo[l], ln_g[l], ln_b[l], w1[l], b1[l], w2[l], b2[l])
        return x
    x = x + _L0_xattn_ref(ctx_1024, _layernorm(x, axis=-1), L0_xattn_wq, L0_xattn_wk, L0_xattn_wv, L0_xattn_wo, L0_xattn_q_norm_w, L0_xattn_k_norm_w)
    x = x + _L0_ffn_ref(_layernorm(x, axis=-1), L0_ffn_wg, L0_ffn_w1, L0_ffn_w3, L0_ffn_w2)
    x = x + _L1_xattn_ref(_layernorm(x, axis=-1), ctx_1024, ctx_1024, mask_1x1xSxS2_ik0, L1_xattn_w_q, L1_xattn_w_k, L1_xattn_w_v, L1_xattn_w_o)
    x = x + _L1_ffn_ref(_layernorm(x, axis=-1), L1_ffn_wqkv, L1_ffn_q_scale, L1_ffn_k_scale, L1_ffn_wo, L1_ffn_ln_g, L1_ffn_ln_b, L1_ffn_w1, L1_ffn_b1, L1_ffn_w2, L1_ffn_b2)
    return x

_drawn_inputs = setup_inputs


def setup_inputs(seed=0):
    import zlib

    import numpy as np

    out = dict(_drawn_inputs(seed))
    spreads = {'L0_xattn_q_norm_w': (1.0, 0.2),
     'L0_xattn_k_norm_w': (1.0, 0.2),
     'L1_ffn_q_scale': (1.0, 0.6),
     'L1_ffn_k_scale': (1.0, 0.6),
     'L1_ffn_ln_g': (1.0, 0.6),
     'L1_ffn_ln_b': (0.0, 0.8),
     'L1_ffn_b1': (0.0, 0.8),
     'L1_ffn_b2': (0.0, 0.8)}
    factors = {'L0_ffn_wg': 8.0,
     'L0_ffn_w1': 8.0,
     'L0_ffn_w3': 8.0,
     'L0_ffn_w2': 8.0,
     'L1_xattn_w_q': 54.2,
     'L1_xattn_w_k': 52.16,
     'L1_ffn_w1': 7.275,
     'L1_ffn_w2': 7.107,
     'L1_xattn_w_v': 4.085,
     'L1_xattn_w_o': 4.15}
    for name, (base, spread) in spreads.items():
        noise = np.random.default_rng([zlib.crc32(name.encode()), seed]).standard_normal(out[name].shape)
        drawn = base * np.exp(spread * noise) if base else spread * noise
        out[name] = jnp.asarray(drawn.astype(out[name].dtype))
    for name, factor in factors.items():
        out[name] = (out[name] * factor).astype(out[name].dtype)
    return out
```

```python
from contextlib import ExitStack

import numpy as np

import concourse.bass as bass
from concourse import mybir

F32 = mybir.dt.float32
F32R = mybir.dt.float32r
BF16 = mybir.dt.bfloat16
I32 = mybir.dt.int32
ALU = mybir.AluOpType
ACT = mybir.ActivationFunctionType
AX = mybir.AxisListType

NB = 32
T = 128
D = 128
SK = 77
H0, HK0, DH0 = 16, 4, 64
NE, INTER = 8, 256
NCH = NE * INTER // 128
H1, DH1 = 16, 8
DEPTH, HL, DL = 2, 8, 64
WINDOW = 64
HID = int(D * 4 * 2 / 3)
HC = [128, 128, HID - 256]
GB = 4
NG = NB // GB
LN_EPS = 1e-5
RMS_EPS = 1e-6
NEG = -1e9
BAND = -1e30


class It:

    def __init__(self, i, phase, n, unroll):
        self.i, self.phase, self.n, self.unroll = i, phase, n, unroll
        self.static = type(i) is int

    def b(self, lag):
        if self.static and not 0 <= self.i - lag < self.n:
            return None
        return self.i - lag

    def m(self, lag, size):
        return (self.phase - lag) % size

    def seen(self, lag):
        return not self.static or self.i >= lag

    def upto(self, lag, base=0):
        last = min(self.i - lag, self.n - 1) if self.static else self.i - lag
        return last + base + 1


def pipeline(eng, n, lags, unroll, body):
    assert lags % unroll == 0 and (n - lags) % unroll == 0
    for i in range(lags):
        body(It(i, i % unroll, n, unroll))
    with eng.Fori(lags, n - unroll + 1, unroll) as r:
        for u in range(unroll):
            body(It(r + u, u, n, unroll))
    for i in range(n, n + lags):
        body(It(i, i % unroll, n, unroll))


def past(b):
    return type(b) is not int or b >= 0


def count(b, j=1, k=1, base=0):
    return (b + base) * k + j


def program(nc, out, x_in, ctx_in, mask_in, wq0_in, wkv0_in, wo0_in, nrm0_in, wg_in, w1e_in, w3e_in, w2e_in,
            l1_in, wqkv_in, qks_in, wol_in, lng_in, w1l_in, b1l_in, w2l_in,
            ident_in, band_in, rot_in, keyi_in, head_in):
    with ExitStack() as ctx:
        def sem(name):
            return ctx.enter_context(nc.semaphore(name))

        first = (nc.sbuf_base + 31) // 32 * 32
        room = [first]

        def at(name, shape, dt=F32):
            size = 2 if dt == BF16 else 4
            for n in shape[1:]:
                size *= n
            t = nc.alloc_sbuf_tensor_at(name, shape, dt, offset=room[0])
            room[0] += (size + 31) // 32 * 32
            assert room[0] <= nc.sbuf_usable_end, name
            return t

        R = [ctx.enter_context(nc.psum_tensor(f"slot{i}", [128, 2, 512], F32)) for i in range(4)]

        def bank(k):
            return R[k // 2][:, k % 2, :]

        X = at("X", [128, NB, D])
        mv = at("mv", [128, NB, 2])
        agg = at("agg", [128, GB, 2])
        eps = at("eps", [128, GB, 2])
        rs = at("rs", [128, NB])
        ident = at("ident", [128, 128])
        identb = at("identb", [128, 128], BF16)
        band = at("band", [128, 128])
        bandb = at("bandb", [128, 4, 128], BF16)
        mask = at("mask", [128, SK], I32)
        maskz = at("maskz", [128, SK], I32)
        negt = at("negt", [128, SK])
        nhalf = at("nhalf", [128, 32])
        head = at("head", [128, 4])
        keyi = at("keyi", [128, GB, NE])
        nrm0 = at("nrm0", [128, 2])
        st = at("st", [128, 4, 6])
        stage = at("stage", [128, 2, 2048])
        wol = at("wol", [128, DEPTH, 4, 128])
        w2l = at("w2l", [128, DEPTH, 3, 128])
        lng = at("lng", [128, DEPTH, 2])
        b1l = at("b1l", [128, DEPTH, 6])
        rot = at("rot", [128, 2, 2, 64])
        qks = at("qks", [128, DEPTH, 2, 2, 64])
        T1 = at("T1", [128, DEPTH, 2, 64])
        T2 = at("T2", [128, DEPTH, 2, 64])

        attentions = room[0]
        wq0 = [at(f"wq0{p}", [128, H0 * DH0], F32R) for p in "hl"]
        wkv0 = [at(f"wkv0{p}", [128, 512], F32R) for p in "hl"]
        wo0 = at("wo0", [128, 8, 128])
        l1 = at("l1", [128, 4, 128])
        l1s = [at(f"l1{p}", [128, 3, 128], F32R) for p in "hl"]
        wgs = [at(f"wg{p}", [128, NE], F32R) for p in "hl"]
        wg = at("wg", [128, NE])
        experts = room[0]
        w1e = [at(f"w1e{p}", [128, 2048], F32R) for p in "hl"]
        w3e = [at(f"w3e{p}", [128, 2048], F32R) for p in "hl"]
        w2e = [at(f"w2e{p}", [128, NCH, 128], F32R) for p in "hl"]
        weights_end = room[0]
        room[0] = attentions
        H2 = at("H2", [128, NB, D])
        assert room[0] <= experts
        room[0] = experts
        wqkv = [[at(f"wqkv{l}{p}", [128, 1536], F32R) for p in "hl"] for l in range(DEPTH)]
        w1l = [[at(f"w1l{l}{p}", [128, 2 * HID], F32R) for p in "hl"] for l in range(DEPTH)]
        assert room[0] <= weights_end
        room[0] = weights_end
        ctx_sb = at("ctx_sb", [128, NB, SK])
        ctx_end = room[0]
        a = {}
        a["xn"] = at("ac_xn", [128, 2, 128])
        a["xT"] = [at(f"a_xT{p}", [128, 2, 128], F32R) for p in "hl"]
        a["c"] = [at(f"a_c{p}", [128, 4, SK], F32R) for p in "hl"]
        a["sq"] = at("a_sq", [128, 1024])
        a["sqk"] = at("a_sqk", [128, 256])
        a["kr"] = at("a_kr", [128, 2, 256])
        a["ss"] = at("a_ss", [128, 2, 20])
        a["vv"] = at("a_vv", [128, 2, 20])
        a["r"] = at("a_r", [128, 2, 20])
        a["kn"] = at("a_kn", [128, 2, 4, 2, 64])
        a["v1"] = at("a_v1", [128, 4, 4, 65])
        a["kT"] = at("a_kT", [128, 2, 4, SK])
        a["wqk"] = at("a_wqk", [128, 1])
        a["qn"] = at("a_qn", [128, 2, 1024])
        a["qT"] = at("a_qT", [128, 8, 128])
        a["nm"] = at("a_nm", [128, 2, 16])
        a["p"] = at("a_p", [128, 2, 16, SK])
        a["pT"] = at("a_pT", [128, 16, 128])
        a["rc"] = at("a_rc", [128, 16])
        a["on"] = at("a_on", [128, 2, 1024])
        a["oT"] = at("a_oT", [128, 8, 128])
        room[0] = ctx_end
        g_ = {}
        g_["xn"] = at("b_xn", [128, GB, 128])
        g_["xT"] = [at(f"b_xT{p}", [128, 2, 512], F32R) for p in "hl"]
        g_["wt"] = at("b_wt", [128, 2, GB, NE])
        g_["wb"] = at("b_wb", [128, 2, 512])
        g_["s"] = at("b_s", [128, 2, 512])
        g_["sp"] = at("b_sp", [128, 2, 512])
        g_["g"] = at("b_g", [128, 4, 512])
        g_["gs"] = [at(f"b_g{p}", [128, 4, 512], F32R) for p in "hl"]
        g_["yT"] = at("b_yT", [128, 512])
        for n in ("m", "s", "rc", "m1", "k1", "m2", "k2", "dn", "rd"):
            g_["r" + n] = at("b_r" + n, [128, GB])
        for n in ("l", "e", "p", "q", "k", "o", "q2", "e2", "k2", "o2", "t"):
            g_["R" + n] = at("b_R" + n, [128, GB, NE])
        room[0] = ctx_end
        c_ = {}
        c_["xn"] = at("ac_xn", [128, 2, 128])
        c_["xT"] = [at(f"c_xT{p}", [128, 2, 128], F32R) for p in "hl"]
        c_["c"] = [at(f"c_c{p}", [128, 4, SK + 1], F32R) for p in "hl"]
        c_["qT"] = at("c_qT", [128, 2, 128])
        c_["kb"] = at("c_kb", [128, 2, 4, SK])
        c_["v1"] = at("c_v1", [128, 4, 16, 9])
        c_["nm"] = at("c_nm", [128, 2, 16])
        c_["p"] = at("c_p", [128, 2, 16, SK])
        c_["pT"] = at("c_pT", [128, 16, 128])
        c_["rc"] = at("c_rc", [128, 16])
        c_["on"] = at("c_on", [128, 2, 128])
        c_["oT"] = at("c_oT", [128, 128])
        room[0] = weights_end
        Z = at("Z", [128, NB, D])
        d = {}
        d["v1"] = at("d_v1", [128, 4, HL, 65])
        d["hT"] = [at(f"d_hT{p}", [128, 2, 128], F32R) for p in "hl"]
        both = room[0]
        d["sq"] = at("d_sq", [128, 1024])
        d["ss"] = at("d_ss", [128, 2, 16])
        d["vv"] = at("d_vv", [128, 2, 16])
        d["r"] = at("d_r", [128, 2, 16])
        d["z"] = at("d_zx", [128, 2, 128])
        d["A"] = at("d_A", [128, 2, 1024])
        d["B"] = at("d_B", [128, 2, 1024])
        d["qT"] = at("d_qT", [128, 8, 128])
        d["nm"] = at("d_nm", [128, 2, 8])
        d["p"] = at("d_p", [128, 2, 8, 128])
        d["pT"] = at("d_pT", [128, 8, 128])
        d["rc"] = at("d_rc", [128, 8])
        d["on"] = at("d_on", [128, 2, 512])
        d["oT"] = at("d_oT", [128, 4, 128])
        room[0] = both
        f = {}
        f["xn"] = at("f_xn", [128, GB, 128])
        f["hn"] = at("f_hn", [128, 2, 512])
        f["hs"] = [at(f"f_h{p}", [128, 2, 512], F32R) for p in "hl"]
        f["gl"] = at("f_gl", [128, 3, 512])
        f["gt"] = at("f_gt", [128, 2, 3, 512])
        f["o"] = at("f_o", [128, 2, 512])

        made = {}

        def S(name):
            if name not in made:
                made[name] = sem(name)
            return made[name]

        def load(e):
            e.dma_start(X[:, 0:16, :], x_in[:, 0:2048].rearrange("p (b d) -> p b d", d=D)).then_inc(S("x_in"), 16)
            e.dma_start(X[:, 16:32, :], x_in[:, 2048:4096].rearrange("p (b d) -> p b d", d=D)).then_inc(S("x_in"), 16)
            e.dma_start(stage[:, 0, 0:1024], wq0_in).then_inc(S("stage0_in"), 16)
            e.dma_start(stage[:, 1, 0:512], wkv0_in).then_inc(S("stage1_in"), 16)
            for dst, src in ((wo0, wo0_in), (ident, ident_in), (band, band_in), (mask, mask_in), (head, head_in),
                             (keyi, keyi_in), (nrm0, nrm0_in), (wg, wg_in), (l1, l1_in), (wol, wol_in), (w2l, w2l_in),
                             (lng, lng_in), (b1l, b1l_in), (rot, rot_in), (qks, qks_in)):
                names = "abcd"[:len(dst.shape) - 1]
                e.dma_start(dst[:].rearrange(f"p {' '.join(names)} -> p ({' '.join(names)})"), src)\
                    .then_inc(S("const_in"), 16)
            for n, src in enumerate((w1e_in, w3e_in, w2e_in)):
                e.wait_ge(S("split"), n + 1)
                e.dma_start(stage[:, n % 2, :], src).then_inc(S(f"stage{n % 2}_in"), 16)
            e.wait_ge(S("split"), 5)
            e.dma_start(ctx_sb[:].rearrange("p b s -> p (b s)"), ctx_in).then_inc(S("ctx_in"), 16)

        N_CONST = 15

        def split_act(e):
            for n, (dst, w) in enumerate(((wq0[0][:], 1024), (wkv0[0][:], 512), (w1e[0][:], 2048), (w3e[0][:], 2048),
                                          (w2e[0][:].rearrange("p a b -> p (a b)"), 2048))):
                e.wait_ge(S(f"stage{n % 2}_in"), 16 * (n // 2 + 1))
                e.activation(dst, stage[:, n % 2, 0:w], ACT.Copy).then_inc(S("high"), 1)
            e.wait_ge(S("const_in"), 16 * N_CONST)
            e.activation(wgs[0][:], wg[:], ACT.Copy).then_inc(S("high"), 1)
            e.activation(l1s[0][:], l1[:, 0:3, :], ACT.Copy).then_inc(S("high"), 1)
            e.activation(identb[:], ident[:], ACT.Copy).then_inc(S("high"), 1)
            for k in range(4):
                e.activation(bandb[:, k, :], band[:], ACT.Copy).then_inc(S("high"), 1)

        def split_dve(e):
            e.memset(eps[:, :, 0:1], 0.0).then_inc(S("eps"), 1)
            e.memset(eps[:, :, 1:2], LN_EPS).then_inc(S("eps"), 1)
            e.wait_ge(S("eps"), 2)
            e.wait_ge(S("x_in"), 32)
            with e.Fori(0, NB - GB + 1, GB) as b:
                for u in range(GB):
                    e.bn_stats(st[:, u, :], X[:, bass.ds(b + u, 1), :]).then_inc(S("stat0"), 1)
                for u in range(GB):
                    e.wait_ge(S("stat0"), b + u + 1)
                    apart(e)
                    e.bn_aggr(agg[:, u, :], st[:, u, :]).then_inc(S("stat"), 1)
                e.wait_ge(S("stat"), b + GB)
                e.tensor_tensor(mv[:, bass.ds(b, GB), :], agg[:], eps[:], ALU.add).then_inc(S("var0"), 1)
            e.memset(nhalf[:], -0.5).then_inc(S("var0"), 1)
            e.memset(negt[:], NEG).then_inc(S("const"), 1)
            e.memset(a["v1"][:], 1.0).then_inc(S("const"), 1)
            e.memset(a["ss"][:], 1.0).then_inc(S("const"), 1)
            for n, (hi, lo, w) in enumerate(((wq0[0][:], wq0[1][:], 1024), (wkv0[0][:], wkv0[1][:], 512),
                                             (w1e[0][:], w1e[1][:], 2048), (w3e[0][:], w3e[1][:], 2048),
                                             (w2e[0][:].rearrange("p a b -> p (a b)"),
                                              w2e[1][:].rearrange("p a b -> p (a b)"), 2048))):
                e.wait_ge(S("high"), n + 1)
                e.tensor_tensor(lo, stage[:, n % 2, 0:w], hi.bitcast(F32), ALU.subtract).then_inc(S("split"), 1)
            e.wait_ge(S("high"), 7)
            e.tensor_tensor(wgs[1][:], wg[:], wgs[0][:].bitcast(F32), ALU.subtract).then_inc(S("split"), 1)
            e.tensor_tensor(l1s[1][:], l1[:, 0:3, :], l1s[0][:].bitcast(F32), ALU.subtract).then_inc(S("split"), 1)
            e.tensor_scalar(maskz[:], mask[:], 0.0, None, ALU.is_equal).then_inc(S("const"), 1)
            e.tensor_tensor(a["wqk"][:], nrm0[:, 0:1], nrm0[:, 1:2], ALU.mult).then_inc(S("const"), 1)
            e.wait_ge(S("const"), 5)

        def start_pool(e):
            e.wait_ge(S("var0"), NG + 1)
            e.tensor_tensor(rs[:], mv[:, :, 1], nhalf[:], ALU.pow).then_inc(S("rs"), 1)

        def rows(ap, b):
            return ap[:, bass.ds(b, 1), :]

        def apart(e):
            e.sem_inc(S("apart"), 1)

        def passes(e, o, ws, xs):
            e.matmul(o, ws[1], xs[0], start=True, stop=False)
            e.matmul(o, ws[0], xs[1], start=False, stop=False)
            return e.matmul(o, ws[0], xs[0], start=False, stop=True)


        def a_tensor(e):
            e.wait_ge(S("split"), 7)
            e.wait_ge(S("const"), 5)

            def body(it):
                b = it.b(1)
                if b is not None:
                    p = it.m(1, 2)
                    if past(it.i - 2):
                        e.wait_ge(S("a_qn"), count(it.i - 2))
                    e.wait_ge(S("ac_xl"), count(b))
                    for h in range(2):
                        mm = passes(e, R[0][:, h, :], [x[:, p, :] for x in a["xT"]],
                                    [w[:, 512 * h:512 * h + 512] for w in wq0])
                    mm.then_inc(S("a_projq"), 1)
                    if it.seen(5):
                        e.wait_ge(S("ac_add"), it.upto(5))
                    if it.seen(1):
                        e.wait_ge(S("ac_xl"), it.upto(1))
                    e.wait_ge(S("ac_cl"), count(b))
                    passes(e, R[1][0:SK, 0, :], [c[:, it.m(1, 4), :] for c in a["c"]], [w[:] for w in wkv0])\
                        .then_inc(S("a_kv"), 1)
                b = it.b(2)
                if b is not None:
                    if it.seen(2):
                        e.wait_ge(S("a_kTe"), it.upto(2))
                    e.wait_ge(S("a_qn"), count(b))
                    for c in range(8):
                        mm = e.transpose(R[2][:, c // 4, 128 * (c % 4):128 * (c % 4) + 128],
                                         a["qn"][:, it.m(2, 2), 128 * c:128 * c + 128], ident[:])
                    mm.then_inc(S("a_qT"), 1)
                b = it.b(3)
                if b is not None:
                    for half, slot in ((0, 3), (1, 1)):
                        if half == 0:
                            if it.seen(4):
                                e.wait_ge(S("a_onb"), it.upto(4))
                            if it.static:
                                if it.seen(3):
                                    e.wait_ge(S("ac_suba"), it.upto(3))
                        else:
                            if it.seen(1):
                                e.wait_ge(S("a_kr"), it.upto(1))
                            if it.static:
                                if it.seen(5):
                                    e.wait_ge(S("ac_add"), it.upto(5))
                                if it.seen(1):
                                    e.wait_ge(S("ac_xl"), it.upto(1))
                        e.wait_ge(S(("ac_expa", "ac_expb")[half]), count(b))
                        for c in range(8):
                            mm = e.transpose(R[slot][0:SK, c // 4, 128 * (c % 4):128 * (c % 4) + 128],
                                             a["p"][:, it.m(3, 2), 8 * half + c, :], ident[:])
                        mm.then_inc(S(("ac_PTa", "ac_PTb")[half]), 1)
                b = it.b(4)
                if b is not None:
                    if it.seen(2):
                        e.wait_ge(S("a_qTe"), it.upto(2))
                    if it.static:
                        if it.seen(4):
                            e.wait_ge(S("a_ona"), it.upto(4))
                    e.wait_ge(S("a_onb"), count(b))
                    for c in range(8):
                        mm = e.transpose(R[2][:, c // 4, 128 * (c % 4):128 * (c % 4) + 128],
                                         a["on"][:, it.m(4, 2), 128 * c:128 * c + 128], ident[:])
                    mm.then_inc(S("ac_OT"), 1)
                b = it.b(2)
                if b is not None:
                    e.wait_ge(S("a_qTe"), count(b))
                    e.wait_ge(S("a_kTe"), count(b))
                    for half, slot in ((0, 3), (1, 1)):
                        if half == 0:
                            if it.seen(3):
                                e.wait_ge(S("ac_pTa"), it.upto(3))
                        else:
                            if it.seen(3):
                                e.wait_ge(S("ac_pTb"), it.upto(3))
                            if it.static:
                                if it.seen(1):
                                    e.wait_ge(S("a_kr"), it.upto(1))
                        for k in range(8):
                            h = 8 * half + k
                            o = DH0 * (h % 2)
                            mm = e.matmul(R[slot][:, h % 2, SK * (k // 2):SK * (k // 2) + SK],
                                          a["qT"][o:o + DH0, h // 2, :],
                                          a["kT"][o:o + DH0, it.m(2, 2), h // 4, :], start=True, stop=True)
                        mm.then_inc(S(("ac_Sa", "ac_Sb")[half]), 1)
                b = it.b(3)
                if b is not None:
                    for half, slot in ((0, 2), (1, 3)):
                        if half == 0:
                            if it.seen(4):
                                e.wait_ge(S("ac_oTe"), it.upto(4))
                            if it.static:
                                if it.seen(2):
                                    e.wait_ge(S("a_qTe"), it.upto(2))
                        else:
                            if it.seen(2):
                                e.wait_ge(S("ac_suba"), it.upto(2))
                            if it.static:
                                if it.seen(3):
                                    e.wait_ge(S("ac_pTa"), it.upto(3))
                        e.wait_ge(S(("ac_pTa", "ac_pTb")[half]), count(b))
                        for k in range(8):
                            h = 8 * half + k
                            mm = e.matmul(R[slot][:, k // 4, 65 * (k % 4):65 * (k % 4) + 65],
                                          a["pT"][0:SK, 8 * half + 4 * (k % 2) + k // 2, :],
                                          a["v1"][0:SK, it.m(3, 4), h // 4, :], start=True, stop=True)
                        mm.then_inc(S(("a_PVa", "a_PVb")[half]), 1)
                if it.b(4) is not None or it.b(0) is not None:
                    if it.seen(2):
                        e.wait_ge(S("ac_subb"), it.upto(2))
                    if it.static:
                        if it.seen(1):
                            e.wait_ge(S("a_kr"), it.upto(1))
                        if it.seen(3):
                            e.wait_ge(S("ac_pTb"), it.upto(3))
                        if it.seen(5):
                            e.wait_ge(S("ac_add"), it.upto(5))
                        if it.seen(1):
                            e.wait_ge(S("ac_xl"), it.upto(1))
                b = it.b(4)
                if b is not None:
                    e.wait_ge(S("ac_oTe"), count(b))
                    for c in range(8):
                        mm = e.matmul(R[1][:, 0, 0:128], a["oT"][:, c, :], wo0[:, c, :], start=(c == 0), stop=(c == 7))
                    mm.then_inc(S("ac_wo"), 1)
                b = it.b(0)
                if b is not None:
                    e.wait_ge(S("ac_xn"), count(b))
                    e.transpose(R[1][:, 1, 0:128], a["xn"][:, it.m(0, 2), :], ident[:]).then_inc(S("ac_xTp"), 1)
                b = it.b(1)
                if b is not None:
                    if it.seen(3):
                        e.wait_ge(S("a_ona"), it.upto(3))
                    if it.static:
                        if it.seen(2):
                            e.wait_ge(S("a_qTe"), it.upto(2))
                    e.wait_ge(S("a_kn"), count(b))
                    for c in range(4):
                        mm = e.transpose(R[2][:, 0, SK * c:SK * c + SK],
                                         a["kn"][0:SK, it.m(1, 2), c, :, :].rearrange("p a b -> p (a b)"),
                                         ident[0:SK, 0:SK])
                    mm.then_inc(S("a_kT"), 1)
            pipeline(e, NB, 4, 4, body)

        def a_scalar(e):
            def body(it):
                b = it.b(1)
                if b is not None:
                    e.wait_ge(S("a_projq"), count(b))
                    if past(it.i - 2):
                        e.wait_ge(S("a_redq"), count(it.i - 2))
                    e.activation(a["sq"][:].rearrange("p (a b) -> p a b", a=2), R[0][:], ACT.Square).then_inc(S("a_sq"), 1)
                    e.wait_ge(S("a_kv"), count(b))
                    e.activation(a["v1"][0:SK, it.m(1, 4), :, 0:64],
                                 R[1][0:SK, 0, 256:512].rearrange("p (a b) -> p a b", a=4), ACT.Copy).then_inc(S("a_v"), 1)
                    if past(it.i - 3):
                        e.wait_ge(S("a_kn"), count(it.i - 3))
                    e.activation(a["kr"][0:SK, it.m(1, 2), :], R[1][0:SK, 0, 0:256], ACT.Copy).then_inc(S("a_kr"), 1)
                b = it.b(2)
                if b is not None:
                    e.wait_ge(S("a_qT"), count(b))
                    e.activation(a["qT"][:].rearrange("p (a c) t -> p a (c t)", a=2), R[2][:], ACT.Copy).then_inc(S("a_qTe"), 1)
                b = it.b(3)
                if b is not None:
                    for half, slot in ((0, 3), (1, 1)):
                        e.wait_ge(S(("ac_PTa", "ac_PTb")[half]), count(b))
                        e.activation(a["pT"][0:SK, 8 * half:8 * half + 8, :].rearrange("p (a c) t -> p a (c t)", a=2),
                                     R[slot][0:SK, :, :], ACT.Copy).then_inc(S(("ac_pTa", "ac_pTb")[half]), 1)
                b = it.b(4)
                if b is not None:
                    e.wait_ge(S("ac_OT"), count(b))
                    e.activation(a["oT"][:].rearrange("p (a c) t -> p a (c t)", a=2), R[2][:], ACT.Copy).then_inc(S("ac_oTe"), 1)
                b = it.b(2)
                if b is not None:
                    for half in range(2):
                        e.wait_ge(S(("ac_suba", "ac_subb")[half]), count(b))
                        p = a["p"][:, it.m(2, 2), 8 * half:8 * half + 8, :]
                        e.activation(p, p, ACT.Exp).then_inc(S(("ac_expa", "ac_expb")[half]), 1)
                b = it.b(0)
                if b is not None:
                    e.wait_ge(S("ac_xTp"), count(b))
                    e.activation(a["xT"][0][:, it.m(0, 2), :], R[1][:, 1, 0:128], ACT.Copy).then_inc(S("ac_xh"), 1)
            pipeline(e, NB, 4, 4, body)

        def softmax_less_max(e, it, b, half, slot, ph, t, names, nheads, nk, base=0, base_s=None):
            s = R[slot][:, :, 0:nheads // 2 * nk].rearrange("p a (j k) -> p a j k", k=nk)
            nm = t["nm"][:, it.m(2, 2), nheads * half:nheads * half + nheads]
            e.wait_ge(S(names[0]), count(b, base=base if base_s is None else base_s))
            e.tensor_reduce(nm, s, AX.X, ALU.max, negate=True).then_inc(S(names[1]), 1)
            e.wait_ge(S(names[1]), count(b, base=base))
            e.tensor_tensor(t["p"][:, it.m(2, 2), nheads * half:nheads * half + nheads, :]
                            .rearrange("p (a j) k -> p a j k", a=2), s,
                            nm.rearrange("p (a j) -> p a j", a=2).unsqueeze(3).to_broadcast([128, 2, nheads // 2, nk]),
                            ALU.add).then_inc(S(names[2]), 1)

        def layernorm(e, src, dst, b, m):
            return e.tensor_scalar(dst[:, m:m + 1, :], rows(src, b), mv[:, bass.ds(b, 1), 0:1].rearrange("p a b -> p (a b)"),
                                   rs[:, bass.ds(b, 1)], ALU.subtract, ALU.mult)

        def a_vector(e):
            e.wait_ge(S("rs"), 1)

            def body(it):
                b = it.b(0)
                if b is not None:
                    layernorm(e, X, a["xn"], b, it.m(0, 2)).then_inc(S("ac_xn"), 1)
                b = it.b(1)
                if b is not None:
                    p = it.m(1, 2)
                    e.wait_ge(S("a_sq"), count(b))
                    e.tensor_reduce(a["ss"][:, p, 0:16], a["sq"][:].rearrange("p (h d) -> p h d", d=DH0), AX.X, ALU.add)\
                        .then_inc(S("a_redq"), 1)
                    e.wait_ge(S("a_sqk"), count(b))
                    e.tensor_reduce(a["ss"][0:SK, p, 16:20], a["sqk"][0:SK, :].rearrange("p (h d) -> p h d", d=DH0),
                                    AX.X, ALU.add).then_inc(S("a_redk"), 1)
                b = it.b(2)
                if b is not None:
                    softmax_less_max(e, it, b, 0, 3, "a", a, ("ac_Sa", "ac_nma", "ac_suba"), 8, SK)
                b = it.b(1)
                if b is not None:
                    e.wait_ge(S("a_redk"), count(b))
                    if past(it.i - 3):
                        e.wait_ge(S("a_r"), count(it.i - 3))
                    e.tensor_scalar(a["vv"][:, p, :], a["ss"][:, p, :], 1.0 / DH0, RMS_EPS, ALU.mult, ALU.add)\
                        .then_inc(S("a_vv"), 1)
                b = it.b(2)
                if b is not None:
                    softmax_less_max(e, it, b, 1, 1, "a", a, ("ac_Sb", "ac_nmb", "ac_subb"), 8, SK)
                b = it.b(3)
                if b is not None:
                    for half, slot in ((0, 2), (1, 3)):
                        o = R[slot][:, :, 0:260].rearrange("p a (j k) -> p a j k", k=65)
                        rc = a["rc"][:, 8 * half:8 * half + 8].rearrange("p (a j) -> p a j", a=2)
                        e.wait_ge(S(("a_PVa", "a_PVb")[half]), count(b))
                        e.reciprocal(rc, o[:, :, :, 64]).then_inc(S(("a_rca", "a_rcb")[half]), 1)
                        e.wait_ge(S(("a_rca", "a_rcb")[half]), count(b))
                        e.tensor_tensor(a["on"][:, it.m(3, 2), 512 * half:512 * half + 512]
                                        .rearrange("p (a j k) -> p a j k", a=2, j=4), o[:, :, :, 0:64],
                                        rc.unsqueeze(3).to_broadcast([128, 2, 4, 64]), ALU.mult)\
                            .then_inc(S(("a_ona", "a_onb")[half]), 1)
                b = it.b(1)
                if b is not None:
                    e.wait_ge(S("a_r"), count(b))
                    e.tensor_tensor(a["qn"][:, p, :].rearrange("p (a j k) -> p a j k", a=2, j=8),
                                    R[0][:].rearrange("p a (j k) -> p a j k", k=DH0),
                                    a["r"][:, p, 0:16].rearrange("p (a j) -> p a j", a=2).unsqueeze(3)
                                    .to_broadcast([128, 2, 8, DH0]), ALU.mult).then_inc(S("a_qn"), 1)
                b4 = it.b(4)
                if b4 is not None:
                    e.wait_ge(S("ac_wo"), count(b4))
                    e.tensor_tensor(rows(X, b4), rows(X, b4), R[1][:, 0:1, 0:128], ALU.add).then_inc(S("ac_add"), 1)
                b = it.b(0)
                if b is not None:
                    e.wait_ge(S("ac_xh"), count(b))
                    e.tensor_tensor(a["xT"][1][:, it.m(0, 2), :], R[1][:, 1, 0:128],
                                    a["xT"][0][:, it.m(0, 2), :].bitcast(F32), ALU.subtract).then_inc(S("ac_xl"), 1)
                if b4 is not None:
                    e.wait_ge(S("ac_add"), count(b4))
                    apart(e)
                    e.bn_stats(st[:, 0, :], rows(X, b4)).then_inc(S("ac_bn"), 1)
                b = it.b(1)
                if b is not None:
                    e.wait_ge(S("a_kT"), count(b))
                    e.tensor_scalar(a["kT"][:, it.m(1, 2), :, :].rearrange("p a b -> p (a b)"), R[2][:, 0, 0:4 * SK],
                                    a["wqk"][:, 0:1], None, ALU.mult).then_inc(S("a_kTe"), 1)
                if b4 is not None:
                    stats_tail(e, b4, S("ac_bn"), S("ac_ag"), S("ac_ve"))
            pipeline(e, NB, 4, 4, body)

        def stats_tail(e, b, bn, ag, vs, k=1, j=0, base=0):
            e.wait_ge(bn, count(b, j + 1, k, base))
            apart(e)
            e.bn_aggr(agg[:, 0, :], st[:, 0, :]).then_inc(ag, 1)
            e.wait_ge(ag, count(b, j + 1, k, base))
            e.tensor_tensor(rows(mv, b), agg[:, 0:1, :], eps[:, 0:1, :], ALU.add).then_inc(vs, 1)

        def root(e, b):
            apart(e)
            return e.tensor_tensor(rs[:, bass.ds(b, 1)], mv[:, bass.ds(b, 1), 1:2].rearrange("p a b -> p (a b)"),
                                   nhalf[:, 0:1], ALU.pow)

        def a_pool(e):
            e.wait_ge(S("ctx_in"), 16)

            def body(it):
                b = it.b(0)
                if b is not None:
                    split_context(e, a, it, b)
                b = it.b(1)
                if b is not None:
                    p = it.m(1, 2)
                    e.wait_ge(S("a_kr"), count(b))
                    if past(it.i - 2):
                        e.wait_ge(S("a_redk"), count(it.i - 2))
                    e.tensor_tensor(a["sqk"][0:SK, :], a["kr"][0:SK, p, :], a["kr"][0:SK, p, :], ALU.mult)\
                        .then_inc(S("a_sqk"), 1)
                    e.wait_ge(S("a_vv"), count(b))
                    if past(it.i - 3):
                        e.wait_ge(S("a_qn"), count(it.i - 3))
                    e.tensor_tensor(a["r"][:, p, :], a["vv"][:, p, :], nhalf[:, 0:20], ALU.pow).then_inc(S("a_r"), 1)
                    e.wait_ge(S("a_r"), count(b))
                    if past(it.i - 3):
                        e.wait_ge(S("a_kT"), count(it.i - 3))
                    e.tensor_tensor(a["kn"][0:SK, p, :, :, :],
                                    a["kr"][0:SK, p, :].rearrange("p (h d) -> p h d", d=DH0).unsqueeze(2)
                                    .to_broadcast([SK, 4, 2, DH0]),
                                    a["r"][0:SK, p, 16:20].unsqueeze(2).unsqueeze(3).to_broadcast([SK, 4, 2, DH0]),
                                    ALU.mult).then_inc(S("a_kn"), 1)
                b = it.b(4)
                if b is not None:
                    e.wait_ge(S("ac_ve"), count(b))
                    root(e, b).then_inc(S("ac_rs"), 1)
            pipeline(e, NB, 4, 4, body)

        def split_context(e, t, it, b):
            m = it.m(0, 4)
            if past(it.i - 4):
                e.wait_ge(S("a_kv"), count(it.i - 4))
            e.tensor_copy(t["c"][0][:, m:m + 1, :], rows(ctx_sb, b)).then_inc(S("ac_ch"), 1)
            e.wait_ge(S("ac_ch"), count(b))
            apart(e)
            e.tensor_tensor(t["c"][1][:, m:m + 1, :], rows(ctx_sb, b), t["c"][0][:, m:m + 1, :].bitcast(F32),
                            ALU.subtract).then_inc(S("ac_cl"), 1)

        def b_tensor(e):
            e.wait_ge(S("ac_add"), count(NB - 1))
            e.wait_ge(S("ac_xl"), count(NB - 1))
            e.wait_ge(S("a_kTe"), count(NB - 1))
            e.wait_ge(S("a_onb"), count(NB - 1))
            t = g_

            def body(it):
                for c in range(NCH):
                    b = it.b(1)
                    if b is not None:
                        q = it.m(1, 2)
                        if c % 2 == 0:
                            if past(b - 1 if c == 0 else b):
                                e.wait_ge(S("b_wb"), count(b - 1 if c == 0 else b, NE if c == 0 else c // 2, NE))
                            e.wait_ge(S("b_wt"), count(b))
                            for j in range(GB):
                                mm = e.transpose(bank(1)[:, 128 * j:128 * j + 128],
                                                 t["wt"][:, q, j, c // 2:c // 2 + 1].to_broadcast([128, 128]), ident[:])
                            mm.then_inc(S("b_wbp"), 1)
                        xs = [x[:, q, :] for x in t["xT"]]
                        if c == 0:
                            e.wait_ge(S("b_xl"), count(b))
                        if c < 2:
                            if past(b - 1):
                                e.wait_ge(S("b_sil"), count(b - 1, NCH - 1 + c, NCH))
                            if past(b - 1):
                                e.wait_ge(S("b_g"), count(b - 1, NCH - 1 + c, NCH))
                        else:
                            e.wait_ge(S("b_sil"), count(b, c - 1, NCH))
                        passes(e, bank(3 + 2 * (c % 2)), [w[:, 128 * c:128 * c + 128] for w in w1e], xs)\
                            .then_inc(S("b_h1"), 1)
                        if c >= 2:
                            e.wait_ge(S("b_g"), count(b, c - 1, NCH))
                        passes(e, bank(4 + 2 * (c % 2)), [w[:, 128 * c:128 * c + 128] for w in w3e], xs)\
                            .then_inc(S("b_h3"), 1)
                    b, cy = (it.b(1), c - 3) if c >= 3 else (it.b(2), c - 3 + NCH)
                    if b is not None:
                        lag = 1 if c >= 3 else 2
                        if cy == 0:
                            if past(b - 2):
                                e.wait_ge(S("b_yT"), count(b - 2))
                        e.wait_ge(S("b_gl"), count(b, cy + 1, NCH))
                        y = bank((2, 7)[it.m(lag, 2)])
                        for n, (w, x) in enumerate(((1, 0), (0, 1), (0, 0))):
                            mm = e.matmul(y, w2e[w][:, cy, :], t["gs"][x][:, cy % 4, :],
                                          start=(cy == 0 and n == 0), stop=(cy == NCH - 1 and n == 2))
                        if cy == NCH - 1:
                            mm.then_inc(S("b_y"), 1)
                    b = it.b(0)
                    if b is not None and c == 4:
                        if past(min(it.i - 3, NG - 1) if it.static else it.i - 3):
                            e.wait_ge(S("b_add"), count(min(it.i - 3, NG - 1) if it.static else it.i - 3))
                        if past(b - 1):
                            e.wait_ge(S("b_lm"), count(b - 1))
                        e.wait_ge(S("b_xn"), count(b))
                        for j in range(GB):
                            mm = e.transpose(bank(0)[:, 128 * j:128 * j + 128], t["xn"][:, j, :], ident[:])
                        mm.then_inc(S("b_xTp"), 1)
                    if b is not None and c == 8:
                        e.wait_ge(S("b_xl"), count(b))
                        for j in range(GB):
                            mm = passes(e, bank(0)[:, NE * j:NE * j + NE],
                                        [x[:, it.m(0, 2), 128 * j:128 * j + 128] for x in t["xT"]], [w[:] for w in wgs])
                        mm.then_inc(S("b_lg"), 1)
                    b = it.b(2)
                    if b is not None and c == 12:
                        if it.b(0) is not None:
                            e.wait_ge(S("b_lm"), it.i + 1)
                        elif it.static:
                            if past(b - 1):
                                e.wait_ge(S("b_add"), count(b - 1))
                            e.wait_ge(S("b_lm"), count(NG - 1))
                        e.wait_ge(S("b_yT"), count(b))
                        for j in range(GB):
                            mm = e.transpose(bank(0)[:, 128 * j:128 * j + 128], t["yT"][:, 128 * j:128 * j + 128], ident[:])
                        mm.then_inc(S("b_yt"), 1)
            pipeline(e, NG, 4, 2, body)

        def b_scalar(e):
            t = g_
            e.wait_ge(S("ac_add"), count(NB - 1))

            def body(it):
                for c in range(NCH + 0):
                    b = it.b(1)
                    if b is not None:
                        if c % 2 == 0:
                            k = c // 2
                            e.wait_ge(S("b_wbp"), count(b, k + 1, NE))
                            if k >= 2:
                                e.wait_ge(S("b_sp"), count(b, 2 * k - 2, NCH))
                            else:
                                if past(b - 1):
                                    e.wait_ge(S("b_sp"), count(b - 1, NCH + 2 * k - 2, NCH))
                            e.activation(t["wb"][:, k % 2, :], bank(1), ACT.Copy).then_inc(S("b_wb"), 1)
                        e.wait_ge(S("b_h1"), count(b, c + 1, NCH))
                        if c >= 2:
                            e.wait_ge(S("b_sp"), count(b, c - 1, NCH))
                        else:
                            if past(b - 1):
                                e.wait_ge(S("b_sp"), count(b - 1, NCH + c - 1, NCH))
                        e.activation(t["s"][:, c % 2, :], bank(3 + 2 * (c % 2)), ACT.Silu).then_inc(S("b_sil"), 1)
                    b, cg = (it.b(1), c - 2) if c >= 2 else (it.b(2), c - 2 + NCH)
                    if b is not None:
                        e.wait_ge(S("b_g"), count(b, cg + 1, NCH))
                        e.activation(t["gs"][0][:, cg % 4, :], t["g"][:, cg % 4, :], ACT.Copy).then_inc(S("b_gh"), 1)
                    b = it.b(2)
                    if b is not None and c == 4:
                        e.wait_ge(S("b_y"), count(b))
                        if past(b - 1):
                            e.wait_ge(S("b_yt"), count(b - 1))
                        e.activation(t["yT"][:], bank((2, 7)[it.m(2, 2)]), ACT.Copy).then_inc(S("b_yT"), 1)
                    b = it.b(0)
                    if b is not None and c == 5:
                        e.wait_ge(S("b_xTp"), count(b))
                        e.activation(t["xT"][0][:, it.m(0, 2), :], bank(0), ACT.Copy).then_inc(S("b_xh"), 1)
                    if b is not None and c == 10:
                        e.wait_ge(S("b_lm"), count(b))
                        e.activation(t["Re"][:], t["Rl"][:], ACT.Exp).then_inc(S("b_ex"), 1)
            pipeline(e, NG, 4, 2, body)

        def b_vector(e):
            t = g_
            e.wait_ge(S("ac_rs"), count(NB - 1))

            bc = lambda x: t[x][:].unsqueeze(2).to_broadcast([128, GB, NE])
            lg = bank(0)[:, 0:GB * NE].rearrange("p (a b) -> p a b", b=NE)
            NR = 21
            router_from = {9: 0, 10: 2, 11: 2, 12: 6, 13: 10, 14: 14, 15: 18, 16: NR}

            def router(it, b, n):
                if n == 0:
                    e.wait_ge(S("b_lg"), count(b))
                    e.tensor_reduce(t["rm"][:], lg, AX.X, ALU.max, negate=True).then_inc(S("b_m0"), 1)
                if n == 1:
                    e.wait_ge(S("b_m0"), count(b))
                    e.tensor_tensor(t["Rl"][:], lg, bc("rm"), ALU.add).then_inc(S("b_lm"), 1)
                if n == 2:
                    e.wait_ge(S("b_ex"), count(b))
                    e.tensor_reduce(t["rs"][:], t["Re"][:], AX.X, ALU.add).then_inc(S("b_ro"), 1)
                if n == 3:
                    e.wait_ge(S("b_ro"), count(b, 1, NR - 3))
                    e.reciprocal(t["rrc"][:], t["rs"][:]).then_inc(S("b_ro"), 1)
                if n == 4:
                    e.wait_ge(S("b_ro"), count(b, 2, NR - 3))
                    e.tensor_tensor(t["Rp"][:], t["Re"][:], bc("rrc"), ALU.mult).then_inc(S("b_ro"), 1)
                if n == 5:
                    e.wait_ge(S("b_ro"), count(b, 3, NR - 3))
                    e.tensor_reduce(t["rm1"][:], t["Rp"][:], AX.X, ALU.max).then_inc(S("b_ro"), 1)
                if n == 6:
                    e.wait_ge(S("b_ro"), count(b, 4, NR - 3))
                    e.tensor_tensor(t["Rq"][:], t["Rp"][:], bc("rm1"), ALU.is_equal).then_inc(S("b_ro"), 1)
                if n == 7:
                    e.wait_ge(S("b_ro"), count(b, 5, NR - 3))
                    e.tensor_tensor(t["Rk"][:], t["Rq"][:], keyi[:], ALU.mult).then_inc(S("b_ro"), 1)
                if n == 8:
                    e.wait_ge(S("b_ro"), count(b, 6, NR - 3))
                    e.tensor_reduce(t["rk1"][:], t["Rk"][:], AX.X, ALU.max).then_inc(S("b_ro"), 1)
                if n == 9:
                    e.wait_ge(S("b_ro"), count(b, 7, NR - 3))
                    e.tensor_tensor(t["Ro"][:], t["Rk"][:], bc("rk1"), ALU.is_equal).then_inc(S("b_ro"), 1)
                if n == 10:
                    e.wait_ge(S("b_ro"), count(b, 8, NR - 3))
                    e.scalar_tensor_tensor(out=t["Rq2"][:], in0=t["Ro"][:], scalar=-2.0, in1=t["Rp"][:],
                                       op0=ALU.mult, op1=ALU.add).then_inc(S("b_ro"), 1)
                if n == 11:
                    e.wait_ge(S("b_ro"), count(b, 9, NR - 3))
                    e.tensor_reduce(t["rm2"][:], t["Rq2"][:], AX.X, ALU.max).then_inc(S("b_ro"), 1)
                if n == 12:
                    e.wait_ge(S("b_ro"), count(b, 10, NR - 3))
                    e.tensor_tensor(t["Re2"][:], t["Rq2"][:], bc("rm2"), ALU.is_equal).then_inc(S("b_ro"), 1)
                if n == 13:
                    e.wait_ge(S("b_ro"), count(b, 11, NR - 3))
                    e.tensor_tensor(t["Rk2"][:], t["Re2"][:], keyi[:], ALU.mult).then_inc(S("b_ro"), 1)
                if n == 14:
                    e.wait_ge(S("b_ro"), count(b, 12, NR - 3))
                    e.tensor_reduce(t["rk2"][:], t["Rk2"][:], AX.X, ALU.max).then_inc(S("b_ro"), 1)
                if n == 15:
                    e.wait_ge(S("b_ro"), count(b, 13, NR - 3))
                    e.tensor_tensor(t["Ro2"][:], t["Rk2"][:], bc("rk2"), ALU.is_equal).then_inc(S("b_ro"), 1)
                if n == 16:
                    e.wait_ge(S("b_ro"), count(b, 14, NR - 3))
                    e.tensor_tensor(t["Rt"][:], t["Ro"][:], t["Ro2"][:], ALU.add).then_inc(S("b_ro"), 1)
                if n == 17:
                    e.wait_ge(S("b_ro"), count(b, 15, NR - 3))
                    e.tensor_tensor(t["Rk"][:], t["Rt"][:], t["Rp"][:], ALU.mult).then_inc(S("b_ro"), 1)
                if n == 18:
                    e.wait_ge(S("b_ro"), count(b, 16, NR - 3))
                    e.tensor_tensor(t["rdn"][:], t["rm1"][:], t["rm2"][:], ALU.add).then_inc(S("b_ro"), 1)
                if n == 19:
                    e.wait_ge(S("b_ro"), count(b, 17, NR - 3))
                    e.reciprocal(t["rrd"][:], t["rdn"][:]).then_inc(S("b_ro"), 1)
                if n == 20:
                    e.wait_ge(S("b_ro"), count(b, 18, NR - 3))
                    e.tensor_tensor(t["wt"][:, it.m(0, 2), :, :], t["Rk"][:], bc("rrd"), ALU.mult).then_inc(S("b_wt"), 1)

            def body(it):
                for c in range(NCH):
                    b = it.b(0)
                    if b is not None and c < GB:
                        e.tensor_scalar(t["xn"][:, c:c + 1, :], rows(X, b * GB + c),
                                        mv[:, bass.ds(b * GB + c, 1), 0:1].rearrange("p a b -> p (a b)"),
                                        rs[:, bass.ds(b * GB + c, 1)], ALU.subtract, ALU.mult)\
                            .then_inc(S("b_xn") if c == GB - 1 else S("b_xnc"), 1)
                    if b is not None and c == 5:
                        e.wait_ge(S("b_xh"), count(b))
                        e.tensor_tensor(t["xT"][1][:, it.m(0, 2), :], bank(0), t["xT"][0][:, it.m(0, 2), :].bitcast(F32),
                                        ALU.subtract).then_inc(S("b_xl"), 1)
                    b, cg = (it.b(1), c - 1) if c >= 1 else (it.b(2), NCH - 1)
                    if b is not None:
                        e.wait_ge(S("b_h3"), count(b, cg + 1, NCH))
                        e.wait_ge(S("b_sp"), count(b, cg + 1, NCH))
                        if cg >= 4:
                            e.wait_ge(S("b_gl"), count(b, cg - 3, NCH))
                        else:
                            if past(b - 1):
                                e.wait_ge(S("b_gl"), count(b - 1, NCH + cg - 3, NCH))
                        e.tensor_tensor(t["g"][:, cg % 4, :], bank(4 + 2 * (cg % 2)), t["sp"][:, cg % 2, :], ALU.mult)\
                            .then_inc(S("b_g"), 1)
                    b, cg = (it.b(1), c - 2) if c >= 2 else (it.b(2), c - 2 + NCH)
                    if b is not None:
                        e.wait_ge(S("b_gh"), count(b, cg + 1, NCH))
                        e.tensor_tensor(t["gs"][1][:, cg % 4, :], t["g"][:, cg % 4, :],
                                        t["gs"][0][:, cg % 4, :].bitcast(F32), ALU.subtract).then_inc(S("b_gl"), 1)
                    b = it.b(0)
                    if b is not None and c >= 9:
                        for n in range(router_from[c], router_from[c + 1]):
                            router(it, b, n)
                    b = it.b(2)
                    if b is not None and c == 13:
                        e.wait_ge(S("b_yt"), count(b))
                        e.tensor_tensor(X[:, bass.ds(b * GB, GB), :], X[:, bass.ds(b * GB, GB), :],
                                        bank(0).rearrange("p (a b) -> p a b", b=128), ALU.add).then_inc(S("b_add"), 1)
                    if b is not None and c == 14:
                        e.wait_ge(S("b_add"), count(b))
                        apart(e)
                        for j in range(GB):
                            e.bn_stats(st[:, j, :], rows(X, b * GB + j)).then_inc(S("b_bn"), 1)
                    if b is not None and c == 15:
                        e.wait_ge(S("b_bn"), count(b, GB, GB))
                        apart(e)
                        for j in range(GB):
                            e.bn_aggr(agg[:, j, :], st[:, j, :]).then_inc(S("b_ag"), 1)
                        e.wait_ge(S("b_ag"), count(b, GB, GB))
                        e.tensor_tensor(mv[:, bass.ds(b * GB, GB), :], agg[:], eps[:], ALU.add).then_inc(S("b_ve"), 1)
            pipeline(e, NG, 4, 2, body)

        def b_pool(e):
            t = g_
            e.wait_ge(S("ac_add"), count(NB - 1))

            def body(it):
                b = it.b(1)
                if b is not None:
                    for c in range(NCH):
                        e.wait_ge(S("b_sil"), count(b, c + 1, NCH))
                        if c % 2 == 0:
                            e.wait_ge(S("b_wb"), count(b, c // 2 + 1, NE))
                        if c >= 2:
                            e.wait_ge(S("b_g"), count(b, c - 1, NCH))
                        else:
                            if past(b - 1):
                                e.wait_ge(S("b_g"), count(b - 1, NCH + c - 1, NCH))
                        e.tensor_tensor(t["sp"][:, c % 2, :], t["s"][:, c % 2, :], t["wb"][:, c // 2 % 2, :], ALU.mult)\
                            .then_inc(S("b_sp"), 1)
                b = it.b(2)
                if b is not None:
                    e.wait_ge(S("b_ve"), count(b))
                    apart(e)
                    e.tensor_tensor(rs[:, bass.ds(b * GB, GB)], mv[:, bass.ds(b * GB, GB), 1:2].rearrange("p a b -> p (a b)"),
                                    nhalf[:, 0:GB], ALU.pow)\
                        .then_inc(S("b_rs"), 1)
            pipeline(e, NG, 4, 2, body)


        def c_tensor(e):
            t = c_
            e.wait_ge(S("b_add"), count(NG - 1))
            e.wait_ge(S("c_v1s"), count(2))

            def body(it):
                b = it.b(1)
                if b is not None:
                    if it.seen(2):
                        e.wait_ge(S("c_v"), it.upto(2))
                    if it.seen(2):
                        e.wait_ge(S("c_kb"), it.upto(2))
                    e.wait_ge(S("ac_xl"), count(b, base=NB))
                    e.wait_ge(S("ac_cl"), count(b, base=NB))
                    x = [x[:, it.m(1, 2), :] for x in t["xT"]]
                    c = [c[:, it.m(1, 4), :] for c in t["c"]]
                    passes(e, R[0][:, 0, 0:128], [w[:, 0, :] for w in l1s], x)
                    passes(e, R[0][:, 0, 128:128 + SK + 1], [w[:, 1, :] for w in l1s], c).then_inc(S("c_qk"), 1)
                    passes(e, R[0][0:SK, 1, 0:128], [z[:, 0:SK] for z in c], [w[:, 2, :] for w in l1s]).then_inc(S("c_vp"), 1)
                b = it.b(3)
                if b is not None:
                    for half, slot in ((0, 3), (1, 1)):
                        if half == 0:
                            if it.seen(3):
                                e.wait_ge(S("ac_suba"), it.upto(3, NB))
                        else:
                            if it.seen(5):
                                e.wait_ge(S("ac_add"), it.upto(5, NB))
                            if it.seen(1):
                                e.wait_ge(S("ac_xl"), it.upto(1, NB))
                        e.wait_ge(S(("ac_expa", "ac_expb")[half]), count(b, base=NB))
                        for k in range(8):
                            mm = e.transpose(R[slot][0:SK, k // 4, 128 * (k % 4):128 * (k % 4) + 128],
                                             t["p"][:, it.m(3, 2), 8 * half + k, :], ident[:])
                        mm.then_inc(S(("ac_PTa", "ac_PTb")[half]), 1)
                b = it.b(4)
                if b is not None:
                    if it.seen(4):
                        e.wait_ge(S("c_on"), it.upto(4))
                    e.wait_ge(S("c_on"), count(b))
                    e.transpose(R[2][:, 0, 0:128], t["on"][:, it.m(4, 2), :], ident[:]).then_inc(S("ac_OT"), 1)
                b = it.b(2)
                if b is not None:
                    e.wait_ge(S("c_qT"), count(b))
                    e.wait_ge(S("c_kb"), count(b))
                    for half, slot in ((0, 3), (1, 1)):
                        if half == 0:
                            if it.seen(3):
                                e.wait_ge(S("ac_pTa"), it.upto(3, NB))
                        else:
                            if it.seen(3):
                                e.wait_ge(S("ac_pTb"), it.upto(3, NB))
                            if it.static:
                                if it.seen(5):
                                    e.wait_ge(S("ac_add"), it.upto(5, NB))
                                if it.seen(1):
                                    e.wait_ge(S("ac_xl"), it.upto(1, NB))
                        for k in range(2):
                            o = 32 * (2 * half + k)
                            mm = e.matmul(R[slot][:, k, 0:4 * SK], t["qT"][o:o + 32, it.m(2, 2), :],
                                          t["kb"][o:o + 32, it.m(2, 2), :, :].rearrange("p a b -> p (a b)"),
                                          start=True, stop=True)
                        mm.then_inc(S(("ac_Sa", "ac_Sb")[half]), 1)
                b = it.b(3)
                if b is not None:
                    if it.seen(4):
                        e.wait_ge(S("ac_oTe"), it.upto(4, NB))
                    e.wait_ge(S("ac_pTb"), count(b, base=NB))
                    for h in range(H1):
                        mm = e.matmul(R[2][:, 0, 9 * h:9 * h + 9], t["pT"][0:SK, h, :],
                                      t["v1"][0:SK, it.m(3, 4), h, :], start=True, stop=True)
                    mm.then_inc(S("c_PV"), 1)
                if it.b(4) is not None or it.b(0) is not None:
                    if it.seen(2):
                        e.wait_ge(S("ac_subb"), it.upto(2, NB))
                    if it.static:
                        if it.seen(3):
                            e.wait_ge(S("ac_pTb"), it.upto(3, NB))
                        if it.seen(5):
                            e.wait_ge(S("ac_add"), it.upto(5, NB))
                        if it.seen(1):
                            e.wait_ge(S("ac_xl"), it.upto(1, NB))
                b = it.b(4)
                if b is not None:
                    e.wait_ge(S("ac_oTe"), count(b, base=NB))
                    e.matmul(R[1][:, 0, 0:128], t["oT"][:], l1[:, 3, :], start=True, stop=True).then_inc(S("ac_wo"), 1)
                b = it.b(0)
                if b is not None:
                    e.wait_ge(S("ac_xn"), count(b, base=NB))
                    e.transpose(R[1][:, 1, 0:128], t["xn"][:, it.m(0, 2), :], ident[:]).then_inc(S("ac_xTp"), 1)
            pipeline(e, NB, 4, 4, body)

        def c_scalar(e):
            t = c_
            e.wait_ge(S("b_add"), count(NG - 1))

            def body(it):
                b = it.b(1)
                if b is not None:
                    e.wait_ge(S("c_qk"), count(b))
                    e.activation(t["qT"][:, it.m(1, 2), :], R[0][:, 0, 0:128], ACT.Copy, scale=float(DH1) ** -0.5)\
                        .then_inc(S("c_qT"), 1)
                    e.wait_ge(S("c_vp"), count(b))
                    e.activation(t["v1"][0:SK, it.m(1, 4), :, 0:DH1],
                                 R[0][0:SK, 1, 0:128].rearrange("p (a b) -> p a b", b=DH1), ACT.Copy).then_inc(S("c_v"), 1)
                b = it.b(3)
                if b is not None:
                    for half, slot in ((0, 3), (1, 1)):
                        e.wait_ge(S(("ac_PTa", "ac_PTb")[half]), count(b, base=NB))
                        e.activation(t["pT"][0:SK, 8 * half:8 * half + 8, :].rearrange("p (a c) t -> p a (c t)", a=2),
                                     R[slot][0:SK, :, :], ACT.Copy).then_inc(S(("ac_pTa", "ac_pTb")[half]), 1)
                b = it.b(4)
                if b is not None:
                    e.wait_ge(S("ac_OT"), count(b, base=NB))
                    e.activation(t["oT"][:], R[2][:, 0, 0:128], ACT.Copy).then_inc(S("ac_oTe"), 1)
                b = it.b(2)
                if b is not None:
                    for half in range(2):
                        e.wait_ge(S(("ac_suba", "ac_subb")[half]), count(b, base=NB))
                        p = t["p"][:, it.m(2, 2), 8 * half:8 * half + 8, :]
                        e.activation(p, p, ACT.Exp).then_inc(S(("ac_expa", "ac_expb")[half]), 1)
                b = it.b(0)
                if b is not None:
                    e.wait_ge(S("ac_xTp"), count(b, base=NB))
                    e.activation(t["xT"][0][:, it.m(0, 2), :], R[1][:, 1, 0:128], ACT.Copy).then_inc(S("ac_xh"), 1)
            pipeline(e, NB, 4, 4, body)

        def c_vector(e):
            t = c_
            e.wait_ge(S("b_rs"), count(NG - 1))
            e.memset(t["v1"][:], 1.0).then_inc(S("c_v1s"), 1)
            for x in t["c"]:
                e.memset(x[:, :, SK:SK + 1].bitcast(F32), 0.0).then_inc(S("c_v1s"), 1)

            def masked(b, half, slot):
                s = R[slot][:, :, 0:4 * SK].rearrange("p a (j k) -> p a j k", k=SK)
                e.wait_ge(S(("ac_Sa", "ac_Sb")[half]), count(b, base=NB))
                apart(e)
                for k in range(2):
                    i = e.copy_predicated(s[:, k, :, :], maskz[:].unsqueeze(1).to_broadcast([128, 4, SK]),
                                          negt[:].unsqueeze(1).to_broadcast([128, 4, SK]))
                i.then_inc(S(("c_ma", "c_mb")[half]), 1)

            def body(it):
                b = it.b(0)
                if b is not None:
                    layernorm(e, X, t["xn"], b, it.m(0, 2)).then_inc(S("ac_xn"), 1)
                b = it.b(1)
                if b is not None:
                    e.wait_ge(S("c_qT"), count(b))
                    e.tensor_tensor(t["kb"][:, it.m(1, 2), :, :],
                                    R[0][:, 0, 128:128 + SK].unsqueeze(1).to_broadcast([128, 4, SK]),
                                    head[:].unsqueeze(2).to_broadcast([128, 4, SK]), ALU.mult).then_inc(S("c_kb"), 1)
                b = it.b(2)
                if b is not None:
                    masked(b, 0, 3)
                    softmax_less_max(e, it, b, 0, 3, "c", t, ("c_ma", "ac_nma", "ac_suba"), 8, SK, NB, 0)
                    masked(b, 1, 1)
                    softmax_less_max(e, it, b, 1, 1, "c", t, ("c_mb", "ac_nmb", "ac_subb"), 8, SK, NB, 0)
                b = it.b(3)
                if b is not None:
                    o = R[2][:, 0, 0:9 * H1].rearrange("p (h k) -> p h k", k=9)
                    e.wait_ge(S("c_PV"), count(b))
                    e.reciprocal(t["rc"][:], o[:, :, DH1]).then_inc(S("c_rc"), 1)
                    e.wait_ge(S("c_rc"), count(b))
                    e.tensor_tensor(t["on"][:, it.m(3, 2), :].rearrange("p (h k) -> p h k", k=DH1), o[:, :, 0:DH1],
                                    t["rc"][:].unsqueeze(2).to_broadcast([128, H1, DH1]), ALU.mult).then_inc(S("c_on"), 1)
                b4 = it.b(4)
                if b4 is not None:
                    e.wait_ge(S("ac_wo"), count(b4, base=NB))
                    e.tensor_tensor(rows(X, b4), rows(X, b4), R[1][:, 0:1, 0:128], ALU.add).then_inc(S("ac_add"), 1)
                b = it.b(0)
                if b is not None:
                    e.wait_ge(S("ac_xh"), count(b, base=NB))
                    e.tensor_tensor(t["xT"][1][:, it.m(0, 2), :], R[1][:, 1, 0:128],
                                    t["xT"][0][:, it.m(0, 2), :].bitcast(F32), ALU.subtract).then_inc(S("ac_xl"), 1)
                if b4 is not None:
                    e.wait_ge(S("ac_add"), count(b4, base=NB))
                    apart(e)
                    e.bn_stats(st[:, 0, :], rows(X, b4)).then_inc(S("ac_bn"), 1)
                    stats_tail(e, b4, S("ac_bn"), S("ac_ag"), S("ac_ve"), base=NB)
            pipeline(e, NB, 4, 4, body)

        def c_pool(e):
            e.wait_ge(S("b_add"), count(NG - 1))

            def body(it):
                b = it.b(0)
                if b is not None:
                    m = it.m(0, 4)
                    if past(it.i - 4):
                        e.wait_ge(S("c_vp"), count(it.i - 4))
                    e.tensor_copy(c_["c"][0][:, m:m + 1, 0:SK], rows(ctx_sb, b)).then_inc(S("ac_ch"), 1)
                    e.wait_ge(S("ac_ch"), count(b, base=NB))
                    apart(e)
                    e.tensor_tensor(c_["c"][1][:, m:m + 1, 0:SK], rows(ctx_sb, b), c_["c"][0][:, m:m + 1, 0:SK].bitcast(F32),
                                    ALU.subtract).then_inc(S("ac_cl"), 1)
                b = it.b(4)
                if b is not None:
                    e.wait_ge(S("ac_ve"), count(b, base=NB))
                    root(e, b).then_inc(S("ac_rs"), 1)
            pipeline(e, NB, 4, 4, body)

        def load_d(e):
            e.wait_ge(S("b_add"), count(NG - 1))
            e.dma_start(stage[:, 0, 0:1536], wqkv_in[:, 0:1536]).then_inc(S("stage0_in"), 16)
            e.dma_start(stage[:, 1, 0:1536], wqkv_in[:, 1536:3072]).then_inc(S("stage1_in"), 16)
            e.wait_ge(S("split"), 8)
            e.dma_start(stage[:, 0, 0:4 * HID], w1l_in).then_inc(S("stage0_in"), 16)

        def d_weights():
            for n in range(DEPTH):
                yield n, stage[:, n, 0:1536], wqkv[n], (64, 48)[n]
            for n in range(DEPTH):
                yield 0, stage[:, 0, 2 * HID * n:2 * HID * n + 2 * HID], w1l[n], 80

        def split_act_d(e):
            e.wait_ge(S("ac_add"), count(NB - 1, base=NB))
            for half, src, dst, n in d_weights():
                e.wait_ge(S(f"stage{half}_in"), n)
                e.activation(dst[0][:], src, ACT.Copy).then_inc(S("high"), 1)

        def split_dve_d(e):
            for n, (half, src, dst, _) in enumerate(d_weights()):
                e.wait_ge(S("high"), 12 + n + 1)
                e.tensor_tensor(dst[1][:], src, dst[0][:].bitcast(F32), ALU.subtract).then_inc(S("split"), 1)
            for l in range(DEPTH):
                e.tensor_tensor(T1[:, l, :, :], rot[:, 0, :, :], qks[:, l, 0, :, :], ALU.mult).then_inc(S("d_con"), 1)
                e.tensor_tensor(T2[:, l, :, :], rot[:, 1, :, :], qks[:, l, 1, :, :], ALU.mult).then_inc(S("d_con"), 1)
            e.memset(H2[0:1, :, 64:128], 0.0).then_inc(S("d_con"), 1)
            e.memset(d["v1"][:], 1.0).then_inc(S("d_con"), 1)
            for x in d["hT"]:
                e.memset(x[64:128, :, 0:1].bitcast(F32), 0.0).then_inc(S("d_con"), 1)
            e.wait_ge(S("d_con"), 8)


        def da_start(e, l):
            if l == 0:
                e.wait_ge(S("ac_add"), count(NB - 1, base=NB))
                e.wait_ge(S("ac_rs"), count(NB - 1, base=NB))
            else:
                e.wait_ge(S("f_add"), count(NG - 1))
                e.wait_ge(S("f_lo"), count(NG - 1))

        def da_tensor(e, l):
            t, B = d, NB * l
            da_start(e, l)
            e.wait_ge(S("split"), 11)
            e.wait_ge(S("d_con"), 8)

            def body(it):
                b = it.b(1)
                if b is not None:
                    x = [x[:, it.m(1, 2), :] for x in t["hT"]]
                    if past(b - 1):
                        e.wait_ge(S("d_B"), count(b - 1, base=B))
                    e.wait_ge(S("d_hl"), count(b, base=B))
                    for h in range(2):
                        mm = passes(e, R[0][:, h, :], x, [w[:, 512 * h:512 * h + 512] for w in wqkv[l]])
                    mm.then_inc(S("d_qkp"), 1)
                    if it.seen(5):
                        e.wait_ge(S("d_add"), it.upto(5, B))
                    if it.seen(1):
                        e.wait_ge(S("d_hl"), it.upto(1, B))
                    passes(e, R[1][:, 0, :], x, [w[:, 1024:1536] for w in wqkv[l]]).then_inc(S("d_vp"), 1)
                b = it.b(2)
                if b is not None:
                    if it.seen(3):
                        e.wait_ge(S("d_sub"), it.upto(3, B))
                    e.wait_ge(S("d_qkn"), count(b, base=B))
                    for c in range(8):
                        mm = e.transpose(R[2][:, c // 4, 128 * (c % 4):128 * (c % 4) + 128],
                                         t["A"][:, it.m(2, 2), 128 * c:128 * c + 128], ident[:])
                    mm.then_inc(S("d_qkTp"), 1)
                b = it.b(3)
                if b is not None:
                    if it.seen(4):
                        e.wait_ge(S("d_on"), it.upto(4, B))
                    e.wait_ge(S("d_exp"), count(b, base=B))
                    for c in range(8):
                        mm = e.transpose(R[3][:, c // 4, 128 * (c % 4):128 * (c % 4) + 128], t["p"][:, it.m(3, 2), c, :], ident[:])
                    mm.then_inc(S("d_PT"), 1)
                b = it.b(4)
                if b is not None:
                    if it.seen(1):
                        e.wait_ge(S("d_v"), it.upto(1, B))
                    if it.static:
                        if it.seen(5):
                            e.wait_ge(S("d_add"), it.upto(5, B))
                        if it.seen(1):
                            e.wait_ge(S("d_hl"), it.upto(1, B))
                    e.wait_ge(S("d_on"), count(b, base=B))
                    for c in range(4):
                        mm = e.transpose(R[1][:, 0, 128 * c:128 * c + 128], t["on"][:, it.m(4, 2), 128 * c:128 * c + 128], ident[:])
                    mm.then_inc(S("d_OT"), 1)
                b = it.b(2)
                if b is not None:
                    if it.seen(2):
                        e.wait_ge(S("d_qkT"), it.upto(2, B))
                    e.wait_ge(S("d_qkT"), count(b, base=B))
                    for k in range(2):
                        e.matmul(R[2][:, k, :], identb[:], bandb[:].rearrange("p a b -> p (a b)"), start=True, stop=False)
                    for h in range(HL):
                        o = DL * (h % 2)
                        mm = e.matmul(R[2][:, h % 2, 128 * (h // 2):128 * (h // 2) + 128], t["qT"][o:o + DL, h // 2, :],
                                      t["qT"][o:o + DL, 4 + h // 2, :], start=False, stop=(h >= HL - 2))
                    mm.then_inc(S("d_S"), 1)
                b = it.b(3)
                if b is not None:
                    if it.seen(3):
                        e.wait_ge(S("d_pT"), it.upto(3, B))
                    e.wait_ge(S("d_pT"), count(b, base=B))
                    for h in range(HL):
                        mm = e.matmul(R[3][:, h // 4, 65 * (h % 4):65 * (h % 4) + 65], t["pT"][:, 4 * (h % 2) + h // 2, :],
                                      t["v1"][:, it.m(3, 4), h, :], start=True, stop=True)
                    mm.then_inc(S("d_PV"), 1)
                if it.b(4) is not None or it.b(0) is not None:
                    if it.seen(4):
                        e.wait_ge(S("d_oTe"), it.upto(4, B))
                    if it.static:
                        if it.seen(1):
                            e.wait_ge(S("d_v"), it.upto(1, B))
                b = it.b(4)
                if b is not None:
                    e.wait_ge(S("d_oTe"), count(b, base=B))
                    for c in range(4):
                        mm = e.matmul(R[1][:, 0, 0:128], t["oT"][:, c, :], wol[:, l, c, :], start=(c == 0), stop=(c == 3))
                    mm.then_inc(S("d_wo"), 1)
                b = it.b(0)
                if b is not None:
                    e.wait_ge(S("d_zn"), count(b, base=B))
                    e.matmul(R[1][:, 1, 0:128], t["z"][:, it.m(0, 2), :], ident[:], is_transpose=True, start=True, stop=True)\
                        .then_inc(S("d_zT"), 1)
            pipeline(e, NB, 8, 4, body)

        def da_scalar(e, l):
            t, B = d, NB * l
            da_start(e, l)

            def body(it):
                b = it.b(1)
                if b is not None:
                    e.wait_ge(S("d_qkp"), count(b, base=B))
                    if past(b - 1):
                        e.wait_ge(S("d_red"), count(b - 1, base=B))
                    e.activation(t["sq"][:].rearrange("p (a b) -> p a b", a=2), R[0][:], ACT.Square).then_inc(S("d_sq"), 1)
                    e.wait_ge(S("d_vp"), count(b, base=B))
                    e.activation(t["v1"][:, it.m(1, 4), :, 0:DL], R[1][:, 0, :].rearrange("p (a b) -> p a b", b=DL), ACT.Copy)\
                        .then_inc(S("d_v"), 1)
                b = it.b(2)
                if b is not None:
                    e.wait_ge(S("d_qkTp"), count(b, base=B))
                    e.activation(t["qT"][:].rearrange("p (a c) t -> p a (c t)", a=2), R[2][:], ACT.Copy).then_inc(S("d_qkT"), 1)
                b = it.b(3)
                if b is not None:
                    e.wait_ge(S("d_PT"), count(b, base=B))
                    e.activation(t["pT"][:].rearrange("p (a c) t -> p a (c t)", a=2), R[3][:], ACT.Copy).then_inc(S("d_pT"), 1)
                b = it.b(4)
                if b is not None:
                    e.wait_ge(S("d_OT"), count(b, base=B))
                    e.activation(t["oT"][:].rearrange("p c t -> p (c t)"), R[1][:, 0, :], ACT.Copy).then_inc(S("d_oTe"), 1)
                b = it.b(2)
                if b is not None:
                    e.wait_ge(S("d_sub"), count(b, base=B))
                    p = t["p"][:, it.m(2, 2), :, :]
                    e.activation(p, p, ACT.Exp).then_inc(S("d_exp"), 1)
                b = it.b(0)
                if b is not None:
                    e.wait_ge(S("d_zT"), count(b, base=B))
                    m = it.m(0, 2)
                    e.activation(t["hT"][0][0:64, m, :], R[1][0:64, 1, 0:128], ACT.Copy)
                    e.activation(t["hT"][0][64:128, m, 1:128], R[1][64:128, 1, 0:127], ACT.Copy).then_inc(S("d_hh"), 1)
            pipeline(e, NB, 8, 4, body)

        def da_vector(e, l):
            t, B = d, NB * l
            da_start(e, l)

            def body(it):
                b = it.b(0)
                if b is not None:
                    if l == 0:
                        layernorm(e, X, t["z"], b, it.m(0, 2)).then_inc(S("d_zn"), 1)
                        e.tensor_scalar(rows(Z, b), rows(X, b), mv[:, bass.ds(b, 1), 0:1].rearrange("p a b -> p (a b)"),
                                        rs[:, bass.ds(b, 1)], ALU.subtract, ALU.mult).then_inc(S("d_z"), 1)
                    else:
                        e.tensor_copy(t["z"][:, it.m(0, 2):it.m(0, 2) + 1, :], rows(Z, b)).then_inc(S("d_zn"), 1)
                b = it.b(1)
                if b is not None:
                    p = it.m(1, 2)
                    e.wait_ge(S("d_sq"), count(b, base=B))
                    e.tensor_reduce(t["ss"][:, p, :], t["sq"][:].rearrange("p (h d) -> p h d", d=DL), AX.X, ALU.add)\
                        .then_inc(S("d_red"), 1)
                    if past(it.i - 3):
                        e.wait_ge(S("d_qkn"), count(it.i - 3, base=B))
                    qk = R[0][:].rearrange("p a (h d) -> p a h d", d=DL)
                    A = t["A"][:, p, :].rearrange("p (a h d) -> p a h d", a=2, d=DL)
                    Bt = t["B"][:, p, :].rearrange("p (a h d) -> p a h d", a=2, d=DL)
                    e.tensor_tensor(A, qk, T1[:, l, :, :].unsqueeze(2).to_broadcast([128, 2, HL, DL]), ALU.mult)
                    for h in range(2):
                        i = e.tensor_tensor(Bt[:, :, :, 32 * h:32 * h + 32], qk[:, :, :, 32 - 32 * h:64 - 32 * h],
                                            T2[:, l, :, 32 * h:32 * h + 32].unsqueeze(2).to_broadcast([128, 2, HL, 32]),
                                            ALU.mult)
                    i.then_inc(S("d_B"), 1)
                    e.wait_ge(S("d_red"), count(b, base=B))
                    if past(it.i - 3):
                        e.wait_ge(S("d_r"), count(it.i - 3, base=B))
                    e.tensor_scalar(t["vv"][:, p, :], t["ss"][:, p, :], 1e-24, None, ALU.max).then_inc(S("d_vv"), 1)
                b = it.b(2)
                if b is not None:
                    softmax_less_max(e, it, b, 0, 2, "d", t, ("d_S", "d_nm", "d_sub"), 8, 128, B)
                b = it.b(3)
                if b is not None:
                    o = R[3][:, :, 0:260].rearrange("p a (j k) -> p a j k", k=65)
                    rc = t["rc"][:].rearrange("p (a j) -> p a j", a=2)
                    e.wait_ge(S("d_PV"), count(b, base=B))
                    e.reciprocal(rc, o[:, :, :, 64]).then_inc(S("d_rc"), 1)
                    e.wait_ge(S("d_rc"), count(b, base=B))
                    e.tensor_tensor(t["on"][:, it.m(3, 2), :].rearrange("p (a j k) -> p a j k", a=2, j=4), o[:, :, :, 0:64],
                                    rc.unsqueeze(3).to_broadcast([128, 2, 4, 64]), ALU.mult).then_inc(S("d_on"), 1)
                b4 = it.b(4)
                if b4 is not None:
                    e.wait_ge(S("d_wo"), count(b4, base=B))
                    e.tensor_tensor(rows(Z, b4), rows(Z, b4), R[1][:, 0:1, 0:128], ALU.add).then_inc(S("d_add"), 1)
                b5 = it.b(5)
                if b5 is not None:
                    m = it.m(5, 4)
                    e.wait_ge(S(f"d_h2_{m}"), 8 * (b5 + B) + 32 - 8 * m)
                    apart(e)
                    e.bn_stats(st[:, 0, :], rows(H2, b5)).then_inc(S("d_bn"), 1)
                b = it.b(0)
                if b is not None:
                    e.wait_ge(S("d_hh"), count(b, base=B))
                    m = it.m(0, 2)
                    e.tensor_tensor(t["hT"][1][0:64, m, :], R[1][0:64, 1, 0:128], t["hT"][0][0:64, m, :].bitcast(F32), ALU.subtract)
                    e.tensor_tensor(t["hT"][1][64:128, m, 1:128], R[1][64:128, 1, 0:127],
                                    t["hT"][0][64:128, m, 1:128].bitcast(F32), ALU.subtract).then_inc(S("d_hl"), 1)
                if b5 is not None:
                    stats_tail(e, b5, S("d_bn"), S("d_ag"), S("d_ve"), base=B)
            pipeline(e, NB, 8, 4, body)

        def da_pool(e, l):
            t, B = d, NB * l
            da_start(e, l)

            def body(it):
                b = it.b(1)
                if b is not None:
                    p = it.m(1, 2)
                    e.wait_ge(S("d_B"), count(b, base=B))
                    e.tensor_tensor(t["A"][:, p, :], t["A"][:, p, :], t["B"][:, p, :], ALU.add).then_inc(S("d_rt"), 1)
                    e.wait_ge(S("d_vv"), count(b, base=B))
                    e.tensor_tensor(t["r"][:, p, :], t["vv"][:, p, :], nhalf[:, 0:16], ALU.pow).then_inc(S("d_r"), 1)
                    e.wait_ge(S("d_r"), count(b, base=B))
                    A = t["A"][:, p, :].rearrange("p (h d) -> p h d", d=DL)
                    e.tensor_tensor(A, A, t["r"][:, p, :].unsqueeze(2).to_broadcast([128, 16, DL]), ALU.mult)\
                        .then_inc(S("d_qkn"), 1)
                b = it.b(5)
                if b is not None:
                    e.wait_ge(S("d_ve"), count(b, base=B))
                    root(e, b).then_inc(S("d_rs"), 1)
            pipeline(e, NB, 8, 4, body)

        def da_sync(e, l):
            B = NB * l
            if l == 0:
                e.wait_ge(S("d_con"), 8)
            else:
                e.wait_ge(S("f_xn"), count(NG - 1))

            def body(it):
                b = it.b(4)
                if b is not None:
                    s = S(f"d_h2_{it.m(4, 4)}")
                    e.wait_ge(S("d_add"), count(b, base=B))
                    e.dma_start(H2[:, bass.ds(b, 1), 0:64], Z[:, bass.ds(b, 1), 0:64]).then_inc(s, 16)
                    e.dma_start(H2[1:128, bass.ds(b, 1), 64:128], Z[0:127, bass.ds(b, 1), 64:128]).then_inc(s, 16)
            pipeline(e, NB, 8, 4, body)

        def df_start(e, l):
            e.wait_ge(S("d_rs"), count(NB - 1, base=NB * l))
            e.wait_ge(S("d_hl"), count(NB - 1, base=NB * l))

        def df_tensor(e, l):
            t, B = f, NG * l
            df_start(e, l)
            e.wait_ge(S("d_add"), count(NB - 1, base=NB * l))
            e.wait_ge(S("f_con"), l + 1)

            def body(it):
                b = it.b(2)
                if b is not None:
                    if past(b - 1):
                        e.wait_ge(S("f_add"), count(b - 1, base=B))
                    e.wait_ge(S("f_gt"), count(b, 3, 3, base=B))
                    for j in range(GB):
                        for c in range(3):
                            n = 128 if c < 2 else HC[2] + 1
                            mm = e.matmul(R[0][:, 1, 128 * j:128 * j + 128], t["gt"][0:n, it.m(2, 2), c, 128 * j:128 * j + 128],
                                          w2l[0:n, l, c, :], start=(c == 0), stop=(c == 2))
                    mm.then_inc(S("f_y"), 1)
                b = it.b(0)
                if b is not None:
                    if past(b - 1):
                        e.wait_ge(S("f_hn"), count(b - 1, base=B))
                    e.wait_ge(S("f_xn"), count(b, base=B))
                    for j in range(GB):
                        mm = e.transpose(R[0][:, 0, 128 * j:128 * j + 128], t["xn"][:, j, :], ident[:])
                    mm.then_inc(S("f_xT"), 1)
                b = it.b(1)
                if b is not None:
                    x = [x[:, it.m(1, 2), :] for x in t["hs"]]
                    e.wait_ge(S("f_lo"), count(b, base=B))
                    for c, n in enumerate(HC):
                        if past(b - 1):
                            e.wait_ge(S("f_gt"), count(b - 1, c + 1, 3, base=B))
                        for half in (1, 0):
                            o = half * HID + 128 * c
                            passes(e, R[1 + c][0:n, half, :], [w[:, o:o + n] for w in w1l[l]], x)\
                                .then_inc(S("f_g" if half else "f_a"), 1)
            pipeline(e, NG, 4, 2, body)

        def df_scalar(e, l):
            t, B = f, NG * l
            df_start(e, l)

            def body(it):
                b = it.b(0)
                if b is not None:
                    e.wait_ge(S("f_hn"), count(b, base=B))
                    e.activation(t["hs"][0][:, it.m(0, 2), :], t["hn"][:, it.m(0, 2), :], ACT.Copy).then_inc(S("f_hi"), 1)
                b = it.b(1)
                if b is not None:
                    for c, n in enumerate(HC):
                        e.wait_ge(S("f_g"), count(b, c + 1, 3, base=B))
                        if past(b - 1):
                            e.wait_ge(S("f_gt"), count(b - 1, c + 1, 3, base=B))
                        e.activation(t["gl"][0:n, c, :], R[1 + c][0:n, 1, :], ACT.Gelu, bias=b1l[0:n, l, 3 + c:4 + c])\
                            .then_inc(S("f_gl"), 1)
            pipeline(e, NG, 4, 2, body)

        def df_vector(e, l):
            t, B = f, NG * l
            df_start(e, l)
            e.memset(t["gt"][:], 1.0).then_inc(S("f_con"), 1)
            e.wait_ge(S("f_con"), l + 1)

            def body(it):
                b = it.b(0)
                if b is not None:
                    for j in range(GB):
                        bj = b * GB + j
                        e.tensor_scalar(t["xn"][:, j:j + 1, :], rows(H2, bj),
                                        mv[:, bass.ds(bj, 1), 0:1].rearrange("p a b -> p (a b)"), rs[:, bass.ds(bj, 1)],
                                        ALU.subtract, ALU.mult).then_inc(S("f_xn") if j == GB - 1 else S("f_xnj"), 1)
                b = it.b(2)
                if b is not None:
                    zr = Z[:, bass.ds(b * GB, GB), :]
                    e.wait_ge(S("f_y"), count(b, base=B))
                    e.tensor_tensor(zr, zr, R[0][:, 1, :].rearrange("p (a b) -> p a b", b=128), ALU.add).then_inc(S("f_add"), 1)
                    if l == DEPTH - 1:
                        m = it.m(2, 2)
                        e.wait_ge(S("f_add"), count(b, base=B))
                        if not (it.static and it.i < 4):
                            e.wait_ge(S(f"out{m}"), 8 * (b - m))
                        e.tensor_tensor(t["o"][:, m, :].rearrange("p (a b) -> p a b", b=128), zr, X[:, bass.ds(b * GB, GB), :],
                                        ALU.add).then_inc(S("f_o"), 1)
                b = it.b(0)
                if b is not None:
                    m = it.m(0, 2)
                    e.wait_ge(S("f_xT"), count(b, base=B))
                    e.tensor_scalar(t["hn"][:, m, :], R[0][:, 0, :], lng[:, l, 0:1], lng[:, l, 1:2], ALU.mult, ALU.add)\
                        .then_inc(S("f_hn"), 1)
                    e.wait_ge(S("f_hi"), count(b, base=B))
                    e.tensor_tensor(t["hs"][1][:, m, :], t["hn"][:, m, :], t["hs"][0][:, m, :].bitcast(F32), ALU.subtract)\
                        .then_inc(S("f_lo"), 1)
                b = it.b(1)
                if b is not None:
                    for c, n in enumerate(HC):
                        e.wait_ge(S("f_a"), count(b, c + 1, 3, base=B))
                        e.wait_ge(S("f_gl"), count(b, c + 1, 3, base=B))
                        e.scalar_tensor_tensor(out=t["gt"][0:n, it.m(1, 2), c, :], in0=R[1 + c][0:n, 0, :],
                                               scalar=b1l[0:n, l, c:c + 1], in1=t["gl"][0:n, c, :], op0=ALU.add, op1=ALU.mult)\
                            .then_inc(S("f_gt"), 1)
            pipeline(e, NG, 4, 2, body)

        def df_sync(e):
            def body(it):
                b = it.b(2)
                if b is not None:
                    m = it.m(2, 2)
                    e.wait_ge(S("f_o"), count(b))
                    e.dma_start(out[:, bass.ds(b * 512, 512)], f["o"][:, m, :]).then_inc(S(f"out{m}"), 16)
            pipeline(e, NG, 4, 2, body)
            for m in range(2):
                e.wait_ge(S(f"out{m}"), 16 * NG // 2)
        block = ctx.enter_context(nc.Block())

        @block.sync
        def _(sync):
            load(sync)
            load_d(sync)
            for l in range(DEPTH):
                da_sync(sync, l)
            df_sync(sync)

        @block.scalar
        def _(act):
            split_act(act)
            a_scalar(act)
            b_scalar(act)
            c_scalar(act)
            split_act_d(act)
            for l in range(DEPTH):
                da_scalar(act, l)
                df_scalar(act, l)

        @block.vector
        def _(dve):
            split_dve(dve)
            a_vector(dve)
            b_vector(dve)
            c_vector(dve)
            split_dve_d(dve)
            for l in range(DEPTH):
                da_vector(dve, l)
                df_vector(dve, l)

        @block.gpsimd
        def _(pool):
            start_pool(pool)
            a_pool(pool)
            b_pool(pool)
            c_pool(pool)
            for l in range(DEPTH):
                da_pool(pool, l)

        @block.tensor
        def _(pe):
            a_tensor(pe)
            b_tensor(pe)
            c_tensor(pe)
            for l in range(DEPTH):
                da_tensor(pe, l)
                df_tensor(pe, l)


def lay_out(i):
    x = i["x"]
    a = {}
    a["x"] = x.transpose(1, 0, 2).reshape(T, NB * D)
    a["ctx"] = i["ctx_1024"].transpose(2, 0, 1).reshape(D, NB * SK)
    a["mask"] = i["mask_1x1xSxS2_ik0"].reshape(T, SK)
    a["wq0"] = i["L0_xattn_wq"].T
    a["wkv0"] = np.concatenate([i["L0_xattn_wk"].T, i["L0_xattn_wv"].T], axis=1)
    a["wo0"] = i["L0_xattn_wo"].T.reshape(8, 128, D).transpose(1, 0, 2).reshape(128, 8 * D)
    a["nrm0"] = np.stack([np.tile(i["L0_xattn_q_norm_w"], 2), np.tile(i["L0_xattn_k_norm_w"], 2)], axis=1)
    a["wg"] = i["L0_ffn_wg"].T
    a["w1e"] = i["L0_ffn_w1"].reshape(NE * INTER, D).T
    a["w3e"] = i["L0_ffn_w3"].reshape(NE * INTER, D).T
    a["w2e"] = i["L0_ffn_w2"].transpose(0, 2, 1).reshape(NCH, 128, D).transpose(1, 0, 2).reshape(128, NCH * D)
    a["l1"] = np.concatenate([i["L1_xattn_w_" + n].T for n in "qkvo"], axis=1)
    a["wqkv"] = i["L1_ffn_wqkv"].transpose(1, 0, 2).reshape(D, DEPTH * 1536)
    qk = np.stack([i["L1_ffn_q_scale"], i["L1_ffn_k_scale"]], axis=1)
    swapped = np.concatenate([qk[..., DL // 2:], qk[..., :DL // 2]], axis=-1)
    a["qks"] = np.tile(np.stack([qk, swapped], axis=1).reshape(1, -1), (T, 1))
    a["wol"] = i["L1_ffn_wo"].reshape(DEPTH, 4, 128, D).transpose(2, 0, 1, 3).reshape(128, DEPTH * 4 * D)
    a["lng"] = np.stack([i["L1_ffn_ln_g"], i["L1_ffn_ln_b"]], axis=2).transpose(1, 0, 2).reshape(D, DEPTH * 2)
    a["w1l"] = i["L1_ffn_w1"].transpose(1, 0, 2).reshape(D, DEPTH * 2 * HID)
    b1 = np.zeros((128, DEPTH, 6), np.float32)
    w2 = np.zeros((128, DEPTH, 3, D), np.float32)
    for c, n in enumerate(HC):
        for half in range(2):
            b1[:n, :, 3 * half + c] = i["L1_ffn_b1"][:, half * HID + 128 * c:half * HID + 128 * c + n].T
        w2[:n, :, c] = i["L1_ffn_w2"][:, 128 * c:128 * c + n].transpose(1, 0, 2)
    w2[HC[2], :, 2] = i["L1_ffn_b2"]
    a["b1l"] = b1.reshape(128, DEPTH * 6)
    a["w2l"] = w2.reshape(128, DEPTH * 3 * D)
    return a


def constants():
    c = {}
    c["ident"] = np.eye(128, dtype=np.float32)
    t = np.arange(T)
    c["band"] = np.where((t[:, None] < t[None, :]) | (t[:, None] > t[None, :] + WINDOW), BAND, 0.0).astype(np.float32)
    half = np.arange(0, DL, 2, dtype=np.float32)
    freqs = (t.astype(np.float32)[:, None] * (1.0 / np.float32(10000.0) ** (half / DL)).astype(np.float32)[None]).astype(np.float64)
    base = (half + 0.4 * DL) / (1.4 * DL)
    scale = base[None, :].astype(np.float64) ** ((t - T // 2) / float(WINDOW // 2))[:, None]
    cos, sin = np.cos(freqs), np.sin(freqs)
    both = lambda x, y: np.concatenate([x, y], axis=-1)
    q = [both(cos * scale, cos * scale) * 8.0, both(-sin * scale, sin * scale) * 8.0]
    k = [both(cos / scale, cos / scale), both(-sin / scale, sin / scale)]
    c["rot"] = np.stack([np.stack([q[0], k[0]], 1), np.stack([q[1], k[1]], 1)], 1).reshape(T, 256).astype(np.float32)
    c["keyi"] = np.tile(np.arange(NE, 0, -1, dtype=np.float32), (128, GB))
    c["head"] = (np.arange(128)[:, None] // DH1 % 4 == np.arange(4)[None]).astype(np.float32)
    return c


def kernel(**inputs):
    import concourse.bacc as bacc
    from concourse.bass_utils import run_bass_kernel_spmd

    nc = bacc.Bacc("TRN2", target_bir_lowering=False, num_devices=1)
    laid = {**lay_out({k: np.asarray(v) for k, v in inputs.items()}), **constants()}
    arrays, args = {}, {}
    for name, value in laid.items():
        value = np.ascontiguousarray(value)
        arrays["in_" + name] = value
        args[name + "_in"] = nc.dram_tensor("in_" + name, value.shape, mybir.dt.from_np(value.dtype), kind="ExternalInput").ap()
    out = nc.dram_tensor("out", (T, NB * D), F32, kind="ExternalOutput").ap()
    program(nc, out=out, **args)
    result = run_bass_kernel_spmd(nc, [arrays], core_ids=[0]).results[0]["out"]
    return result.reshape(T, NB, D).transpose(1, 0, 2)
```

```python
from contextlib import ExitStack

import numpy as np

import concourse.bass as bass
from concourse import mybir

F32 = mybir.dt.float32
F32R = mybir.dt.float32r
BF16 = mybir.dt.bfloat16
I32 = mybir.dt.int32
ALU = mybir.AluOpType
ACT = mybir.ActivationFunctionType
AX = mybir.AxisListType

NB = 32
T = 128
D = 128
SK = 77
H0, HK0, DH0 = 16, 4, 64
NE, INTER = 8, 256
NCH = NE * INTER // 128
H1, DH1 = 16, 8
DEPTH, HL, DL = 2, 8, 64
WINDOW = 64
HID = int(D * 4 * 2 / 3)
HC = [128, 128, HID - 256]
GB = 4
NG = NB // GB
ST = 8
LN_EPS = 1e-5
RMS_EPS = 1e-6
NEG = -1e9
BAND = -1e30



class It:

    def __init__(self, i, phase, n, unroll):
        self.i, self.phase, self.n, self.unroll = i, phase, n, unroll
        self.static = type(i) is int

    def b(self, lag):
        if self.static and not 0 <= self.i - lag < self.n:
            return None
        return self.i - lag

    def m(self, lag, size):
        return (self.phase - lag) % size

    def seen(self, lag):
        return not self.static or self.i >= lag

    def upto(self, lag, base=0):
        last = min(self.i - lag, self.n - 1) if self.static else self.i - lag
        return last + base + 1


def pipeline(eng, n, lags, unroll, body):
    assert lags % unroll == 0 and (n - lags) % unroll == 0
    for i in range(lags):
        body(It(i, i % unroll, n, unroll))
    with eng.Fori(lags, n - unroll + 1, unroll) as r:
        for u in range(unroll):
            body(It(r + u, u, n, unroll))
    for i in range(n, n + lags):
        body(It(i, i % unroll, n, unroll))


def past(b):
    return type(b) is not int or b >= 0


def count(b, j=1, k=1, base=0):
    return (b + base) * k + j


def program(nc, out, x_in, ctx_in, mask_in, wq0_in, wkv0_in, wo0_in, nrm0_in, wg_in, w1e_in, w3e_in, w2e_in,
            l1_in, wqkv_in, qks_in, wol_in, lng_in, w1l_in, b1l_in, w2l_in,
            ident_in, band_in, rot_in, keyi_in, head_in):
    with ExitStack() as ctx:
        def sem(name):
            return ctx.enter_context(nc.semaphore(name))

        first = (nc.sbuf_base + 31) // 32 * 32
        room = [first]

        def at(name, shape, dt=F32):
            size = 2 if dt == BF16 else 4
            for n in shape[1:]:
                size *= n
            t = nc.alloc_sbuf_tensor_at(name, shape, dt, offset=room[0])
            room[0] += (size + 31) // 32 * 32
            assert room[0] <= nc.sbuf_usable_end, name
            return t

        R = [ctx.enter_context(nc.psum_tensor(f"slot{i}", [128, 2, 512], F32)) for i in range(4)]

        def bank(k):
            return R[k // 2][:, k % 2, :]

        X = at("X", [128, NB, D])
        mv = at("mv", [128, NB, 2])
        agg = at("agg", [128, ST, 2])
        eps = at("eps", [128, ST, 2])
        rs = at("rs", [128, NB])
        ident = at("ident", [128, 128])
        identb = at("identb", [128, 128], BF16)
        band = at("band", [128, 128])
        bandb = at("bandb", [128, 4, 128], BF16)
        mask = at("mask", [128, SK], I32)
        maskz = at("maskz", [128, SK], I32)
        negt = at("negt", [128, SK])
        nhalf = at("nhalf", [128, 32])
        head = at("head", [128, 4])
        keyi = at("keyi", [128, GB, NE])
        nrm0 = at("nrm0", [128, 2])
        st = at("st", [128, ST, 6])
        stage = at("stage", [128, 2, 2048])
        wol = at("wol", [128, DEPTH, 4, 128])
        w2l = at("w2l", [128, DEPTH, 3, 128])
        lng = at("lng", [128, DEPTH, 2])
        b1l = at("b1l", [128, DEPTH, 6])
        rot = at("rot", [128, 2, 2, 64])
        qks = at("qks", [128, DEPTH, 2, 2, 64])
        T1 = at("T1", [128, DEPTH, 2, 64])
        T2 = at("T2", [128, DEPTH, 2, 64])

        attentions = room[0]
        wq0 = [at(f"wq0{p}", [128, H0 * DH0], F32R) for p in "hl"]
        wkv0 = [at(f"wkv0{p}", [128, 512], F32R) for p in "hl"]
        wo0 = at("wo0", [128, 8, 128])
        l1 = at("l1", [128, 4, 128])
        wgs = [at(f"wg{p}", [128, NE], F32R) for p in "hl"]
        wg = at("wg", [128, NE])
        experts = room[0]
        w1e = [at(f"w1e{p}", [128, 2048], F32R) for p in "hl"]
        w3e = [at(f"w3e{p}", [128, 2048], F32R) for p in "hl"]
        w2e = [at(f"w2e{p}", [128, NCH, 128], F32R) for p in "hl"]
        weights_end = room[0]
        room[0] = attentions
        H2 = at("H2", [128, NB, D])
        assert room[0] <= experts
        room[0] = experts
        wqkv = [[at(f"wqkv{l}{p}", [128, 1536], F32R) for p in "hl"] for l in range(DEPTH)]
        w1l = [[at(f"w1l{l}{p}", [128, 2 * HID], F32R) for p in "hl"] for l in range(DEPTH)]
        assert room[0] <= weights_end
        room[0] = weights_end
        ctx_sb = at("ctx_sb", [128, NB, SK])
        ctx_end = room[0]
        a = {}
        a["xn"] = at("ac_xn", [128, 2, 128])
        a["xT"] = [at(f"a_xT{p}", [128, 2, 128], F32R) for p in "hl"]
        a["c"] = [at(f"a_c{p}", [128, 4, SK], F32R) for p in "hl"]
        a["sq"] = at("a_sq", [128, 1024])
        a["sqk"] = at("a_sqk", [128, 256])
        a["kr"] = at("a_kr", [128, 256])
        a["ssq"] = at("a_ssq", [128, 16])
        a["ssk"] = at("a_ssk", [128, 4])
        a["vvq"] = at("a_vvq", [128, 16])
        a["vvk"] = at("a_vvk", [128, 4])
        a["rq"] = at("a_rq", [128, 2, 16])
        a["rk"] = at("a_rk", [128, 4])
        a["kn"] = at("a_kn", [128, 4, 2, 64])
        a["v"] = at("a_vt", [128, 4, 256])
        a["kb"] = at("a_kb", [128, 2, 4, 2 * SK])
        a["wqk"] = at("a_wqk", [128, 1])
        a["q"] = at("a_q", [128, 1024])
        a["qT"] = at("a_qT", [128, 8, 128])
        a["mx"] = at("a_mx", [128, 16])
        a["nm"] = at("a_nm", [128, 16])
        a["p"] = at("a_p", [128, 16, SK])
        a["sum"] = at("a_sum", [128, 16])
        a["rc"] = at("a_rc", [128, 16])
        a["pT"] = at("a_pT", [128, 16, 128])
        a["oT"] = at("a_oT", [128, 2, 8, 128])
        room[0] = ctx_end
        g_ = {}
        g_["xn"] = at("b_xn", [128, GB, 128])
        g_["xT"] = [at(f"b_xT{p}", [128, 2, 512], F32R) for p in "hl"]
        g_["wt"] = at("b_wt", [128, 2, GB, NE])
        g_["wb"] = at("b_wb", [128, 2, 512])
        g_["s"] = at("b_s", [128, 2, 512])
        g_["sp"] = at("b_sp", [128, 2, 512])
        g_["g"] = at("b_g", [128, 4, 512])
        g_["gs"] = [at(f"b_g{p}", [128, 4, 512], F32R) for p in "hl"]
        g_["yT"] = at("b_yT", [128, 512])
        for n in ("m", "s", "rc", "m1", "k1", "m2", "k2", "dn", "rd"):
            g_["r" + n] = at("b_r" + n, [128, GB])
        for n in ("l", "e", "p", "q", "k", "o", "q2", "e2", "k2", "o2", "t"):
            g_["R" + n] = at("b_R" + n, [128, GB, NE])
        room[0] = ctx_end
        c_ = {}
        c_["xn"] = at("ac_xn", [128, 2, 128])
        c_["xT"] = at("c_xT", [128, 2, 128])
        c_["c"] = at("c_c", [128, 4, SK])
        c_["qT"] = [at(f"c_qT{p}", [128, 2, 128], F32R) for p in "hl"]
        c_["kh"] = at("c_kh", [128, SK], F32R)
        c_["kl"] = at("c_kl", [128, SK])
        c_["kb"] = [at(f"c_kb{p}", [128, 2, 4, SK], F32R) for p in "hl"]
        c_["vz"] = at("c_vz", [128, 4, 4, 4 * 40])
        c_["nm"] = at("c_nm", [128, 16])
        c_["p"] = at("c_p", [128, 2, 16, SK])
        c_["sum"] = at("c_sum", [128, 16])
        c_["rc"] = at("c_rc", [128, 16])
        c_["pT"] = at("c_pT", [128, 16, 128])
        c_["oT"] = at("c_oT", [128, 2, 128])
        room[0] = weights_end
        Z = at("Z", [128, NB, D])
        d = {}
        d["v1"] = at("d_v1", [128, 4, HL, 65])
        d["hT"] = [at(f"d_hT{p}", [128, 2, 128], F32R) for p in "hl"]
        both = room[0]
        d["sq"] = at("d_sq", [128, 1024])
        d["ss"] = at("d_ss", [128, 2, 16])
        d["vv"] = at("d_vv", [128, 2, 16])
        d["r"] = at("d_r", [128, 2, 16])
        d["z"] = at("d_zx", [128, 2, 128])
        d["A"] = at("d_A", [128, 2, 1024])
        d["B"] = at("d_B", [128, 2, 1024])
        d["qT"] = at("d_qT", [128, 8, 128])
        d["mx"] = at("d_mx", [128, 8])
        d["nm"] = at("d_nm", [128, 8])
        d["p"] = at("d_p", [128, 2, 8, 128])
        d["pT"] = at("d_pT", [128, 8, 128])
        d["rc"] = at("d_rc", [128, 8])
        d["on"] = at("d_on", [128, 2, 512])
        d["oT"] = at("d_oT", [128, 4, 128])
        room[0] = both
        f = {}
        f["xn"] = at("f_xn", [128, GB, 128])
        f["hn"] = at("f_hn", [128, 2, 512])
        f["hs"] = [at(f"f_h{p}", [128, 2, 512], F32R) for p in "hl"]
        f["gl"] = at("f_gl", [128, 3, 512])
        f["gt"] = at("f_gt", [128, 2, 3, 512])
        f["o"] = at("f_o", [128, 2, 512])

        made = {}

        def S(name):
            if name not in made:
                made[name] = sem(name)
            return made[name]

        def load(e):
            def laid(dst, src, done):
                names = "abcd"[:len(dst.shape) - 1]
                e.dma_start(dst[:].rearrange(f"p {' '.join(names)} -> p ({' '.join(names)})"), src).then_inc(S(done), 16)

            half = NB // 2 * D
            e.dma_start(stage[:, 0, 0:1024], wq0_in).then_inc(S("stage0_in"), 16)
            e.dma_start(stage[:, 1, 0:512], wkv0_in).then_inc(S("stage1_in"), 16)
            e.dma_start(X[:, 0:NB // 2, :], x_in[:, 0:half].rearrange("p (b d) -> p b d", d=D)).then_inc(S("x0_in"), 16)
            for dst, src in ((ident, ident_in), (band, band_in), (mask, mask_in), (nrm0, nrm0_in), (wg, wg_in)):
                laid(dst, src, "const_in")
            laid(ctx_sb, ctx_in, "ctx_in")
            e.dma_start(X[:, NB // 2:NB, :], x_in[:, half:2 * half].rearrange("p (b d) -> p b d", d=D)).then_inc(S("x1_in"), 16)
            for dst, src in ((wo0, wo0_in), (head, head_in), (keyi, keyi_in), (l1, l1_in), (wol, wol_in), (w2l, w2l_in),
                             (lng, lng_in), (b1l, b1l_in), (rot, rot_in), (qks, qks_in)):
                laid(dst, src, "late_in")
            for n, src in enumerate((w1e_in, w3e_in, w2e_in)):
                e.wait_ge(S("split"), (1, 2, 4)[n])
                e.dma_start(stage[:, n % 2, :], src).then_inc(S(f"stage{n % 2}_in"), 16)

        N_CONST, N_LATE = 5, 10

        def split_act(e):
            for n, (dst, w) in enumerate(((wq0[0][:], 1024), (wkv0[0][:], 512))):
                e.wait_ge(S(f"stage{n}_in"), 16)
                e.activation(dst, stage[:, n, 0:w], ACT.Copy).then_inc(S("high"), 1)
            e.wait_ge(S("const_in"), 16 * N_CONST)
            e.activation(wgs[0][:], wg[:], ACT.Copy).then_inc(S("high"), 1)
            e.activation(identb[:], ident[:], ACT.Copy).then_inc(S("high"), 1)
            for k in range(4):
                e.activation(bandb[:, k, :], band[:], ACT.Copy).then_inc(S("high"), 1)

        expert_weights = (w1e, w3e, w2e)

        def flat(w):
            return w[:] if len(w.shape) == 2 else w[:].rearrange("p a b -> p (a b)")

        def split_expert_act(e, n):
            e.wait_ge(S(f"stage{n % 2}_in"), 32 + 16 * (n // 2))
            e.activation(flat(expert_weights[n][0]), stage[:, n % 2, :], ACT.Copy).then_inc(S("high"), 1)

        def split_expert_dve(e, n):
            hi, lo = expert_weights[n]
            e.wait_ge(S("high"), 8 + n + 1)
            e.tensor_tensor(flat(lo), stage[:, n % 2, :], flat(hi).bitcast(F32), ALU.subtract).then_inc(S("split"), 1)

        def split_dve(e):
            e.memset(eps[:, :, 0:1], 0.0).then_inc(S("eps"), 1)
            e.memset(eps[:, :, 1:2], LN_EPS).then_inc(S("eps"), 1)
            e.memset(nhalf[:], -0.5).then_inc(S("eps"), 1)
            e.wait_ge(S("eps"), 3)
            e.memset(negt[:], NEG).then_inc(S("const"), 1)
            e.memset(a["kb"][:], 0.0).then_inc(S("const"), 1)
            for n, ((hi, lo), w) in enumerate(((wq0, 1024), (wkv0, 512))):
                e.wait_ge(S("high"), n + 1)
                e.tensor_tensor(lo[:], stage[:, n, 0:w], hi[:].bitcast(F32), ALU.subtract).then_inc(S("split"), 1)
            e.wait_ge(S("high"), 3)
            e.tensor_tensor(wgs[1][:], wg[:], wgs[0][:].bitcast(F32), ALU.subtract).then_inc(S("split"), 1)
            e.tensor_scalar(maskz[:], mask[:], 0.0, None, ALU.is_equal).then_inc(S("const"), 1)
            e.tensor_tensor(a["wqk"][:], nrm0[:, 0:1], nrm0[:, 1:2], ALU.mult).then_inc(S("const"), 1)
            first_stats(e, 0)
            e.wait_ge(S("const"), 4)

        def first_stats(e, n):
            b = n * ST
            e.wait_ge(S(f"x{2 * b // NB}_in"), 16)
            for u in range(ST):
                e.bn_stats(st[:, u, :], X[:, b + u, :]).then_inc(S("stat0"), 1)
            for u in range(ST):
                e.wait_ge(S("stat0"), b + u + 1)
                e.bn_aggr(agg[:, u, :], st[:, u, :]).then_inc(S("stat"), 1)
            e.wait_ge(S("stat"), b + ST)
            e.tensor_tensor(mv[:, b:b + ST, :], agg[:], eps[:], ALU.add).then_inc(S("var0"), 1)

        def first_roots(e, n):
            b = n * ST
            e.wait_ge(S("var0"), n + 1)
            e.tensor_tensor(rs[:, b:b + ST], mv[:, b:b + ST, 1:2].rearrange("p a b -> p (a b)"),
                            nhalf[:, 0:ST], ALU.pow).then_inc(S("rs"), 1)

        def start_pool(e):
            e.wait_ge(S("eps"), 3)
            first_roots(e, 0)

        def rows(ap, b):
            return ap[:, bass.ds(b, 1), :]

        def apart(e):
            e.sem_inc(S("apart"), 1)

        def passes(e, o, ws, xs):
            e.matmul(o, ws[1], xs[0], start=True, stop=False)
            e.matmul(o, ws[0], xs[1], start=False, stop=False)
            return e.matmul(o, ws[0], xs[0], start=False, stop=True)


        def a_tensor(e):
            e.wait_ge(S("split"), 3)
            e.wait_ge(S("const"), 4)

            def body(it):
                b = it.b(2)
                if b is not None:
                    if it.seen(4):
                        e.wait_ge(S("ac_oTe"), it.upto(4))
                    if it.static:
                        if it.seen(2):
                            e.wait_ge(S("ac_v"), it.upto(2))
                    e.wait_ge(S("a_q"), count(b))
                    for c in range(8):
                        mm = e.transpose(R[1][:, c // 4, 128 * (c % 4):128 * (c % 4) + 128],
                                         a["q"][:, 128 * c:128 * c + 128], ident[:])
                    mm.then_inc(S("a_qT"), 1)
                b = it.b(1)
                if b is not None:
                    p = it.m(1, 2)
                    if it.seen(5):
                        e.wait_ge(S("ac_add"), it.upto(5))
                    if it.static:
                        if it.seen(2):
                            e.wait_ge(S("a_q"), it.upto(2))
                    if it.seen(1):
                        e.wait_ge(S("ac_xl"), it.upto(1))
                    if it.seen(2):
                        e.wait_ge(S("a_kTe"), it.upto(2))
                    e.wait_ge(S("ac_xl"), count(b))
                    for h in range(2):
                        mm = passes(e, R[0][:, h, :], [x[:, p, :] for x in a["xT"]],
                                    [w[:, 512 * h:512 * h + 512] for w in wq0])
                    mm.then_inc(S("a_projq"), 1)
                b = it.b(3)
                if b is not None:
                    for half, slot in ((0, 2), (1, 3)):
                        if half == 0:
                            if it.seen(3):
                                e.wait_ge(S("ac_expa"), it.upto(3))
                        else:
                            if it.seen(3):
                                e.wait_ge(S("ac_expb"), it.upto(3))
                        e.wait_ge(S(("ac_na", "ac_nb")[half]), count(b))
                        for c in range(8):
                            h = 8 * half + 4 * (c // 4) + 2 * (c % 2) + c // 2 % 2
                            mm = e.transpose(R[slot][0:SK, c // 4, 128 * (c % 4):128 * (c % 4) + 128], a["p"][:, h, :], ident[:])
                        mm.then_inc(S(("ac_PTa", "ac_PTb")[half]), 1)
                b = it.b(1)
                if b is not None:
                    if it.seen(2):
                        e.wait_ge(S("a_qTe"), it.upto(2))
                    e.wait_ge(S("ac_cl"), count(b))
                    passes(e, R[1][0:SK, 0, :], [c[:, it.m(1, 4), :] for c in a["c"]], [w[:] for w in wkv0])\
                        .then_inc(S("a_kv"), 1)
                b = it.b(2)
                if b is not None:
                    e.wait_ge(S("a_qTe"), count(b))
                    e.wait_ge(S("a_kTe"), count(b))
                    for half, slot in ((0, 2), (1, 3)):
                        if half == 0:
                            if it.seen(3):
                                e.wait_ge(S("ac_pTa"), it.upto(3))
                        else:
                            if it.seen(3):
                                e.wait_ge(S("ac_pTb"), it.upto(3))
                        for k in range(4):
                            c = 4 * half + k
                            mm = e.matmul(R[slot][:, k // 2, 2 * SK * (k % 2):2 * SK * (k % 2) + 2 * SK],
                                          a["qT"][:, c, :], a["kb"][:, it.m(2, 2), c // 2, :], start=True, stop=True)
                        mm.then_inc(S(("ac_Sa", "ac_Sb")[half]), 1)
                b = it.b(3)
                if b is not None:
                    if it.seen(1):
                        e.wait_ge(S("ac_v"), it.upto(1))
                    if it.static:
                        if it.seen(2):
                            e.wait_ge(S("a_qTe"), it.upto(2))
                        if it.seen(4):
                            e.wait_ge(S("ac_oTe"), it.upto(4))
                    e.wait_ge(S("ac_pTa"), count(b))
                    e.wait_ge(S("ac_pTb"), count(b))
                    for g in range(HK0):
                        for odd in range(2):
                            mm = e.matmul(R[1][64 * odd:64 * odd + 64, g // 2, 256 * (g % 2):256 * (g % 2) + 256],
                                          a["v"][0:SK, it.m(3, 4), DH0 * g:DH0 * g + DH0],
                                          a["pT"][0:SK, 4 * g + 2 * odd:4 * g + 2 * odd + 2, :].rearrange("p a b -> p (a b)"),
                                          start=True, stop=True)
                    mm.then_inc(S("ac_PV"), 1)
                if it.b(0) is not None or it.b(1) is not None:
                    if it.seen(1):
                        e.wait_ge(S("a_q"), it.upto(1))
                b = it.b(0)
                if b is not None:
                    e.wait_ge(S("ac_xn"), count(b))
                    e.transpose(R[0][:, 1, 384:512], a["xn"][:, it.m(0, 2), :], ident[:]).then_inc(S("ac_xTp"), 1)
                b = it.b(1)
                if b is not None:
                    e.wait_ge(S("a_kn"), count(b))
                    for c in range(4):
                        mm = e.transpose(R[0][:, 1, SK * c:SK * c + SK],
                                         a["kn"][0:SK, c, :, :].rearrange("p a b -> p (a b)"), ident[0:SK, 0:SK])
                    mm.then_inc(S("a_kT"), 1)
                b = it.b(4)
                if b is not None:
                    if it.seen(1):
                        e.wait_ge(S("a_q"), it.upto(1))
                    if it.static:
                        if it.seen(5):
                            e.wait_ge(S("ac_add"), it.upto(5))
                    e.wait_ge(S("ac_oTe"), count(b))
                    for c in range(8):
                        mm = e.matmul(R[0][:, 0, 0:128], a["oT"][:, it.m(4, 2), c, :], wo0[:, c, :], start=(c == 0), stop=(c == 7))
                    mm.then_inc(S("ac_wo"), 1)
                if it.static and it.i == 3:
                    e.wait_ge(S("late_in"), 16 * N_LATE)
            pipeline(e, NB, 4, 4, body)

        def a_scalar(e):
            def body(it):
                b = it.b(2)
                if b is not None:
                    e.wait_ge(S("a_qT"), count(b))
                    e.activation(a["qT"][:].rearrange("p (a c) t -> p a (c t)", a=2), R[1][:], ACT.Copy).then_inc(S("a_qTe"), 1)
                b = it.b(1)
                if b is not None:
                    e.wait_ge(S("a_projq"), count(b))
                    if past(b - 1):
                        e.wait_ge(S("a_redq"), count(b - 1))
                    e.activation(a["sq"][:].rearrange("p (a b) -> p a b", a=2), R[0][:], ACT.Square).then_inc(S("a_sq"), 1)
                b = it.b(3)
                if b is not None:
                    e.wait_ge(S("ac_PTa"), count(b))
                    e.activation(a["pT"][0:SK, 0:8, :].rearrange("p (a c) t -> p a (c t)", a=2), R[2][0:SK, :, :], ACT.Copy)\
                        .then_inc(S("ac_pTa"), 1)
                b = it.b(1)
                if b is not None:
                    e.wait_ge(S("a_kv"), count(b))
                    if past(b - 1):
                        e.wait_ge(S("a_kn"), count(b - 1))
                    e.activation(a["kr"][0:SK, :], R[1][0:SK, 0, 0:256], ACT.Copy).then_inc(S("a_kr"), 1)
                    e.activation(a["v"][0:SK, it.m(1, 4), :], R[1][0:SK, 0, 256:512], ACT.Copy).then_inc(S("ac_v"), 1)
                    if past(b - 1):
                        e.wait_ge(S("a_qT"), count(b - 1))
                    e.activation(a["q"][:].rearrange("p (a b) -> p a b", a=2), R[0][:], ACT.Copy).then_inc(S("a_q"), 1)
                b = it.b(2)
                if b is not None:
                    e.wait_ge(S("a_nma"), count(b))
                    exponentials(e, a, 2, 0, 4, SK, S("ac_expa"), a["rq"][:, it.m(2, 2), :])
                b = it.b(3)
                if b is not None:
                    e.wait_ge(S("ac_PV"), count(b))
                    e.activation(a["oT"][:, it.m(3, 2), :, :].rearrange("p (a c) t -> p a (c t)", a=2), R[1][:], ACT.Copy)\
                        .then_inc(S("ac_oTe"), 1)
                b = it.b(2)
                if b is not None:
                    e.wait_ge(S("a_nmb"), count(b))
                    exponentials(e, a, 3, 1, 4, SK, S("ac_expb"), a["rq"][:, it.m(2, 2), :])
                if it.static and 1 <= it.i <= 3:
                    split_expert_act(e, it.i - 1)
            pipeline(e, NB, 4, 4, body)

        def exponentials(e, t, slot, half, nbank, nk, done, scale=None, head=lambda h: h):
            for k in range(2 * nbank):
                h = 2 * nbank * half + k
                i = e.activation(t["p"][:, h, :], R[slot][:, k // nbank, nk * (k % nbank):nk * (k % nbank) + nk], ACT.Exp,
                                 bias=t["nm"][:, h:h + 1], scale=1.0 if scale is None else scale[:, head(h):head(h) + 1])
            i.then_inc(done, 1)

        def normalize(e, t, h, nk):
            p = t["p"][:, h, :]
            return e.tensor_tensor(p, p, t["rc"][:, h].unsqueeze(2).to_broadcast([128, h.stop - h.start, nk]), ALU.mult)

        def layernorm(e, src, dst, b, m):
            return e.tensor_scalar(dst[:, m:m + 1, :], rows(src, b), mv[:, bass.ds(b, 1), 0:1].rearrange("p a b -> p (a b)"),
                                   rs[:, bass.ds(b, 1)], ALU.subtract, ALU.mult)

        def a_vector(e):
            e.wait_ge(S("rs"), 1)

            def largest(b, it, half, slot):
                s = R[slot][:, :, 0:4 * SK].rearrange("p a (j k) -> p a j k", k=SK)
                h = slice(8 * half, 8 * half + 8)
                e.wait_ge(S(("ac_Sa", "ac_Sb")[half]), count(b))
                e.tensor_reduce(a["mx"][:, h], s, AX.X, ALU.max, negate=True).then_inc(S(("ac_mxa", "ac_mxb")[half]), 1)
                e.wait_ge(S("a_rq"), count(b))
                e.wait_ge(S(("ac_mxa", "ac_mxb")[half]), count(b))
                e.tensor_tensor(a["nm"][:, h], a["mx"][:, h], a["rq"][:, it.m(2, 2), h], ALU.mult)\
                    .then_inc(S(("a_nma", "a_nmb")[half]), 1)

            def sums(b, half):
                h = slice(8 * half, 8 * half + 8)
                e.wait_ge(S(("ac_expa", "ac_expb")[half]), count(b))
                e.tensor_reduce(a["sum"][:, h], a["p"][:, h, :], AX.X, ALU.add).then_inc(S(("ac_suma", "ac_sumb")[half]), 1)
                e.wait_ge(S(("ac_suma", "ac_sumb")[half]), count(b))
                e.reciprocal(a["rc"][:, h], a["sum"][:, h]).then_inc(S(("ac_rca", "ac_rcb")[half]), 1)

            def body(it):
                b = it.b(0)
                if b is not None:
                    layernorm(e, X, a["xn"], b, it.m(0, 2)).then_inc(S("ac_xn"), 1)
                b = it.b(3)
                if b is not None:
                    e.wait_ge(S("ac_PTb"), count(b))
                    e.tensor_copy(a["pT"][0:SK, 8:16, :].rearrange("p (a c) t -> p a (c t)", a=2), R[3][0:SK, :, :])\
                        .then_inc(S("ac_pTb"), 1)
                b = it.b(2)
                if b is not None:
                    largest(b, it, 0, 2)
                b = it.b(1)
                if b is not None:
                    e.wait_ge(S("a_sqk"), count(b))
                    e.tensor_reduce(a["ssk"][0:SK, :], a["sqk"][0:SK, :].rearrange("p (h d) -> p h d", d=DH0),
                                    AX.X, ALU.add).then_inc(S("a_redk"), 1)
                    e.wait_ge(S("a_redk"), count(b))
                    e.tensor_scalar(a["vvk"][0:SK, :], a["ssk"][0:SK, :], 1.0 / DH0, RMS_EPS, ALU.mult, ALU.add)\
                        .then_inc(S("a_vvk"), 1)
                    e.wait_ge(S("a_sq"), count(b))
                    e.tensor_reduce(a["ssq"][:], a["sq"][:].rearrange("p (h d) -> p h d", d=DH0), AX.X, ALU.add)\
                        .then_inc(S("a_redq"), 1)
                b = it.b(2)
                if b is not None:
                    largest(b, it, 1, 3)
                b = it.b(1)
                if b is not None:
                    e.wait_ge(S("a_redq"), count(b))
                    if past(b - 1):
                        e.wait_ge(S("a_rq"), count(b - 1))
                    e.tensor_scalar(a["vvq"][:], a["ssq"][:], 1.0 / DH0, RMS_EPS, ALU.mult, ALU.add)\
                        .then_inc(S("a_vvq"), 1)
                b = it.b(2)
                if b is not None:
                    sums(b, 0)
                b = it.b(0)
                if b is not None:
                    e.wait_ge(S("ac_xTp"), count(b))
                    if it.b(1) is not None:
                        e.wait_ge(S("a_kT"), count(it.b(1)))
                    e.tensor_copy(a["xT"][0][:, it.m(0, 2), :], R[0][:, 1, 384:512]).then_inc(S("ac_xh"), 1)
                    e.wait_ge(S("ac_xh"), count(b))
                    e.tensor_tensor(a["xT"][1][:, it.m(0, 2), :], R[0][:, 1, 384:512],
                                    a["xT"][0][:, it.m(0, 2), :].bitcast(F32), ALU.subtract).then_inc(S("ac_xl"), 1)
                b = it.b(1)
                if b is not None:
                    e.wait_ge(S("a_kT"), count(b))
                    for odd in range(2):
                        o = slice(64 * odd, 64 * odd + 64)
                        i = e.tensor_scalar(a["kb"][o, it.m(1, 2), :, SK * odd:SK * odd + SK],
                                            R[0][o, 1, 0:4 * SK].rearrange("p (g k) -> p g k", k=SK), a["wqk"][o, 0:1], None, ALU.mult)
                    i.then_inc(S("a_kTe"), 1)
                b4 = it.b(4)
                if b4 is not None:
                    e.wait_ge(S("ac_wo"), count(b4))
                    e.tensor_tensor(rows(X, b4), rows(X, b4), R[0][:, 0:1, 0:128], ALU.add).then_inc(S("ac_add"), 1)
                b = it.b(2)
                if b is not None:
                    sums(b, 1)
                    e.wait_ge(S("ac_rcb"), count(b))
                    normalize(e, a, slice(8, 16), SK).then_inc(S("ac_nb"), 1)
                if b4 is not None:
                    e.wait_ge(S("ac_add"), count(b4))
                    apart(e)
                    e.bn_stats(st[:, 0, :], rows(X, b4)).then_inc(S("ac_bn"), 1)
                    stats_tail(e, b4, S("ac_bn"), S("ac_ag"), S("ac_ve"))
                if it.static and it.i < NB // ST:
                    if it.i >= 1:
                        split_expert_dve(e, it.i - 1)
                    if it.i < NB // ST - 1:
                        first_stats(e, it.i + 1)
                    else:
                        e.wait_ge(S("rs"), NB // ST)
            pipeline(e, NB, 4, 4, body)

        def stats_tail(e, b, bn, ag, vs, k=1, j=0, base=0):
            e.wait_ge(bn, count(b, j + 1, k, base))
            apart(e)
            e.bn_aggr(agg[:, 0, :], st[:, 0, :]).then_inc(ag, 1)
            e.wait_ge(ag, count(b, j + 1, k, base))
            e.tensor_tensor(rows(mv, b), agg[:, 0:1, :], eps[:, 0:1, :], ALU.add).then_inc(vs, 1)

        def root(e, b):
            apart(e)
            return e.tensor_tensor(rs[:, bass.ds(b, 1)], mv[:, bass.ds(b, 1), 1:2].rearrange("p a b -> p (a b)"),
                                   nhalf[:, 0:1], ALU.pow)

        def a_pool(e):
            e.wait_ge(S("ctx_in"), 16)

            def body(it):
                b = it.b(0)
                if b is not None:
                    split_context(e, a, it, b)
                b = it.b(1)
                if b is not None:
                    e.wait_ge(S("a_kr"), count(b))
                    if past(b - 1):
                        e.wait_ge(S("a_redk"), count(b - 1))
                    e.tensor_tensor(a["sqk"][0:SK, :], a["kr"][0:SK, :], a["kr"][0:SK, :], ALU.mult).then_inc(S("a_sqk"), 1)
                    e.wait_ge(S("a_vvk"), count(b))
                    e.tensor_tensor(a["rk"][0:SK, :], a["vvk"][0:SK, :], nhalf[0:SK, 0:4], ALU.pow).then_inc(S("a_rk"), 1)
                    e.wait_ge(S("a_rk"), count(b))
                    if past(b - 1):
                        e.wait_ge(S("a_kT"), count(b - 1))
                    e.tensor_tensor(a["kn"][0:SK, :, :, :],
                                    a["kr"][0:SK, :].rearrange("p (h d) -> p h d", d=DH0).unsqueeze(2).to_broadcast([SK, 4, 2, DH0]),
                                    a["rk"][0:SK, :].unsqueeze(2).unsqueeze(3).to_broadcast([SK, 4, 2, DH0]),
                                    ALU.mult).then_inc(S("a_kn"), 1)
                b = it.b(2)
                if b is not None:
                    e.wait_ge(S("ac_rca"), count(b))
                    normalize(e, a, slice(0, 8), SK).then_inc(S("ac_na"), 1)
                b = it.b(1)
                if b is not None:
                    e.wait_ge(S("a_vvq"), count(b))
                    if past(b - 2):
                        e.wait_ge(S("ac_expb"), count(b - 2))
                    e.tensor_tensor(a["rq"][:, it.m(1, 2), :], a["vvq"][:], nhalf[:, 0:16], ALU.pow).then_inc(S("a_rq"), 1)
                b = it.b(4)
                if b is not None:
                    e.wait_ge(S("ac_ve"), count(b))
                    root(e, b).then_inc(S("ac_rs"), 1)
                if it.static and it.i < NB // ST - 1:
                    first_roots(e, it.i + 1)
            pipeline(e, NB, 4, 4, body)

        def split_context(e, t, it, b):
            m = it.m(0, 4)
            if past(it.i - 4):
                e.wait_ge(S("a_kv"), count(it.i - 4))
            e.tensor_copy(t["c"][0][:, m:m + 1, :], rows(ctx_sb, b)).then_inc(S("ac_ch"), 1)
            e.wait_ge(S("ac_ch"), count(b))
            apart(e)
            e.tensor_tensor(t["c"][1][:, m:m + 1, :], rows(ctx_sb, b), t["c"][0][:, m:m + 1, :].bitcast(F32),
                            ALU.subtract).then_inc(S("ac_cl"), 1)

        def b_tensor(e):
            e.wait_ge(S("ac_add"), count(NB - 1))
            e.wait_ge(S("ac_xl"), count(NB - 1))
            e.wait_ge(S("a_kTe"), count(NB - 1))
            e.wait_ge(S("ac_expb"), count(NB - 1))
            e.wait_ge(S("split"), 6)
            t = g_

            def body(it):
                for c in range(NCH):
                    b = it.b(1)
                    if b is not None:
                        q = it.m(1, 2)
                        if c % 2 == 0:
                            if past(b - 1 if c == 0 else b):
                                e.wait_ge(S("b_wb"), count(b - 1 if c == 0 else b, NE if c == 0 else c // 2, NE))
                            e.wait_ge(S("b_wt"), count(b))
                            for j in range(GB):
                                mm = e.transpose(bank(1)[:, 128 * j:128 * j + 128],
                                                 t["wt"][:, q, j, c // 2:c // 2 + 1].to_broadcast([128, 128]), ident[:])
                            mm.then_inc(S("b_wbp"), 1)
                        xs = [x[:, q, :] for x in t["xT"]]
                        if c == 0:
                            e.wait_ge(S("b_xl"), count(b))
                        if c < 2:
                            if past(b - 1):
                                e.wait_ge(S("b_sil"), count(b - 1, NCH - 1 + c, NCH))
                            if past(b - 1):
                                e.wait_ge(S("b_g"), count(b - 1, NCH - 1 + c, NCH))
                        else:
                            e.wait_ge(S("b_sil"), count(b, c - 1, NCH))
                        passes(e, bank(3 + 2 * (c % 2)), [w[:, 128 * c:128 * c + 128] for w in w1e], xs)\
                            .then_inc(S("b_h1"), 1)
                        if c >= 2:
                            e.wait_ge(S("b_g"), count(b, c - 1, NCH))
                        passes(e, bank(4 + 2 * (c % 2)), [w[:, 128 * c:128 * c + 128] for w in w3e], xs)\
                            .then_inc(S("b_h3"), 1)
                    b, cy = (it.b(1), c - 3) if c >= 3 else (it.b(2), c - 3 + NCH)
                    if b is not None:
                        lag = 1 if c >= 3 else 2
                        if cy == 0:
                            if past(b - 2):
                                e.wait_ge(S("b_yT"), count(b - 2))
                        e.wait_ge(S("b_gl"), count(b, cy + 1, NCH))
                        y = bank((2, 7)[it.m(lag, 2)])
                        for n, (w, x) in enumerate(((1, 0), (0, 1), (0, 0))):
                            mm = e.matmul(y, w2e[w][:, cy, :], t["gs"][x][:, cy % 4, :],
                                          start=(cy == 0 and n == 0), stop=(cy == NCH - 1 and n == 2))
                        if cy == NCH - 1:
                            mm.then_inc(S("b_y"), 1)
                    b = it.b(0)
                    if b is not None and c == 2:
                        if past(min(it.i - 3, NG - 1) if it.static else it.i - 3):
                            e.wait_ge(S("b_add"), count(min(it.i - 3, NG - 1) if it.static else it.i - 3))
                        if past(b - 1):
                            e.wait_ge(S("b_lm"), count(b - 1))
                        e.wait_ge(S("b_xn"), count(b, 2, 2))
                        for j in range(GB):
                            mm = e.transpose(bank(0)[:, 128 * j:128 * j + 128], t["xn"][:, j, :], ident[:])
                        mm.then_inc(S("b_xTp"), 1)
                    if b is not None and c == 5:
                        e.wait_ge(S("b_xl"), count(b))
                        for j in range(GB):
                            mm = passes(e, bank(0)[:, NE * j:NE * j + NE],
                                        [x[:, it.m(0, 2), 128 * j:128 * j + 128] for x in t["xT"]], [w[:] for w in wgs])
                        mm.then_inc(S("b_lg"), 1)
                    b = it.b(2)
                    if b is not None and c == 12:
                        if it.b(0) is not None:
                            e.wait_ge(S("b_lm"), it.i + 1)
                        elif it.static:
                            if past(b - 1):
                                e.wait_ge(S("b_add"), count(b - 1))
                            e.wait_ge(S("b_lm"), count(NG - 1))
                        e.wait_ge(S("b_yT"), count(b))
                        for j in range(GB):
                            mm = e.transpose(bank(0)[:, 128 * j:128 * j + 128], t["yT"][:, 128 * j:128 * j + 128], ident[:])
                        mm.then_inc(S("b_yt"), 1)
            pipeline(e, NG, 4, 2, body)

        def b_scalar(e):
            t = g_
            e.wait_ge(S("ac_add"), count(NB - 1))

            def body(it):
                for c in range(NCH):
                    b = it.b(1)
                    if b is not None:
                        if c % 2 == 0:
                            k = c // 2
                            e.wait_ge(S("b_wbp"), count(b, k + 1, NE))
                            if k >= 2:
                                e.wait_ge(S("b_sp"), count(b, 2 * k - 2, NCH))
                            else:
                                if past(b - 1):
                                    e.wait_ge(S("b_sp"), count(b - 1, NCH + 2 * k - 2, NCH))
                            e.activation(t["wb"][:, k % 2, :], bank(1), ACT.Copy).then_inc(S("b_wb"), 1)
                        e.wait_ge(S("b_h1"), count(b, c + 1, NCH))
                        if c >= 2:
                            e.wait_ge(S("b_sp"), count(b, c - 1, NCH))
                        else:
                            if past(b - 1):
                                e.wait_ge(S("b_sp"), count(b - 1, NCH + c - 1, NCH))
                        e.activation(t["s"][:, c % 2, :], bank(3 + 2 * (c % 2)), ACT.Silu).then_inc(S("b_sil"), 1)
                    b, cg = (it.b(1), c - 2) if c >= 2 else (it.b(2), c - 2 + NCH)
                    if b is not None:
                        e.wait_ge(S("b_g"), count(b, cg + 1, NCH))
                        e.activation(t["gs"][0][:, cg % 4, :], t["g"][:, cg % 4, :], ACT.Copy).then_inc(S("b_gh"), 1)
                    b = it.b(2)
                    if b is not None and c == 4:
                        e.wait_ge(S("b_y"), count(b))
                        if past(b - 1):
                            e.wait_ge(S("b_yt"), count(b - 1))
                        e.activation(t["yT"][:], bank((2, 7)[it.m(2, 2)]), ACT.Copy).then_inc(S("b_yT"), 1)
                    b = it.b(0)
                    if b is not None and c == 3:
                        e.wait_ge(S("b_xTp"), count(b))
                        e.activation(t["xT"][0][:, it.m(0, 2), :], bank(0), ACT.Copy).then_inc(S("b_xh"), 1)
                    if b is not None and c == 7:
                        e.wait_ge(S("b_lm"), count(b))
                        e.activation(t["Re"][:], t["Rl"][:], ACT.Exp).then_inc(S("b_ex"), 1)
            pipeline(e, NG, 4, 2, body)

        def b_vector(e):
            t = g_
            e.wait_ge(S("ac_rs"), count(NB - 1))

            bc = lambda x: t[x][:].unsqueeze(2).to_broadcast([128, GB, NE])
            lg = bank(0)[:, 0:GB * NE].rearrange("p (a b) -> p a b", b=NE)
            NR = 21
            router_from = {6: 0, 7: 2, 8: 2, 9: 5, 10: 8, 11: 11, 12: 14, 13: 17, 14: 19, 15: NR, 16: NR}

            def router(it, b, n):
                if n == 0:
                    e.wait_ge(S("b_lg"), count(b))
                    e.tensor_reduce(t["rm"][:], lg, AX.X, ALU.max, negate=True).then_inc(S("b_m0"), 1)
                if n == 1:
                    e.wait_ge(S("b_m0"), count(b))
                    e.tensor_tensor(t["Rl"][:], lg, bc("rm"), ALU.add).then_inc(S("b_lm"), 1)
                if n == 2:
                    e.wait_ge(S("b_ex"), count(b))
                    e.tensor_reduce(t["rs"][:], t["Re"][:], AX.X, ALU.add).then_inc(S("b_ro"), 1)
                if n == 3:
                    e.wait_ge(S("b_ro"), count(b, 1, NR - 3))
                    e.reciprocal(t["rrc"][:], t["rs"][:]).then_inc(S("b_ro"), 1)
                if n == 4:
                    e.wait_ge(S("b_ro"), count(b, 2, NR - 3))
                    e.tensor_tensor(t["Rp"][:], t["Re"][:], bc("rrc"), ALU.mult).then_inc(S("b_ro"), 1)
                if n == 5:
                    e.wait_ge(S("b_ro"), count(b, 3, NR - 3))
                    e.tensor_reduce(t["rm1"][:], t["Rp"][:], AX.X, ALU.max).then_inc(S("b_ro"), 1)
                if n == 6:
                    e.wait_ge(S("b_ro"), count(b, 4, NR - 3))
                    e.tensor_tensor(t["Rq"][:], t["Rp"][:], bc("rm1"), ALU.is_equal).then_inc(S("b_ro"), 1)
                if n == 7:
                    e.wait_ge(S("b_ro"), count(b, 5, NR - 3))
                    e.tensor_tensor(t["Rk"][:], t["Rq"][:], keyi[:], ALU.mult).then_inc(S("b_ro"), 1)
                if n == 8:
                    e.wait_ge(S("b_ro"), count(b, 6, NR - 3))
                    e.tensor_reduce(t["rk1"][:], t["Rk"][:], AX.X, ALU.max).then_inc(S("b_ro"), 1)
                if n == 9:
                    e.wait_ge(S("b_ro"), count(b, 7, NR - 3))
                    e.tensor_tensor(t["Ro"][:], t["Rk"][:], bc("rk1"), ALU.is_equal).then_inc(S("b_ro"), 1)
                if n == 10:
                    e.wait_ge(S("b_ro"), count(b, 8, NR - 3))
                    e.scalar_tensor_tensor(out=t["Rq2"][:], in0=t["Ro"][:], scalar=-2.0, in1=t["Rp"][:],
                                       op0=ALU.mult, op1=ALU.add).then_inc(S("b_ro"), 1)
                if n == 11:
                    e.wait_ge(S("b_ro"), count(b, 9, NR - 3))
                    e.tensor_reduce(t["rm2"][:], t["Rq2"][:], AX.X, ALU.max).then_inc(S("b_ro"), 1)
                if n == 12:
                    e.wait_ge(S("b_ro"), count(b, 10, NR - 3))
                    e.tensor_tensor(t["Re2"][:], t["Rq2"][:], bc("rm2"), ALU.is_equal).then_inc(S("b_ro"), 1)
                if n == 13:
                    e.wait_ge(S("b_ro"), count(b, 11, NR - 3))
                    e.tensor_tensor(t["Rk2"][:], t["Re2"][:], keyi[:], ALU.mult).then_inc(S("b_ro"), 1)
                if n == 14:
                    e.wait_ge(S("b_ro"), count(b, 12, NR - 3))
                    e.tensor_reduce(t["rk2"][:], t["Rk2"][:], AX.X, ALU.max).then_inc(S("b_ro"), 1)
                if n == 15:
                    e.wait_ge(S("b_ro"), count(b, 13, NR - 3))
                    e.tensor_tensor(t["Ro2"][:], t["Rk2"][:], bc("rk2"), ALU.is_equal).then_inc(S("b_ro"), 1)
                if n == 16:
                    e.wait_ge(S("b_ro"), count(b, 14, NR - 3))
                    e.tensor_tensor(t["Rt"][:], t["Ro"][:], t["Ro2"][:], ALU.add).then_inc(S("b_ro"), 1)
                if n == 17:
                    e.wait_ge(S("b_ro"), count(b, 15, NR - 3))
                    e.tensor_tensor(t["Rk"][:], t["Rt"][:], t["Rp"][:], ALU.mult).then_inc(S("b_ro"), 1)
                if n == 18:
                    e.wait_ge(S("b_ro"), count(b, 16, NR - 3))
                    e.tensor_tensor(t["rdn"][:], t["rm1"][:], t["rm2"][:], ALU.add).then_inc(S("b_ro"), 1)
                if n == 19:
                    e.wait_ge(S("b_ro"), count(b, 17, NR - 3))
                    e.reciprocal(t["rrd"][:], t["rdn"][:]).then_inc(S("b_ro"), 1)
                if n == 20:
                    e.wait_ge(S("b_ro"), count(b, 18, NR - 3))
                    e.tensor_tensor(t["wt"][:, it.m(0, 2), :, :], t["Rk"][:], bc("rrd"), ALU.mult).then_inc(S("b_wt"), 1)

            def body(it):
                for c in range(NCH):
                    b = it.b(0)
                    if b is not None and c < 2:
                        for j in (2 * c, 2 * c + 1):
                            i = e.tensor_scalar(t["xn"][:, j:j + 1, :], rows(X, b * GB + j),
                                                mv[:, bass.ds(b * GB + j, 1), 0:1].rearrange("p a b -> p (a b)"),
                                                rs[:, bass.ds(b * GB + j, 1)], ALU.subtract, ALU.mult)
                        i.then_inc(S("b_xn"), 1)
                    if b is not None and c == 3:
                        e.wait_ge(S("b_xh"), count(b))
                        e.tensor_tensor(t["xT"][1][:, it.m(0, 2), :], bank(0), t["xT"][0][:, it.m(0, 2), :].bitcast(F32),
                                        ALU.subtract).then_inc(S("b_xl"), 1)
                    b, cg = (it.b(1), c - 1) if c >= 1 else (it.b(2), NCH - 1)
                    if b is not None:
                        e.wait_ge(S("b_h3"), count(b, cg + 1, NCH))
                        e.wait_ge(S("b_sp"), count(b, cg + 1, NCH))
                        if cg >= 4:
                            e.wait_ge(S("b_gl"), count(b, cg - 3, NCH))
                        else:
                            if past(b - 1):
                                e.wait_ge(S("b_gl"), count(b - 1, NCH + cg - 3, NCH))
                        e.tensor_tensor(t["g"][:, cg % 4, :], bank(4 + 2 * (cg % 2)), t["sp"][:, cg % 2, :], ALU.mult)\
                            .then_inc(S("b_g"), 1)
                    b, cg = (it.b(1), c - 2) if c >= 2 else (it.b(2), c - 2 + NCH)
                    if b is not None:
                        e.wait_ge(S("b_gh"), count(b, cg + 1, NCH))
                        e.tensor_tensor(t["gs"][1][:, cg % 4, :], t["g"][:, cg % 4, :],
                                        t["gs"][0][:, cg % 4, :].bitcast(F32), ALU.subtract).then_inc(S("b_gl"), 1)
                    b = it.b(0)
                    if b is not None and c >= 6:
                        for n in range(router_from[c], router_from[c + 1]):
                            router(it, b, n)
                    b = it.b(2)
                    if b is not None and c == 13:
                        e.wait_ge(S("b_yt"), count(b))
                        e.tensor_tensor(X[:, bass.ds(b * GB, GB), :], X[:, bass.ds(b * GB, GB), :],
                                        bank(0).rearrange("p (a b) -> p a b", b=128), ALU.add).then_inc(S("b_add"), 1)
                    if b is not None and c == 14:
                        e.wait_ge(S("b_add"), count(b))
                        apart(e)
                        for j in range(GB):
                            e.bn_stats(st[:, j, :], rows(X, b * GB + j)).then_inc(S("b_bn"), 1)
                    if b is not None and c == 15:
                        e.wait_ge(S("b_bn"), count(b, GB, GB))
                        apart(e)
                        for j in range(GB):
                            e.bn_aggr(agg[:, j, :], st[:, j, :]).then_inc(S("b_ag"), 1)
                        e.wait_ge(S("b_ag"), count(b, GB, GB))
                        e.tensor_tensor(mv[:, bass.ds(b * GB, GB), :], agg[:, 0:GB, :], eps[:, 0:GB, :], ALU.add).then_inc(S("b_ve"), 1)
            pipeline(e, NG, 4, 2, body)

        def b_pool(e):
            t = g_
            e.wait_ge(S("ac_add"), count(NB - 1))

            def body(it):
                b = it.b(1)
                if b is not None:
                    for c in range(NCH):
                        e.wait_ge(S("b_sil"), count(b, c + 1, NCH))
                        if c % 2 == 0:
                            e.wait_ge(S("b_wb"), count(b, c // 2 + 1, NE))
                        if c >= 2:
                            e.wait_ge(S("b_g"), count(b, c - 1, NCH))
                        else:
                            if past(b - 1):
                                e.wait_ge(S("b_g"), count(b - 1, NCH + c - 1, NCH))
                        e.tensor_tensor(t["sp"][:, c % 2, :], t["s"][:, c % 2, :], t["wb"][:, c // 2 % 2, :], ALU.mult)\
                            .then_inc(S("b_sp"), 1)
                b = it.b(2)
                if b is not None:
                    e.wait_ge(S("b_ve"), count(b))
                    apart(e)
                    e.tensor_tensor(rs[:, bass.ds(b * GB, GB)], mv[:, bass.ds(b * GB, GB), 1:2].rearrange("p a b -> p (a b)"),
                                    nhalf[:, 0:GB], ALU.pow)\
                        .then_inc(S("b_rs"), 1)
            pipeline(e, NG, 4, 2, body)


        d_weights = ((0, slice(0, 1536), wqkv[0], 64), (1, slice(0, 1536), wqkv[1], 48),
                     (0, slice(0, 2 * HID), w1l[0], 80), (0, slice(2 * HID, 4 * HID), w1l[1], 80))

        def split_layers_act(e, n):
            half, cols, (hi, _), value = d_weights[n]
            e.wait_ge(S(f"stage{half}_in"), value)
            e.activation(hi[:], stage[:, half, cols], ACT.Copy).then_inc(S("high"), 1)

        def split_layers_dve(e, n):
            half, cols, (hi, lo), _ = d_weights[n]
            e.wait_ge(S("high"), 11 + n + 1)
            e.tensor_tensor(lo[:], stage[:, half, cols], hi[:].bitcast(F32), ALU.subtract).then_inc(S("split"), 1)

        def c_tensor(e):
            t = c_
            e.wait_ge(S("b_add"), count(NG - 1))
            e.wait_ge(S("c_const"), count(0))

            def body(it):
                for half, slot in ((0, 2), (1, 3)):
                    b = it.b(3)
                    if b is not None:
                        if half == 0:
                            if it.seen(4):
                                e.wait_ge(S("ac_pTb"), it.upto(4, NB))
                        else:
                            if it.seen(3):
                                e.wait_ge(S("ac_pTa"), it.upto(3, NB))
                        e.wait_ge(S(("ac_na", "ac_nb")[half]), count(b, base=NB))
                        for k in range(8):
                            mm = e.transpose(R[1][0:SK, k // 4, 128 * (k % 4):128 * (k % 4) + 128],
                                             t["p"][:, it.m(3, 2), 8 * half + k, :], ident[:])
                        mm.then_inc(S(("ac_PTa", "ac_PTb")[half]), 1)
                    b = it.b(2)
                    if b is not None:
                        e.wait_ge(S("c_ql"), count(b))
                        e.wait_ge(S("c_kb"), count(b))
                        if half == 0:
                            if it.seen(3):
                                e.wait_ge(S("ac_expa"), it.upto(3, NB))
                        else:
                            if it.seen(3):
                                e.wait_ge(S("ac_expb"), it.upto(3, NB))
                        for k in range(2):
                            o = 32 * (2 * half + k)
                            mm = passes(e, R[slot][:, k, 0:4 * SK], [q[o:o + 32, it.m(2, 2), :] for q in t["qT"]],
                                        [kb[o:o + 32, it.m(2, 2), :, :].rearrange("p a b -> p (a b)") for kb in t["kb"]])
                        mm.then_inc(S(("ac_Sa", "ac_Sb")[half]), 1)
                b = it.b(1)
                if b is not None:
                    if it.seen(2):
                        e.wait_ge(S("c_kb"), it.upto(2))
                    e.wait_ge(S("ac_xh"), count(b, base=NB))
                    e.wait_ge(S("ac_ch"), count(b, base=NB))
                    c = t["c"][:, it.m(1, 4), :]
                    e.matmul(R[0][0:SK, 0, 256:384], c, l1[:, 2, :], start=True, stop=True)
                    e.matmul(R[0][:, 0, 0:128], l1[:, 0, :], t["xT"][:, it.m(1, 2), :], start=True, stop=True)
                    e.matmul(R[0][:, 0, 128:128 + SK], l1[:, 1, :], c, start=True, stop=True).then_inc(S("c_proj"), 1)
                if it.b(3) is not None or it.b(0) is not None or it.b(4) is not None:
                    if it.seen(4):
                        e.wait_ge(S("ac_oTe"), it.upto(4, NB))
                    if it.seen(1):
                        e.wait_ge(S("ac_xh"), it.upto(1, NB))
                    if it.seen(5):
                        e.wait_ge(S("ac_add"), it.upto(5, NB))
                b = it.b(3)
                if b is not None:
                    e.wait_ge(S("ac_pTb"), count(b, base=NB))
                    for j in range(4):
                        for g in range(4):
                            mm = e.matmul(R[0][32 * g:32 * g + 32, 1, 0:128],
                                          t["vz"][0:SK, it.m(3, 4), g, 32 * j:32 * j + 32], t["pT"][0:SK, 4 * g + j, :],
                                          start=(j == 0), stop=(j == 3))
                    mm.then_inc(S("ac_PV"), 1)
                b = it.b(0)
                if b is not None:
                    e.wait_ge(S("ac_xn"), count(b, base=NB))
                    e.transpose(R[0][:, 1, 128:256], t["xn"][:, it.m(0, 2), :], ident[:]).then_inc(S("ac_xTp"), 1)
                b = it.b(4)
                if b is not None:
                    e.wait_ge(S("ac_oTe"), count(b, base=NB))
                    e.matmul(R[0][:, 1, 256:384], t["oT"][:, it.m(4, 2), :], l1[:, 3, :], start=True, stop=True)\
                        .then_inc(S("ac_wo"), 1)
            pipeline(e, NB, 4, 4, body)

        def c_scalar(e):
            t = c_
            e.wait_ge(S("b_add"), count(NG - 1))
            e.wait_ge(S("c_const"), count(0))

            def body(it):
                b = it.b(3)
                if b is not None:
                    for half in range(2):
                        e.wait_ge(S(("ac_PTa", "ac_PTb")[half]), count(b, base=NB))
                        e.activation(t["pT"][0:SK, 8 * half:8 * half + 8, :].rearrange("p (a c) t -> p a (c t)", a=2),
                                     R[1][0:SK, :, :], ACT.Copy).then_inc(S(("ac_pTa", "ac_pTb")[half]), 1)
                b = it.b(2)
                if b is not None:
                    p = {"p": t["p"][:, it.m(2, 2), :, :], "nm": t["nm"]}
                    e.wait_ge(S("ac_mxa"), count(b, base=NB))
                    exponentials(e, p, 2, 0, 4, SK, S("ac_expa"))
                b = it.b(1)
                if b is not None:
                    e.wait_ge(S("c_proj"), count(b))
                    e.activation(t["qT"][0][:, it.m(1, 2), :], R[0][:, 0, 0:128], ACT.Copy, scale=float(DH1) ** -0.5)\
                        .then_inc(S("c_qT"), 1)
                    e.activation(t["kh"][:], R[0][:, 0, 128:128 + SK], ACT.Copy).then_inc(S("c_kh"), 1)
                    vz = t["vz"][0:SK, it.m(1, 4), :, :].rearrange("p g (j k) -> p g j k", k=32 + DH1)[:, :, :, 0:DH1]
                    e.activation(vz, R[0][0:SK, 0, 256:384].rearrange("p (g j k) -> p g j k", g=4, k=DH1), ACT.Copy)\
                        .then_inc(S("ac_v"), 1)
                b = it.b(2)
                if b is not None:
                    e.wait_ge(S("ac_mxb"), count(b, base=NB))
                    exponentials(e, p, 3, 1, 4, SK, S("ac_expb"))
                if it.static and 0 <= it.i <= 3:
                    split_layers_act(e, it.i)
            pipeline(e, NB, 4, 4, body)

        def c_vector(e):
            t = c_
            e.wait_ge(S("b_rs"), count(NG - 1))
            e.memset(t["vz"][:], 0.0).then_inc(S("c_const"), 1)

            def largest(b, half, slot):
                s = R[slot][:, :, 0:4 * SK].rearrange("p a (j k) -> p a j k", k=SK)
                e.wait_ge(S(("ac_Sa", "ac_Sb")[half]), count(b, base=NB))
                apart(e)
                for k in range(2):
                    i = e.copy_predicated(s[:, k, :, :], maskz[:].unsqueeze(1).to_broadcast([128, 4, SK]),
                                          negt[:].unsqueeze(1).to_broadcast([128, 4, SK]))
                i.then_inc(S(("c_ma", "c_mb")[half]), 1)
                e.wait_ge(S(("c_ma", "c_mb")[half]), count(b))
                e.tensor_reduce(t["nm"][:, 8 * half:8 * half + 8], s, AX.X, ALU.max, negate=True)\
                    .then_inc(S(("ac_mxa", "ac_mxb")[half]), 1)

            def sums(b, it, half):
                h = slice(8 * half, 8 * half + 8)
                e.wait_ge(S(("ac_expa", "ac_expb")[half]), count(b, base=NB))
                if past(b - 1):
                    e.wait_ge(S(("ac_na", "ac_nb")[half]), count(b - 1, base=NB))
                e.tensor_reduce(t["sum"][:, h], t["p"][:, it.m(2, 2), h, :], AX.X, ALU.add).then_inc(S(("ac_suma", "ac_sumb")[half]), 1)
                e.wait_ge(S(("ac_suma", "ac_sumb")[half]), count(b, base=NB))
                e.reciprocal(t["rc"][:, h], t["sum"][:, h]).then_inc(S(("ac_rca", "ac_rcb")[half]), 1)

            def body(it):
                b = it.b(0)
                if b is not None:
                    layernorm(e, X, t["xn"], b, it.m(0, 2)).then_inc(S("ac_xn"), 1)
                b = it.b(2)
                if b is not None:
                    largest(b, 0, 2)
                    largest(b, 1, 3)
                b = it.b(2)
                if b is not None:
                    sums(b, it, 0)
                b = it.b(1)
                if b is not None:
                    e.wait_ge(S("ac_v"), count(b, base=NB))
                    e.scalar_tensor_tensor(out=t["qT"][1][:, it.m(1, 2), :], in0=R[0][:, 0, 0:128], scalar=float(DH1) ** -0.5,
                                           in1=t["qT"][0][:, it.m(1, 2), :].bitcast(F32), op0=ALU.mult, op1=ALU.subtract)\
                        .then_inc(S("c_ql"), 1)
                    e.tensor_tensor(t["kl"][:], R[0][:, 0, 128:128 + SK], t["kh"][:].bitcast(F32), ALU.subtract)\
                        .then_inc(S("c_kl"), 1)
                    blocks = head[:].unsqueeze(2).to_broadcast([128, 4, SK])
                    e.tensor_tensor(t["kb"][0][:, it.m(1, 2), :, :], t["kh"][:].bitcast(F32).unsqueeze(1).to_broadcast([128, 4, SK]),
                                    blocks, ALU.mult).then_inc(S("c_kbh"), 1)
                    e.wait_ge(S("c_kl"), count(b))
                    e.tensor_tensor(t["kb"][1][:, it.m(1, 2), :, :], t["kl"][:].unsqueeze(1).to_broadcast([128, 4, SK]),
                                    blocks, ALU.mult).then_inc(S("c_kb"), 1)
                b3, b4, b0 = it.b(3), it.b(4), it.b(0)
                if b4 is not None:
                    e.wait_ge(S("ac_wo"), count(b4, base=NB))
                elif b0 is not None:
                    e.wait_ge(S("ac_xTp"), count(b0, base=NB))
                elif b3 is not None:
                    e.wait_ge(S("ac_PV"), count(b3, base=NB))
                if b3 is not None:
                    e.wait_ge(S("ac_PV"), count(b3, base=NB))
                    e.tensor_copy(t["oT"][:, it.m(3, 2), :], R[0][:, 1, 0:128]).then_inc(S("ac_oTe"), 1)
                if b0 is not None:
                    e.wait_ge(S("ac_xTp"), count(b0, base=NB))
                    e.tensor_copy(t["xT"][:, it.m(0, 2), :], R[0][:, 1, 128:256]).then_inc(S("ac_xh"), 1)
                if b4 is not None:
                    e.tensor_tensor(rows(X, b4), rows(X, b4), R[0][:, 1:2, 256:384], ALU.add).then_inc(S("ac_add"), 1)
                b = it.b(2)
                if b is not None:
                    sums(b, it, 1)
                    e.wait_ge(S("ac_rcb"), count(b, base=NB))
                    normalize(e, {"p": t["p"][:, it.m(2, 2), :, :], "rc": t["rc"]}, slice(8, 16), SK).then_inc(S("ac_nb"), 1)
                if b4 is not None:
                    e.wait_ge(S("ac_add"), count(b4, base=NB))
                    apart(e)
                    e.bn_stats(st[:, 0, :], rows(X, b4)).then_inc(S("ac_bn"), 1)
                    stats_tail(e, b4, S("ac_bn"), S("ac_ag"), S("ac_ve"), base=NB)
                if it.static and 0 <= it.i <= 3:
                    split_layers_dve(e, it.i)
                if it.static and it.i in (1, 2):
                    l = it.i - 1
                    e.tensor_tensor(T1[:, l, :, :], rot[:, 0, :, :], qks[:, l, 0, :, :], ALU.mult).then_inc(S("d_con"), 1)
                    e.tensor_tensor(T2[:, l, :, :], rot[:, 1, :, :], qks[:, l, 1, :, :], ALU.mult).then_inc(S("d_con"), 1)
            pipeline(e, NB, 4, 4, body)

        def c_pool(e):
            e.wait_ge(S("b_add"), count(NG - 1))

            def body(it):
                b = it.b(0)
                if b is not None:
                    m = it.m(0, 4)
                    if past(it.i - 4):
                        e.wait_ge(S("c_proj"), count(it.i - 4))
                    apart(e)
                    e.tensor_copy(c_["c"][:, m:m + 1, :], rows(ctx_sb, b)).then_inc(S("ac_ch"), 1)
                b = it.b(2)
                if b is not None:
                    e.wait_ge(S("ac_rca"), count(b, base=NB))
                    normalize(e, {"p": c_["p"][:, it.m(2, 2), :, :], "rc": c_["rc"]}, slice(0, 8), SK).then_inc(S("ac_na"), 1)
                b = it.b(4)
                if b is not None:
                    e.wait_ge(S("ac_ve"), count(b, base=NB))
                    root(e, b).then_inc(S("ac_rs"), 1)
            pipeline(e, NB, 4, 4, body)

        def load_d(e):
            e.wait_ge(S("b_add"), count(NG - 1))
            e.dma_start(stage[:, 0, 0:1536], wqkv_in[:, 0:1536]).then_inc(S("stage0_in"), 16)
            e.dma_start(stage[:, 1, 0:1536], wqkv_in[:, 1536:3072]).then_inc(S("stage1_in"), 16)
            e.wait_ge(S("split"), 7)
            e.dma_start(stage[:, 0, 0:4 * HID], w1l_in).then_inc(S("stage0_in"), 16)

        def d_start(e):
            e.memset(H2[0:1, :, 64:128], 0.0).then_inc(S("d_con"), 1)
            e.memset(d["v1"][:], 1.0).then_inc(S("d_con"), 1)
            for x in d["hT"]:
                e.memset(x[64:128, :, 0:1].bitcast(F32), 0.0).then_inc(S("d_con"), 1)
            e.wait_ge(S("d_con"), 8)


        def da_start(e, l):
            if l == 0:
                e.wait_ge(S("ac_add"), count(NB - 1, base=NB))
                e.wait_ge(S("ac_rs"), count(NB - 1, base=NB))
            else:
                e.wait_ge(S("f_add"), count(NG - 1))
                e.wait_ge(S("f_lo"), count(NG - 1))

        def da_tensor(e, l):
            t, B = d, NB * l
            da_start(e, l)
            e.wait_ge(S("split"), 10)
            e.wait_ge(S("d_con"), 8)

            def body(it):
                b = it.b(1)
                if b is not None:
                    x = [x[:, it.m(1, 2), :] for x in t["hT"]]
                    if past(b - 1):
                        e.wait_ge(S("d_B"), count(b - 1, base=B))
                    if past(b - 1):
                        e.wait_ge(S("d_sq"), count(b - 1, base=B))
                    e.wait_ge(S("d_hl"), count(b, base=B))
                    for h in range(2):
                        mm = passes(e, R[0][:, h, :], x, [w[:, 512 * h:512 * h + 512] for w in wqkv[l]])
                    mm.then_inc(S("d_qkp"), 1)
                    if it.seen(1):
                        e.wait_ge(S("d_hl"), it.upto(1, B))
                    if it.seen(5):
                        e.wait_ge(S("d_add"), it.upto(5, B))
                    passes(e, R[1][:, 0, :], x, [w[:, 1024:1536] for w in wqkv[l]]).then_inc(S("d_vp"), 1)
                b = it.b(2)
                if b is not None:
                    if it.seen(3):
                        e.wait_ge(S("d_exp"), it.upto(3, B))
                    e.wait_ge(S("d_qkn"), count(b, base=B))
                    for c in range(8):
                        mm = e.transpose(R[2][:, c // 4, 128 * (c % 4):128 * (c % 4) + 128],
                                         t["A"][:, it.m(2, 2), 128 * c:128 * c + 128], ident[:])
                    mm.then_inc(S("d_qkTp"), 1)
                b = it.b(3)
                if b is not None:
                    if it.seen(4):
                        e.wait_ge(S("d_on"), it.upto(4, B))
                    e.wait_ge(S("d_exp"), count(b, base=B))
                    for c in range(8):
                        mm = e.transpose(R[3][:, c // 4, 128 * (c % 4):128 * (c % 4) + 128], t["p"][:, it.m(3, 2), c, :], ident[:])
                    mm.then_inc(S("d_PT"), 1)
                b = it.b(4)
                if b is not None:
                    if it.seen(5):
                        e.wait_ge(S("d_oTe"), it.upto(5, B))
                    e.wait_ge(S("d_on"), count(b, base=B))
                    for c in range(4):
                        mm = e.transpose(R[1][:, 1, 128 * c:128 * c + 128], t["on"][:, it.m(4, 2), 128 * c:128 * c + 128], ident[:])
                    mm.then_inc(S("d_OT"), 1)
                b = it.b(2)
                if b is not None:
                    e.wait_ge(S("d_qkT"), count(b, base=B))
                    for k in range(2):
                        e.matmul(R[2][:, k, :], identb[:], bandb[:].rearrange("p a b -> p (a b)"), start=True, stop=False)
                    for h in range(HL):
                        o = DL * (h % 2)
                        mm = e.matmul(R[2][:, h % 2, 128 * (h // 2):128 * (h // 2) + 128], t["qT"][o:o + DL, h // 2, :],
                                      t["qT"][o:o + DL, 4 + h // 2, :], start=False, stop=(h >= HL - 2))
                    mm.then_inc(S("d_S"), 1)
                if it.b(4) is not None or it.b(0) is not None:
                    if it.seen(1):
                        e.wait_ge(S("d_v"), it.upto(1, B))
                    if it.static:
                        if it.seen(1):
                            e.wait_ge(S("d_hl"), it.upto(1, B))
                        if it.seen(5):
                            e.wait_ge(S("d_add"), it.upto(5, B))
                b = it.b(0)
                if b is not None:
                    e.wait_ge(S("d_zn"), count(b, base=B))
                    e.transpose(R[1][:, 0, 128:256], t["z"][:, it.m(0, 2), :], ident[:]).then_inc(S("d_zT"), 1)
                b = it.b(4)
                if b is not None:
                    e.wait_ge(S("d_oTe"), count(b, base=B))
                    for c in range(4):
                        mm = e.matmul(R[1][:, 0, 0:128], t["oT"][:, c, :], wol[:, l, c, :], start=(c == 0), stop=(c == 3))
                    mm.then_inc(S("d_wo"), 1)
                b = it.b(3)
                if b is not None:
                    e.wait_ge(S("d_pT"), count(b, base=B))
                    for h in range(HL):
                        mm = e.matmul(R[3][:, h // 4, 65 * (h % 4):65 * (h % 4) + 65], t["pT"][:, 4 * (h % 2) + h // 2, :],
                                      t["v1"][:, it.m(3, 4), h, :], start=True, stop=True)
                    mm.then_inc(S("d_PV"), 1)
            pipeline(e, NB, 8, 4, body)

        def da_scalar(e, l):
            t, B = d, NB * l
            da_start(e, l)

            def body(it):
                b = it.b(1)
                if b is not None:
                    e.wait_ge(S("d_qkp"), count(b, base=B))
                    if past(b - 1):
                        e.wait_ge(S("d_red"), count(b - 1, base=B))
                    e.activation(t["sq"][:].rearrange("p (a b) -> p a b", a=2), R[0][:], ACT.Square).then_inc(S("d_sq"), 1)
                b = it.b(2)
                if b is not None:
                    e.wait_ge(S("d_qkTp"), count(b, base=B))
                    e.activation(t["qT"][:].rearrange("p (a c) t -> p a (c t)", a=2), R[2][:], ACT.Copy).then_inc(S("d_qkT"), 1)
                b = it.b(1)
                if b is not None:
                    e.wait_ge(S("d_vp"), count(b, base=B))
                    e.activation(t["v1"][:, it.m(1, 4), :, 0:DL], R[1][:, 0, :].rearrange("p (a b) -> p a b", b=DL), ACT.Copy)\
                        .then_inc(S("d_v"), 1)
                b = it.b(3)
                if b is not None:
                    e.wait_ge(S("d_PT"), count(b, base=B))
                    e.activation(t["pT"][:].rearrange("p (a c) t -> p a (c t)", a=2), R[3][:], ACT.Copy).then_inc(S("d_pT"), 1)
                b = it.b(4)
                if b is not None:
                    e.wait_ge(S("d_OT"), count(b, base=B))
                    e.activation(t["oT"][:].rearrange("p c t -> p (c t)"), R[1][:, 1, :], ACT.Copy).then_inc(S("d_oTe"), 1)
                b = it.b(0)
                if b is not None:
                    e.wait_ge(S("d_zT"), count(b, base=B))
                    if it.b(4) is not None:
                        e.wait_ge(S("d_wo"), count(it.b(4), base=B))
                    m = it.m(0, 2)
                    e.activation(t["hT"][0][0:64, m, :], R[1][0:64, 0, 128:256], ACT.Copy)
                    e.activation(t["hT"][0][64:128, m, 1:128], R[1][64:128, 0, 128:255], ACT.Copy).then_inc(S("d_hh"), 1)
                b = it.b(2)
                if b is not None:
                    e.wait_ge(S("d_nm"), count(b, base=B))
                    exponentials(e, {"p": t["p"][:, it.m(2, 2), :, :], "nm": t["nm"]}, 2, 0, 4, 128, S("d_exp"),
                                 t["r"][:, it.m(2, 2), :], lambda k: 2 * (k % 4) + k // 4)
            pipeline(e, NB, 8, 4, body)

        def da_vector(e, l):
            t, B = d, NB * l
            da_start(e, l)

            def body(it):
                b = it.b(4)
                if b is not None:
                    o = R[3][:, :, 0:260].rearrange("p a (j k) -> p a j k", k=65)
                    rc = t["rc"][:].rearrange("p (a j) -> p a j", a=2)
                    e.wait_ge(S("d_PV"), count(b, base=B))
                    e.reciprocal(rc, o[:, :, :, 64]).then_inc(S("d_rc"), 1)
                    e.wait_ge(S("d_rc"), count(b, base=B))
                    e.tensor_tensor(t["on"][:, it.m(4, 2), :].rearrange("p (a j k) -> p a j k", a=2, j=4), o[:, :, :, 0:64],
                                    rc.unsqueeze(3).to_broadcast([128, 2, 4, 64]), ALU.mult).then_inc(S("d_on"), 1)
                b = it.b(0)
                if b is not None:
                    if l == 0:
                        layernorm(e, X, t["z"], b, it.m(0, 2)).then_inc(S("d_zn"), 1)
                        e.tensor_scalar(rows(Z, b), rows(X, b), mv[:, bass.ds(b, 1), 0:1].rearrange("p a b -> p (a b)"),
                                        rs[:, bass.ds(b, 1)], ALU.subtract, ALU.mult)
                    else:
                        e.tensor_copy(t["z"][:, it.m(0, 2):it.m(0, 2) + 1, :], rows(Z, b)).then_inc(S("d_zn"), 1)
                b = it.b(1)
                if b is not None:
                    p = it.m(1, 2)
                    e.wait_ge(S("d_qkp"), count(b, base=B))
                    qk = R[0][:].rearrange("p a (h d) -> p a h d", d=DL)
                    A = t["A"][:, p, :].rearrange("p (a h d) -> p a h d", a=2, d=DL)
                    Bt = t["B"][:, p, :].rearrange("p (a h d) -> p a h d", a=2, d=DL)
                    e.wait_ge(S("d_sq"), count(b, base=B))
                    e.tensor_reduce(t["ss"][:, p, :], t["sq"][:].rearrange("p (h d) -> p h d", d=DL), AX.X, ALU.add)\
                        .then_inc(S("d_red"), 1)
                    e.wait_ge(S("d_red"), count(b, base=B))
                    if past(it.i - 3):
                        e.wait_ge(S("d_r"), count(it.i - 3, base=B))
                    e.tensor_scalar(t["vv"][:, p, :], t["ss"][:, p, :], 1e-24, None, ALU.max).then_inc(S("d_vv"), 1)
                    e.tensor_tensor(A, qk, T1[:, l, :, :].unsqueeze(2).to_broadcast([128, 2, HL, DL]), ALU.mult)
                    for h in range(2):
                        i = e.tensor_tensor(Bt[:, :, :, 32 * h:32 * h + 32], qk[:, :, :, 32 - 32 * h:64 - 32 * h],
                                            T2[:, l, :, 32 * h:32 * h + 32].unsqueeze(2).to_broadcast([128, 2, HL, 32]),
                                            ALU.mult)
                    i.then_inc(S("d_B"), 1)
                b = it.b(2)
                if b is not None:
                    e.wait_ge(S("d_S"), count(b, base=B))
                    e.tensor_reduce(t["mx"][:], R[2][:].rearrange("p a (j k) -> p a j k", k=128), AX.X, ALU.max, negate=True)\
                        .then_inc(S("d_mx"), 1)
                    e.wait_ge(S("d_mx"), count(b, base=B))
                    e.tensor_tensor(t["nm"][:].rearrange("p (a j) -> p a j", a=2), t["mx"][:].rearrange("p (a j) -> p a j", a=2),
                                    t["r"][:, it.m(2, 2), 0:8].rearrange("p (j a) -> p a j", a=2), ALU.mult).then_inc(S("d_nm"), 1)
                b5 = it.b(5)
                if b5 is not None:
                    m = it.m(5, 4)
                    e.wait_ge(S(f"d_h2_{m}"), 8 * (b5 + B) + 32 - 8 * m)
                    apart(e)
                    e.bn_stats(st[:, 0, :], rows(H2, b5)).then_inc(S("d_bn"), 1)
                b = it.b(0)
                if b is not None:
                    e.wait_ge(S("d_hh"), count(b, base=B))
                    m = it.m(0, 2)
                    e.tensor_tensor(t["hT"][1][0:64, m, :], R[1][0:64, 0, 128:256], t["hT"][0][0:64, m, :].bitcast(F32), ALU.subtract)
                    e.tensor_tensor(t["hT"][1][64:128, m, 1:128], R[1][64:128, 0, 128:255],
                                    t["hT"][0][64:128, m, 1:128].bitcast(F32), ALU.subtract).then_inc(S("d_hl"), 1)
                b4 = it.b(4)
                if b4 is not None:
                    e.wait_ge(S("d_wo"), count(b4, base=B))
                    e.tensor_tensor(rows(Z, b4), rows(Z, b4), R[1][:, 0:1, 0:128], ALU.add).then_inc(S("d_add"), 1)
                if b5 is not None:
                    stats_tail(e, b5, S("d_bn"), S("d_ag"), S("d_ve"), base=B)
            pipeline(e, NB, 8, 4, body)

        def da_pool(e, l):
            t, B = d, NB * l
            da_start(e, l)

            def body(it):
                b = it.b(1)
                if b is not None:
                    p = it.m(1, 2)
                    e.wait_ge(S("d_vv"), count(b, base=B))
                    if past(it.i - 3):
                        e.wait_ge(S("d_exp"), count(it.i - 3, base=B))
                    e.tensor_tensor(t["r"][:, p, :], t["vv"][:, p, :], nhalf[:, 0:16], ALU.pow).then_inc(S("d_r"), 1)
                    e.wait_ge(S("d_B"), count(b, base=B))
                    e.tensor_tensor(t["A"][:, p, :], t["A"][:, p, :], t["B"][:, p, :], ALU.add).then_inc(S("d_rt"), 1)
                    e.wait_ge(S("d_rt"), count(b, base=B))
                    A = t["A"][:, p, 512:1024].rearrange("p (h d) -> p h d", d=DL)
                    e.tensor_tensor(A, A, t["r"][:, p, 8:16].unsqueeze(2).to_broadcast([128, HL, DL]), ALU.mult)\
                        .then_inc(S("d_qkn"), 1)
                b = it.b(5)
                if b is not None:
                    e.wait_ge(S("d_ve"), count(b, base=B))
                    root(e, b).then_inc(S("d_rs"), 1)
            pipeline(e, NB, 8, 4, body)

        def da_sync(e, l):
            B = NB * l
            if l == 0:
                e.wait_ge(S("d_con"), 8)
            else:
                e.wait_ge(S("f_xn"), count(NG - 1))

            def body(it):
                b = it.b(4)
                if b is not None:
                    s = S(f"d_h2_{it.m(4, 4)}")
                    e.wait_ge(S("d_add"), count(b, base=B))
                    e.dma_start(H2[:, bass.ds(b, 1), 0:64], Z[:, bass.ds(b, 1), 0:64]).then_inc(s, 16)
                    e.dma_start(H2[1:128, bass.ds(b, 1), 64:128], Z[0:127, bass.ds(b, 1), 64:128]).then_inc(s, 16)
            pipeline(e, NB, 8, 4, body)

        def df_start(e, l):
            e.wait_ge(S("d_rs"), count(NB - 1, base=NB * l))
            e.wait_ge(S("d_hl"), count(NB - 1, base=NB * l))

        def df_tensor(e, l):
            t, B = f, NG * l
            df_start(e, l)
            e.wait_ge(S("d_add"), count(NB - 1, base=NB * l))
            e.wait_ge(S("f_con"), l + 1)

            def body(it):
                for c, n in enumerate(HC):
                    b = it.b(1)
                    if b is not None:
                        x = [x[:, it.m(1, 2), :] for x in t["hs"]]
                        e.wait_ge(S("f_lo"), count(b, base=B))
                        if past(b - 1):
                            e.wait_ge(S("f_gt"), count(b - 1, c + 1, 3, base=B))
                        for half in (1, 0):
                            o = half * HID + 128 * c
                            passes(e, R[1 + c][0:n, half, :], [w[:, o:o + n] for w in w1l[l]], x)\
                                .then_inc(S("f_g" if half else "f_a"), 1)
                    b = it.b(2)
                    if b is not None and c == 0:
                        if past(b - 1):
                            e.wait_ge(S("f_add"), count(b - 1, base=B))
                        e.wait_ge(S("f_gt"), count(b, 3, 3, base=B))
                        for j in range(GB):
                            for k in range(3):
                                n = 128 if k < 2 else HC[2] + 1
                                mm = e.matmul(R[0][:, 1, 128 * j:128 * j + 128],
                                              t["gt"][0:n, it.m(2, 2), k, 128 * j:128 * j + 128],
                                              w2l[0:n, l, k, :], start=(k == 0), stop=(k == 2))
                        mm.then_inc(S("f_y"), 1)
                    b = it.b(0)
                    if b is not None and c == 0:
                        if past(b - 1):
                            e.wait_ge(S("f_hn"), count(b - 1, base=B))
                        e.wait_ge(S("f_xn"), count(b, base=B))
                        for j in range(GB):
                            mm = e.transpose(R[0][:, 0, 128 * j:128 * j + 128], t["xn"][:, j, :], ident[:])
                        mm.then_inc(S("f_xT"), 1)
            pipeline(e, NG, 4, 2, body)

        def df_scalar(e, l):
            t, B = f, NG * l
            df_start(e, l)

            def body(it):
                for c, n in enumerate(HC):
                    b = it.b(1)
                    if b is not None:
                        e.wait_ge(S("f_g"), count(b, c + 1, 3, base=B))
                        if past(b - 1):
                            e.wait_ge(S("f_gt"), count(b - 1, c + 1, 3, base=B))
                        e.activation(t["gl"][0:n, c, :], R[1 + c][0:n, 1, :], ACT.Gelu, bias=b1l[0:n, l, 3 + c:4 + c])\
                            .then_inc(S("f_gl"), 1)
                    b = it.b(0)
                    if b is not None and c == 1:
                        e.wait_ge(S("f_hn"), count(b, base=B))
                        e.activation(t["hs"][0][:, it.m(0, 2), :], t["hn"][:, it.m(0, 2), :], ACT.Copy).then_inc(S("f_hi"), 1)
            pipeline(e, NG, 4, 2, body)

        def df_vector(e, l):
            t, B = f, NG * l
            df_start(e, l)
            e.memset(t["gt"][:], 1.0).then_inc(S("f_con"), 1)
            e.wait_ge(S("f_con"), l + 1)

            def body(it):
                for c, n in enumerate(HC):
                    b = it.b(1)
                    if b is not None:
                        e.wait_ge(S("f_a"), count(b, c + 1, 3, base=B))
                        e.wait_ge(S("f_gl"), count(b, c + 1, 3, base=B))
                        e.scalar_tensor_tensor(out=t["gt"][0:n, it.m(1, 2), c, :], in0=R[1 + c][0:n, 0, :],
                                               scalar=b1l[0:n, l, c:c + 1], in1=t["gl"][0:n, c, :], op0=ALU.add, op1=ALU.mult)\
                            .then_inc(S("f_gt"), 1)
                    b = it.b(0)
                    if b is not None and c == 0:
                        for j in range(GB):
                            bj = b * GB + j
                            e.tensor_scalar(t["xn"][:, j:j + 1, :], rows(H2, bj),
                                            mv[:, bass.ds(bj, 1), 0:1].rearrange("p a b -> p (a b)"), rs[:, bass.ds(bj, 1)],
                                            ALU.subtract, ALU.mult).then_inc(S("f_xn") if j == GB - 1 else S("f_xnj"), 1)
                    b = it.b(2)
                    if b is not None and c == 0:
                        zr = Z[:, bass.ds(b * GB, GB), :]
                        e.wait_ge(S("f_y"), count(b, base=B))
                        e.tensor_tensor(zr, zr, R[0][:, 1, :].rearrange("p (a b) -> p a b", b=128), ALU.add).then_inc(S("f_add"), 1)
                        if l == DEPTH - 1:
                            m = it.m(2, 2)
                            e.wait_ge(S("f_add"), count(b, base=B))
                            if not (it.static and it.i < 4):
                                e.wait_ge(S(f"out{m}"), 8 * (b - m))
                            e.tensor_tensor(t["o"][:, m, :].rearrange("p (a b) -> p a b", b=128), zr, X[:, bass.ds(b * GB, GB), :],
                                            ALU.add).then_inc(S("f_o"), 1)
                    b = it.b(0)
                    if b is not None and c == 0:
                        m = it.m(0, 2)
                        e.wait_ge(S("f_xT"), count(b, base=B))
                        e.tensor_scalar(t["hn"][:, m, :], R[0][:, 0, :], lng[:, l, 0:1], lng[:, l, 1:2], ALU.mult, ALU.add)\
                            .then_inc(S("f_hn"), 1)
                    b = it.b(0)
                    if b is not None and c == 1:
                        m = it.m(0, 2)
                        e.wait_ge(S("f_hi"), count(b, base=B))
                        e.tensor_tensor(t["hs"][1][:, m, :], t["hn"][:, m, :], t["hs"][0][:, m, :].bitcast(F32), ALU.subtract)\
                            .then_inc(S("f_lo"), 1)
            pipeline(e, NG, 4, 2, body)

        def df_sync(e):
            def body(it):
                b = it.b(2)
                if b is not None:
                    m = it.m(2, 2)
                    e.wait_ge(S("f_o"), count(b))
                    e.dma_start(out[:, bass.ds(b * 512, 512)], f["o"][:, m, :]).then_inc(S(f"out{m}"), 16)
            pipeline(e, NG, 4, 2, body)
            for m in range(2):
                e.wait_ge(S(f"out{m}"), 16 * NG // 2)
        block = ctx.enter_context(nc.Block())

        @block.sync
        def _(sync):
            load(sync)
            load_d(sync)
            for l in range(DEPTH):
                da_sync(sync, l)
            df_sync(sync)

        @block.scalar
        def _(act):
            split_act(act)
            a_scalar(act)
            b_scalar(act)
            c_scalar(act)
            for l in range(DEPTH):
                da_scalar(act, l)
                df_scalar(act, l)

        @block.vector
        def _(dve):
            split_dve(dve)
            a_vector(dve)
            b_vector(dve)
            c_vector(dve)
            d_start(dve)
            for l in range(DEPTH):
                da_vector(dve, l)
                df_vector(dve, l)

        @block.gpsimd
        def _(pool):
            start_pool(pool)
            a_pool(pool)
            b_pool(pool)
            c_pool(pool)
            for l in range(DEPTH):
                da_pool(pool, l)

        @block.tensor
        def _(pe):
            a_tensor(pe)
            b_tensor(pe)
            c_tensor(pe)
            for l in range(DEPTH):
                da_tensor(pe, l)
                df_tensor(pe, l)


def lay_out(i):
    x = i["x"]
    a = {}
    a["x"] = x.transpose(1, 0, 2).reshape(T, NB * D)
    a["ctx"] = i["ctx_1024"].transpose(2, 0, 1).reshape(D, NB * SK)
    a["mask"] = i["mask_1x1xSxS2_ik0"].reshape(T, SK)
    a["wq0"] = i["L0_xattn_wq"].T
    a["wkv0"] = np.concatenate([i["L0_xattn_wk"].T, i["L0_xattn_wv"].T], axis=1)
    a["wo0"] = i["L0_xattn_wo"].T.reshape(8, 128, D).transpose(1, 0, 2).reshape(128, 8 * D)
    a["nrm0"] = np.stack([np.tile(i["L0_xattn_q_norm_w"], 2), np.tile(i["L0_xattn_k_norm_w"], 2)], axis=1)
    a["wg"] = i["L0_ffn_wg"].T
    a["w1e"] = i["L0_ffn_w1"].reshape(NE * INTER, D).T
    a["w3e"] = i["L0_ffn_w3"].reshape(NE * INTER, D).T
    a["w2e"] = i["L0_ffn_w2"].transpose(0, 2, 1).reshape(NCH, 128, D).transpose(1, 0, 2).reshape(128, NCH * D)
    a["l1"] = np.concatenate([i["L1_xattn_w_" + n].T for n in "qkvo"], axis=1)
    a["wqkv"] = i["L1_ffn_wqkv"].transpose(1, 0, 2).reshape(D, DEPTH * 1536)
    qk = np.stack([i["L1_ffn_q_scale"], i["L1_ffn_k_scale"]], axis=1)
    swapped = np.concatenate([qk[..., DL // 2:], qk[..., :DL // 2]], axis=-1)
    a["qks"] = np.tile(np.stack([qk, swapped], axis=1).reshape(1, -1), (T, 1))
    a["wol"] = i["L1_ffn_wo"].reshape(DEPTH, 4, 128, D).transpose(2, 0, 1, 3).reshape(128, DEPTH * 4 * D)
    a["lng"] = np.stack([i["L1_ffn_ln_g"], i["L1_ffn_ln_b"]], axis=2).transpose(1, 0, 2).reshape(D, DEPTH * 2)
    a["w1l"] = i["L1_ffn_w1"].transpose(1, 0, 2).reshape(D, DEPTH * 2 * HID)
    b1 = np.zeros((128, DEPTH, 6), np.float32)
    w2 = np.zeros((128, DEPTH, 3, D), np.float32)
    for c, n in enumerate(HC):
        for half in range(2):
            b1[:n, :, 3 * half + c] = i["L1_ffn_b1"][:, half * HID + 128 * c:half * HID + 128 * c + n].T
        w2[:n, :, c] = i["L1_ffn_w2"][:, 128 * c:128 * c + n].transpose(1, 0, 2)
    w2[HC[2], :, 2] = i["L1_ffn_b2"]
    a["b1l"] = b1.reshape(128, DEPTH * 6)
    a["w2l"] = w2.reshape(128, DEPTH * 3 * D)
    return a


def constants():
    c = {}
    c["ident"] = np.eye(128, dtype=np.float32)
    t = np.arange(T)
    c["band"] = np.where((t[:, None] < t[None, :]) | (t[:, None] > t[None, :] + WINDOW), BAND, 0.0).astype(np.float32)
    half = np.arange(0, DL, 2, dtype=np.float32)
    freqs = (t.astype(np.float32)[:, None] * (1.0 / np.float32(10000.0) ** (half / DL)).astype(np.float32)[None]).astype(np.float64)
    base = (half + 0.4 * DL) / (1.4 * DL)
    scale = base[None, :].astype(np.float64) ** ((t - T // 2) / float(WINDOW // 2))[:, None]
    cos, sin = np.cos(freqs), np.sin(freqs)
    both = lambda x, y: np.concatenate([x, y], axis=-1)
    q = [both(cos * scale, cos * scale) * 8.0, both(-sin * scale, sin * scale) * 8.0]
    k = [both(cos / scale, cos / scale), both(-sin / scale, sin / scale)]
    c["rot"] = np.stack([np.stack([q[0], k[0]], 1), np.stack([q[1], k[1]], 1)], 1).reshape(T, 256).astype(np.float32)
    c["keyi"] = np.tile(np.arange(NE, 0, -1, dtype=np.float32), (128, GB))
    c["head"] = (np.arange(128)[:, None] // DH1 % 4 == np.arange(4)[None]).astype(np.float32)
    return c


def kernel(**inputs):
    import concourse.bacc as bacc
    from concourse.bass_utils import run_bass_kernel_spmd

    nc = bacc.Bacc("TRN2", target_bir_lowering=False, num_devices=1)
    laid = {**lay_out({k: np.asarray(v) for k, v in inputs.items()}), **constants()}
    arrays, args = {}, {}
    for name, value in laid.items():
        value = np.ascontiguousarray(value)
        arrays["in_" + name] = value
        args[name + "_in"] = nc.dram_tensor("in_" + name, value.shape, mybir.dt.from_np(value.dtype), kind="ExternalInput").ap()
    out = nc.dram_tensor("out", (T, NB * D), F32, kind="ExternalOutput").ap()
    program(nc, out=out, **args)
    result = run_bass_kernel_spmd(nc, [arrays], core_ids=[0]).results[0]["out"]
    return result.reshape(T, NB, D).transpose(1, 0, 2)
```
